# Optimizing a Trainium2 kernel written in Bass

```python
import numpy as np
import jax
import jax.numpy as jnp

def _softmax(x, axis=-1):
    return jax.nn.softmax(x, axis=axis)

def _gelu(x):
    return jax.nn.gelu(x, approximate=True)

def _silu(x):
    return jax.nn.silu(x)

def _sigmoid(x):
    return jax.nn.sigmoid(x)

def _layernorm(x, axis=-1, eps=1e-05):
    m = jnp.mean(x, axis=axis, keepdims=True)
    v = jnp.var(x, axis=axis, keepdims=True)
    return (x - m) / jnp.sqrt(v + eps)

def _scatter_add(tgt, idx, src, axis=0):
    return tgt.at[idx].add(src)

def _segment_sum(src, seg, n):
    return jax.ops.segment_sum(src, seg, n)
kernel_name = 'mk_decoder_preln_d2_seqx_r8_fe1afb'

def setup_inputs(seed: int=0):
    np.random.seed(seed)
    _w = jnp.asarray

    def _rec_inputs():
        import jax
        import jax.numpy as jnp
        _rk = jax.random.key(seed)
        x = -0.0002928 + 1 * jax.random.normal(jax.random.fold_in(_rk, 1), (8, 256, 128), jnp.float32)
        _lenS = 256 - jax.random.randint(jax.random.fold_in(_rk, 7), (8,), 0, max(1, 256 // 4) + 1, jnp.int32)
        _lenS2 = 256 - jax.random.randint(jax.random.fold_in(_rk, 8), (8,), 0, max(1, 256 // 4) + 1, jnp.int32)
        _ctx_512P = jax.random.normal(jax.random.fold_in(_rk, 11), (8, 16, 64), jnp.float32)
        _ctx_512c = jax.random.dirichlet(jax.random.fold_in(_rk, 511), 0.3 * jnp.ones((16,), jnp.float32), (8, 256))
        _ctx_512t = jnp.einsum('bsk,bkd->bsd', _ctx_512c, _ctx_512P)
        _ctx_512t = _ctx_512t * jax.lax.rsqrt(jnp.mean(jnp.square(_ctx_512t)) + 1e-12) * 0.953939
        ctx_512 = 0.00222621 + 0.99962 * (_ctx_512t + 0.3 * jax.random.normal(jax.random.fold_in(_rk, 611), (8, 256, 64), jnp.float32))
        return (x, ctx_512)
    x, ctx_512 = _rec_inputs()

    def _L0_attn_setup():
        import jax, jax.numpy as jnp
        import numpy as np
        N_HEAD = 16
        PAGE_SIZE = 32
        ROPE_THETA = 10000.0

        def _rope_tables(T, D, dtype):
            inv = 1.0 / ROPE_THETA ** (np.arange(0, D, 2, dtype=np.float32) / D)
            ang = np.outer(np.arange(T, dtype=np.float32), inv)
            return (jnp.asarray(np.cos(ang), dtype), jnp.asarray(np.sin(ang), dtype))

        def _apply_rope(x, cos, sin):
            x1 = x[..., 0::2]
            x2 = x[..., 1::2]
            c = cos[None, :, None, :]
            s = sin[None, :, None, :]
            out = jnp.stack([x1 * c - x2 * s, x1 * s + x2 * c], axis=-1)
            return out.reshape(x.shape)
        key = jax.random.key(seed)
        ks = jax.random.split(key, 6)
        B, T, E = (2, 256, 128)
        L = E // 2
        sc = lambda fan: 1.0 / np.sqrt(fan)
        return {'x': jax.random.normal(ks[0], (B, T, E), jnp.float32), 'wq': jax.random.normal(ks[1], (E, E), jnp.float32) * sc(E), 'w_down': jax.random.normal(ks[2], (E, L), jnp.float32) * sc(E), 'wk_up': jax.random.normal(ks[3], (L, E), jnp.float32) * sc(L), 'wv_up': jax.random.normal(ks[4], (L, E), jnp.float32) * sc(L), 'wo': jax.random.normal(ks[5], (E, E), jnp.float32) * sc(E)}
    _L0_attn_all = _L0_attn_setup()
    _L0_attn_in = {k: v for k, v in _L0_attn_all.items() if k in ('wq', 'w_down', 'wk_up', 'wv_up', 'wo')}
    del _L0_attn_all

    def _L0_xattn_setup():
        import jax, jax.numpy as jnp
        import numpy as np
        B, T, TC, C, CC, H = (2, 256, 64, 128, 64, 16)
        D = C // H

        def _heads(t):
            b, l, _ = t.shape
            return t.reshape(b, l, H, D).transpose(0, 2, 1, 3)
        key = jax.random.key(seed)
        ks = jax.random.split(key, 18)
        w = lambda k, i, o: jax.random.normal(k, (i, o), jnp.float32) / np.sqrt(i).astype(np.float32)
        return {'x': jax.random.normal(ks[0], (B, T, C), jnp.float32), 'cross_input': jax.random.normal(ks[1], (B, TC, CC), jnp.float32), 'Wk': w(ks[2], C, C), 'bk': jnp.zeros((C,), jnp.float32), 'Wq': w(ks[3], C, C), 'bq': jnp.zeros((C,), jnp.float32), 'Wv': w(ks[4], C, C), 'bv': jnp.zeros((C,), jnp.float32), 'Wck': w(ks[5], CC, C), 'bck': jnp.zeros((C,), jnp.float32), 'Wcq': w(ks[6], C, C), 'bcq': jnp.zeros((C,), jnp.float32), 'Wcv': w(ks[7], CC, C), 'bcv': jnp.zeros((C,), jnp.float32), 'Wp': w(ks[8], C, C), 'bp': jnp.zeros((C,), jnp.float32)}
    _L0_xattn_all = _L0_xattn_setup()
    _L0_xattn_in = {k: v for k, v in _L0_xattn_all.items() if k in ('Wk', 'bk', 'Wq', 'bq', 'Wv', 'bv', 'Wck', 'bck', 'Wcq', 'bcq', 'Wcv', 'bcv', 'Wp', 'bp')}
    del _L0_xattn_all

    def _L0_ffn_setup():
        import jax, jax.numpy as jnp
        import numpy as np
        E = 8
        K = 2
        CAP_RATIO = 1.05
        key = jax.random.key(seed)
        ks = jax.random.split(key, 4)
        B, S, D, H = (2, 256, 128, 512)
        x = jax.random.normal(ks[0], (B, S, D), jnp.float32)
        Wg = jax.random.normal(ks[1], (E, D), jnp.float32) * 0.02
        W1 = jax.random.normal(ks[2], (E, D, H), jnp.float32) * 0.02
        b1 = jnp.zeros((E, H), jnp.float32)
        W2 = jax.random.normal(ks[3], (E, H, D), jnp.float32) * 0.02
        b2 = jnp.zeros((E, D), jnp.float32)
        return {'x': x, 'Wg': Wg, 'W1': W1, 'b1': b1, 'W2': W2, 'b2': b2}
    _L0_ffn_all = _L0_ffn_setup()
    _L0_ffn_in = {k: v for k, v in _L0_ffn_all.items() if k in ('Wg', 'W1', 'b1', 'W2', 'b2')}
    del _L0_ffn_all

    def _L1_attn_setup():
        import jax, jax.numpy as jnp
        import numpy as np
        DIM = 128
        HEADS = 16
        HIDDEN = 512
        EPS_ATTN = 1e-06
        EPS_LN = 1e-05

        def layer_norm(x, g, b):
            mu = jnp.mean(x, axis=-1, keepdims=True)
            var = jnp.var(x, axis=-1, keepdims=True)
            return (x - mu) * jax.lax.rsqrt(var + EPS_LN) * g + b
        key = jax.random.key(seed)
        ks = jax.random.split(key, 8)
        s = 0.02
        return {'x': jax.random.normal(ks[0], (4, 512, DIM), jnp.float32), 'norm1_g': jnp.ones((DIM,), jnp.float32), 'norm1_b': jnp.zeros((DIM,), jnp.float32), 'qkv_w': jax.random.normal(ks[1], (3 * DIM, DIM), jnp.float32) * s, 'proj_w': jax.random.normal(ks[2], (DIM, DIM), jnp.float32) * s, 'proj_b': jnp.zeros((DIM,), jnp.float32), 'norm2_g': jnp.ones((DIM,), jnp.float32), 'norm2_b': jnp.zeros((DIM,), jnp.float32), 'fc1_w': jax.random.normal(ks[3], (HIDDEN, DIM), jnp.float32) * s, 'fc1_b': jnp.zeros((HIDDEN,), jnp.float32), 'fc2_w': jax.random.normal(ks[4], (DIM, HIDDEN), jnp.float32) * s, 'fc2_b': jnp.zeros((DIM,), jnp.float32)}
    _L1_attn_all = _L1_attn_setup()
    _L1_attn_in = {k: v for k, v in _L1_attn_all.items() if k in ('norm1_g', 'norm1_b', 'qkv_w', 'proj_w', 'proj_b', 'norm2_g', 'norm2_b', 'fc1_w', 'fc1_b', 'fc2_w', 'fc2_b')}
    del _L1_attn_all

    def _L1_xattn_setup():
        import jax, jax.numpy as jnp
        import numpy as np
        H, D, C1, C2, S, M, B, W = (16, 32, 128, 64, 256, 64, 2, 4)

        def _ln(x, g, b):
            m = jnp.mean(x, -1, keepdims=True)
            v = jnp.var(x, -1, keepdims=True)
            return (x - m) * jax.lax.rsqrt(v + 1e-05) * g + b

        def _mha(x, y, wq, wk, wv, li1_w, li1_b, lnx_g, lnx_b, lny_g, lny_b, ln3_g, ln3_b, li2_w, li2_b, li3_w, li3_b, causal):
            xn = _ln(x, lnx_g, lnx_b)
            yn = _ln(y, lny_g, lny_b)
            q = jnp.einsum('bsc,hcd->bhsd', xn, wq)
            k = jnp.einsum('btc,hcd->bhtd', yn, wk)
            v = jnp.einsum('btc,hcd->bhtd', yn, wv)
            a = jax.nn.softmax(jnp.einsum('bhsd,bhtd->bhst', q, k) * D ** (-0.5), axis=-1)
            if causal:
                s, t = (a.shape[-2], a.shape[-1])
                mask = (jnp.arange(t)[None, :] > jnp.arange(s)[:, None]).astype(a.dtype)
                a = a * mask
            o = jnp.einsum('bhst,bhtd->bhsd', a, v)
            o = o.transpose(0, 2, 1, 3).reshape(x.shape[0], x.shape[1], H * D)
            x_out = x + o @ li1_w + li1_b
            h = jax.nn.gelu(_ln(x_out, ln3_g, ln3_b) @ li2_w + li2_b, approximate=False)
            return x_out + h @ li3_w + li3_b
        key = jax.random.key(seed)
        ks = iter(jax.random.split(key, 64))

        def w(shape, scale=0.02):
            return jax.random.normal(next(ks), shape, jnp.float32) * scale
        inp = {'xx': jax.random.normal(next(ks), (B, S, C1), jnp.float32), 'ee': jax.random.normal(next(ks), (B, M, C2), jnp.float32), 'ln1_g': jnp.ones(C1, jnp.float32), 'ln1_b': jnp.zeros(C1, jnp.float32), 'ln2_g': jnp.ones(C1, jnp.float32), 'ln2_b': jnp.zeros(C1, jnp.float32)}
        for pfx, cy in (('a1', C1), ('a2', C2)):
            inp[pfx + '_wq'] = w((H, C1, D))
            inp[pfx + '_wk'] = w((H, cy, D))
            inp[pfx + '_wv'] = w((H, cy, D))
            inp[pfx + '_li1_w'] = w((H * D, C1))
            inp[pfx + '_li1_b'] = jnp.zeros(C1, jnp.float32)
            inp[pfx + '_lnx_g'] = jnp.ones(C1, jnp.float32)
            inp[pfx + '_lnx_b'] = jnp.zeros(C1, jnp.float32)
            inp[pfx + '_lny_g'] = jnp.ones(cy, jnp.float32)
            inp[pfx + '_lny_b'] = jnp.zeros(cy, jnp.float32)
            inp[pfx + '_ln3_g'] = jnp.ones(C1, jnp.float32)
            inp[pfx + '_ln3_b'] = jnp.zeros(C1, jnp.float32)
            inp[pfx + '_li2_w'] = w((C1, C1 * W))
            inp[pfx + '_li2_b'] = jnp.zeros(C1 * W, jnp.float32)
            inp[pfx + '_li3_w'] = w((C1 * W, C1))
            inp[pfx + '_li3_b'] = jnp.zeros(C1, jnp.float32)
        inp['training'] = 0
        return inp
    _L1_xattn_all = _L1_xattn_setup()
    _L1_xattn_in = {k: v for k, v in _L1_xattn_all.items() if k in ('ln1_g', 'ln1_b', 'ln2_g', 'ln2_b', 'a1_wq', 'a1_wk', 'a1_wv', 'a1_li1_w', 'a1_li1_b', 'a1_lnx_g', 'a1_lnx_b', 'a1_lny_g', 'a1_lny_b', 'a1_ln3_g', 'a1_ln3_b', 'a1_li2_w', 'a1_li2_b', 'a1_li3_w', 'a1_li3_b', 'a2_wq', 'a2_wk', 'a2_wv', 'a2_li1_w', 'a2_li1_b', 'a2_lnx_g', 'a2_lnx_b', 'a2_lny_g', 'a2_lny_b', 'a2_ln3_g', 'a2_ln3_b', 'a2_li2_w', 'a2_li2_b', 'a2_li3_w', 'a2_li3_b')}
    del _L1_xattn_all

    def _L1_ffn_setup():
        import jax, jax.numpy as jnp
        import numpy as np
        LATENT = 128
        LEAF_W = 64
        DEPTH = 4
        N_LEAVES = 2 ** DEPTH
        N_NODES = 2 ** DEPTH - 1
        B, S = (4, 256)

        def _fff_params(key, prefix):
            ks = jax.random.split(key, 4)
            d, h, l, n = (LATENT, LEAF_W, N_LEAVES, N_NODES)
            s_in = 1.0 / np.sqrt(d).astype(np.float32)
            s_h = 1.0 / np.sqrt(h).astype(np.float32)
            return {f'{prefix}_node_w': jax.random.normal(ks[0], (n, d), jnp.float32) * s_in, f'{prefix}_node_b': jax.random.normal(ks[1], (n,), jnp.float32) * s_in, f'{prefix}_w1': jax.random.normal(ks[2], (l, d, h), jnp.float32) * s_in, f'{prefix}_b1': jnp.zeros((l, h), jnp.float32), f'{prefix}_w2': jax.random.normal(ks[3], (l, h, d), jnp.float32) * s_h, f'{prefix}_b2': jnp.zeros((l, d), jnp.float32)}

        def _fff(x, node_w, node_b, w1, b1, w2, b2):
            Bx, Sx, D = x.shape
            xf = x.reshape(-1, D)
            N = xf.shape[0]
            cur = jnp.zeros((N,), jnp.int32)
            for _ in range(DEPTH):
                pw = node_w[cur]
                score = jnp.einsum('nd,nd->n', xf, pw) + node_b[cur]
                cur = 2 * cur + 1 + (score >= 0).astype(jnp.int32)
            leaf = cur - N_NODES
            sel = jax.nn.one_hot(leaf, N_LEAVES, dtype=xf.dtype)
            hidden_all = jax.nn.relu(jnp.einsum('nd,ldh->lnh', xf, w1) + b1[:, None, :])
            hidden = hidden_all * sel.T[:, :, None]
            out = jnp.einsum('lnh,lho->no', hidden, w2) + sel @ b2
            return out.reshape(Bx, Sx, D)
        key = jax.random.key(seed)
        kx, kq, kk, kv = jax.random.split(key, 4)
        inp = {'x': jax.random.normal(kx, (B, S, LATENT), jnp.float32)}
        inp.update(_fff_params(kq, 'q'))
        inp.update(_fff_params(kk, 'k'))
        inp.update(_fff_params(kv, 'v'))
        return inp
    _L1_ffn_all = _L1_ffn_setup()
    _L1_ffn_in = {k: v for k, v in _L1_ffn_all.items() if k in ('q_node_w', 'q_node_b', 'q_w1', 'q_b1', 'q_w2', 'q_b2', 'k_node_w', 'k_node_b', 'k_w1', 'k_b1', 'k_w2', 'k_b2', 'v_node_w', 'v_node_b', 'v_w1', 'v_b1', 'v_w2', 'v_b2')}
    del _L1_ffn_all
    return {'x': x, 'ctx_512': ctx_512, 'L0_attn_wq': _L0_attn_in['wq'], 'L0_attn_w_down': _L0_attn_in['w_down'], 'L0_attn_wk_up': _L0_attn_in['wk_up'], 'L0_attn_wv_up': _L0_attn_in['wv_up'], 'L0_attn_wo': _L0_attn_in['wo'], 'L0_xattn_Wk': _L0_xattn_in['Wk'], 'L0_xattn_bk': _L0_xattn_in['bk'], 'L0_xattn_Wq': _L0_xattn_in['Wq'], 'L0_xattn_bq': _L0_xattn_in['bq'], 'L0_xattn_Wv': _L0_xattn_in['Wv'], 'L0_xattn_bv': _L0_xattn_in['bv'], 'L0_xattn_Wck': _L0_xattn_in['Wck'], 'L0_xattn_bck': _L0_xattn_in['bck'], 'L0_xattn_Wcq': _L0_xattn_in['Wcq'], 'L0_xattn_bcq': _L0_xattn_in['bcq'], 'L0_xattn_Wcv': _L0_xattn_in['Wcv'], 'L0_xattn_bcv': _L0_xattn_in['bcv'], 'L0_xattn_Wp': _L0_xattn_in['Wp'], 'L0_xattn_bp': _L0_xattn_in['bp'], 'L0_ffn_Wg': _L0_ffn_in['Wg'], 'L0_ffn_W1': _L0_ffn_in['W1'], 'L0_ffn_b1': _L0_ffn_in['b1'], 'L0_ffn_W2': _L0_ffn_in['W2'], 'L0_ffn_b2': _L0_ffn_in['b2'], 'L1_attn_norm1_g': _L1_attn_in['norm1_g'], 'L1_attn_norm1_b': _L1_attn_in['norm1_b'], 'L1_attn_qkv_w': _L1_attn_in['qkv_w'], 'L1_attn_proj_w': _L1_attn_in['proj_w'], 'L1_attn_proj_b': _L1_attn_in['proj_b'], 'L1_attn_norm2_g': _L1_attn_in['norm2_g'], 'L1_attn_norm2_b': _L1_attn_in['norm2_b'], 'L1_attn_fc1_w': _L1_attn_in['fc1_w'], 'L1_attn_fc1_b': _L1_attn_in['fc1_b'], 'L1_attn_fc2_w': _L1_attn_in['fc2_w'], 'L1_attn_fc2_b': _L1_attn_in['fc2_b'], 'L1_xattn_ln1_g': _L1_xattn_in['ln1_g'], 'L1_xattn_ln1_b': _L1_xattn_in['ln1_b'], 'L1_xattn_ln2_g': _L1_xattn_in['ln2_g'], 'L1_xattn_ln2_b': _L1_xattn_in['ln2_b'], 'L1_xattn_a1_wq': _L1_xattn_in['a1_wq'], 'L1_xattn_a1_wk': _L1_xattn_in['a1_wk'], 'L1_xattn_a1_wv': _L1_xattn_in['a1_wv'], 'L1_xattn_a1_li1_w': _L1_xattn_in['a1_li1_w'], 'L1_xattn_a1_li1_b': _L1_xattn_in['a1_li1_b'], 'L1_xattn_a1_lnx_g': _L1_xattn_in['a1_lnx_g'], 'L1_xattn_a1_lnx_b': _L1_xattn_in['a1_lnx_b'], 'L1_xattn_a1_lny_g': _L1_xattn_in['a1_lny_g'], 'L1_xattn_a1_lny_b': _L1_xattn_in['a1_lny_b'], 'L1_xattn_a1_ln3_g': _L1_xattn_in['a1_ln3_g'], 'L1_xattn_a1_ln3_b': _L1_xattn_in['a1_ln3_b'], 'L1_xattn_a1_li2_w': _L1_xattn_in['a1_li2_w'], 'L1_xattn_a1_li2_b': _L1_xattn_in['a1_li2_b'], 'L1_xattn_a1_li3_w': _L1_xattn_in['a1_li3_w'], 'L1_xattn_a1_li3_b': _L1_xattn_in['a1_li3_b'], 'L1_xattn_a2_wq': _L1_xattn_in['a2_wq'], 'L1_xattn_a2_wk': _L1_xattn_in['a2_wk'], 'L1_xattn_a2_wv': _L1_xattn_in['a2_wv'], 'L1_xattn_a2_li1_w': _L1_xattn_in['a2_li1_w'], 'L1_xattn_a2_li1_b': _L1_xattn_in['a2_li1_b'], 'L1_xattn_a2_lnx_g': _L1_xattn_in['a2_lnx_g'], 'L1_xattn_a2_lnx_b': _L1_xattn_in['a2_lnx_b'], 'L1_xattn_a2_lny_g': _L1_xattn_in['a2_lny_g'], 'L1_xattn_a2_lny_b': _L1_xattn_in['a2_lny_b'], 'L1_xattn_a2_ln3_g': _L1_xattn_in['a2_ln3_g'], 'L1_xattn_a2_ln3_b': _L1_xattn_in['a2_ln3_b'], 'L1_xattn_a2_li2_w': _L1_xattn_in['a2_li2_w'], 'L1_xattn_a2_li2_b': _L1_xattn_in['a2_li2_b'], 'L1_xattn_a2_li3_w': _L1_xattn_in['a2_li3_w'], 'L1_xattn_a2_li3_b': _L1_xattn_in['a2_li3_b'], 'L1_ffn_q_node_w': _L1_ffn_in['q_node_w'], 'L1_ffn_q_node_b': _L1_ffn_in['q_node_b'], 'L1_ffn_q_w1': _L1_ffn_in['q_w1'], 'L1_ffn_q_b1': _L1_ffn_in['q_b1'], 'L1_ffn_q_w2': _L1_ffn_in['q_w2'], 'L1_ffn_q_b2': _L1_ffn_in['q_b2'], 'L1_ffn_k_node_w': _L1_ffn_in['k_node_w'], 'L1_ffn_k_node_b': _L1_ffn_in['k_node_b'], 'L1_ffn_k_w1': _L1_ffn_in['k_w1'], 'L1_ffn_k_b1': _L1_ffn_in['k_b1'], 'L1_ffn_k_w2': _L1_ffn_in['k_w2'], 'L1_ffn_k_b2': _L1_ffn_in['k_b2'], 'L1_ffn_v_node_w': _L1_ffn_in['v_node_w'], 'L1_ffn_v_node_b': _L1_ffn_in['v_node_b'], 'L1_ffn_v_w1': _L1_ffn_in['v_w1'], 'L1_ffn_v_b1': _L1_ffn_in['v_b1'], 'L1_ffn_v_w2': _L1_ffn_in['v_w2'], 'L1_ffn_v_b2': _L1_ffn_in['v_b2']}

def reference(x, ctx_512, L0_attn_wq, L0_attn_w_down, L0_attn_wk_up, L0_attn_wv_up, L0_attn_wo, L0_xattn_Wk, L0_xattn_bk, L0_xattn_Wq, L0_xattn_bq, L0_xattn_Wv, L0_xattn_bv, L0_xattn_Wck, L0_xattn_bck, L0_xattn_Wcq, L0_xattn_bcq, L0_xattn_Wcv, L0_xattn_bcv, L0_xattn_Wp, L0_xattn_bp, L0_ffn_Wg, L0_ffn_W1, L0_ffn_b1, L0_ffn_W2, L0_ffn_b2, L1_attn_norm1_g, L1_attn_norm1_b, L1_attn_qkv_w, L1_attn_proj_w, L1_attn_proj_b, L1_attn_norm2_g, L1_attn_norm2_b, L1_attn_fc1_w, L1_attn_fc1_b, L1_attn_fc2_w, L1_attn_fc2_b, L1_xattn_ln1_g, L1_xattn_ln1_b, L1_xattn_ln2_g, L1_xattn_ln2_b, L1_xattn_a1_wq, L1_xattn_a1_wk, L1_xattn_a1_wv, L1_xattn_a1_li1_w, L1_xattn_a1_li1_b, L1_xattn_a1_lnx_g, L1_xattn_a1_lnx_b, L1_xattn_a1_lny_g, L1_xattn_a1_lny_b, L1_xattn_a1_ln3_g, L1_xattn_a1_ln3_b, L1_xattn_a1_li2_w, L1_xattn_a1_li2_b, L1_xattn_a1_li3_w, L1_xattn_a1_li3_b, L1_xattn_a2_wq, L1_xattn_a2_wk, L1_xattn_a2_wv, L1_xattn_a2_li1_w, L1_xattn_a2_li1_b, L1_xattn_a2_lnx_g, L1_xattn_a2_lnx_b, L1_xattn_a2_lny_g, L1_xattn_a2_lny_b, L1_xattn_a2_ln3_g, L1_xattn_a2_ln3_b, L1_xattn_a2_li2_w, L1_xattn_a2_li2_b, L1_xattn_a2_li3_w, L1_xattn_a2_li3_b, L1_ffn_q_node_w, L1_ffn_q_node_b, L1_ffn_q_w1, L1_ffn_q_b1, L1_ffn_q_w2, L1_ffn_q_b2, L1_ffn_k_node_w, L1_ffn_k_node_b, L1_ffn_k_w1, L1_ffn_k_b1, L1_ffn_k_w2, L1_ffn_k_b2, L1_ffn_v_node_w, L1_ffn_v_node_b, L1_ffn_v_w1, L1_ffn_v_b1, L1_ffn_v_w2, L1_ffn_v_b2):
    import jax
    import jax.numpy as jnp

    def _L0_attn_ref(x, wq, w_down, wk_up, wv_up, wo):
        import jax, jax.numpy as jnp
        import numpy as np
        N_HEAD = 16
        PAGE_SIZE = 32
        ROPE_THETA = 10000.0

        def _rope_tables(T, D, dtype):
            inv = 1.0 / ROPE_THETA ** (np.arange(0, D, 2, dtype=np.float32) / D)
            ang = np.outer(np.arange(T, dtype=np.float32), inv)
            return (jnp.asarray(np.cos(ang), dtype), jnp.asarray(np.sin(ang), dtype))

        def _apply_rope(x, cos, sin):
            x1 = x[..., 0::2]
            x2 = x[..., 1::2]
            c = cos[None, :, None, :]
            s = sin[None, :, None, :]
            out = jnp.stack([x1 * c - x2 * s, x1 * s + x2 * c], axis=-1)
            return out.reshape(x.shape)
        B, T, E = x.shape
        H = N_HEAD
        D = E // H
        q = (x @ wq).reshape(B, T, H, D)
        lat = x @ w_down
        k = (lat @ wk_up).reshape(B, T, H, D)
        v = (lat @ wv_up).reshape(B, T, H, D)
        cos, sin = _rope_tables(T, D, x.dtype)
        q = _apply_rope(q, cos, sin)
        k = _apply_rope(k, cos, sin)
        scale = 1.0 / jnp.sqrt(jnp.asarray(D, x.dtype))
        scores = jnp.einsum('bqhd,bkhd->bhqk', q, k) * scale
        pages = jnp.arange(T) // PAGE_SIZE
        allowed = pages[None, :] <= pages[:, None]
        scores = jnp.where(allowed[None, None], scores, jnp.finfo(scores.dtype).min)
        attn = jax.nn.softmax(scores, axis=-1)
        out = jnp.einsum('bhqk,bkhd->bqhd', attn, v).reshape(B, T, E)
        return out @ wo

    def _L0_xattn_ref(x, cross_input, Wk, bk, Wq, bq, Wv, bv, Wck, bck, Wcq, bcq, Wcv, bcv, Wp, bp):
        import jax, jax.numpy as jnp
        import numpy as np
        B, T, TC, C, CC, H = (2, 256, 64, 128, 64, 16)
        D = C // H

        def _heads(t):
            b, l, _ = t.shape
            return t.reshape(b, l, H, D).transpose(0, 2, 1, 3)
        scale = np.float32(1.0 / np.sqrt(D))
        q = _heads(x @ Wq + bq)
        k = _heads(x @ Wk + bk)
        v = _heads(x @ Wv + bv)
        att = jnp.einsum('bhqd,bhkd->bhqk', q, k) * scale
        causal = jnp.tril(jnp.ones((T, T), bool))
        att = jnp.where(causal[None, None], att, -jnp.inf)
        y = jnp.einsum('bhqk,bhkd->bhqd', jax.nn.softmax(att, axis=-1), v)
        qc = _heads(x @ Wcq + bcq)
        kc = _heads(cross_input @ Wck + bck)
        vc = _heads(cross_input @ Wcv + bcv)
        attc = jnp.einsum('bhqd,bhkd->bhqk', qc, kc) * scale
        y = y + jnp.einsum('bhqk,bhkd->bhqd', jax.nn.softmax(attc, axis=-1), vc)
        y = y.transpose(0, 2, 1, 3).reshape(x.shape[0], T, C)
        return y @ Wp + bp

    def _L0_ffn_ref(x, Wg, W1, b1, W2, b2):
        import jax, jax.numpy as jnp
        import numpy as np
        E = 8
        K = 2
        CAP_RATIO = 1.05
        B, S, D = x.shape
        T = B * S
        xf = x.reshape(T, D)
        gates = jax.nn.softmax(xf @ Wg.T, axis=-1)
        topw, topi = jax.lax.top_k(gates, K)
        C = int(round(K * T * CAP_RATIO / E))
        e_ord = topi.T.reshape(-1)
        tok_ord = jnp.tile(jnp.arange(T), K)
        oh = jax.nn.one_hot(e_ord, E, dtype=jnp.int32)
        cnt = jnp.take_along_axis(jnp.cumsum(oh, 0) - oh, e_ord[:, None], 1)[:, 0]
        within = cnt < C
        pos = jnp.where(within, cnt, C)
        x_disp = xf[tok_ord]
        buf = jnp.zeros((E, C + 1, D), xf.dtype).at[e_ord, pos].add(x_disp)[:, :C]
        h = jax.nn.gelu(jnp.einsum('ecd,edh->ech', buf, W1) + b1[:, None, :], approximate=False)
        y = jnp.einsum('ech,ehd->ecd', h, W2) + b2[:, None, :]
        y_ord = y[e_ord, jnp.minimum(pos, C - 1)] * within[:, None].astype(y.dtype)
        y_tk = y_ord.reshape(K, T, D).transpose(1, 0, 2)
        cw = topw * within.reshape(K, T).T.astype(topw.dtype)
        out = jnp.einsum('tk,tkd->td', cw, y_tk)
        return out.reshape(B, S, D)

    def _L1_attn_ref(x, norm1_g, norm1_b, qkv_w, proj_w, proj_b, norm2_g, norm2_b, fc1_w, fc1_b, fc2_w, fc2_b):
        import jax, jax.numpy as jnp
        import numpy as np
        DIM = 128
        HEADS = 16
        HIDDEN = 512
        EPS_ATTN = 1e-06
        EPS_LN = 1e-05

        def layer_norm(x, g, b):
            mu = jnp.mean(x, axis=-1, keepdims=True)
            var = jnp.var(x, axis=-1, keepdims=True)
            return (x - mu) * jax.lax.rsqrt(var + EPS_LN) * g + b
        B, N, C = x.shape
        H = HEADS
        d = C // H
        h = layer_norm(x, norm1_g, norm1_b)
        qkv = jnp.einsum('bnc,oc->bno', h, qkv_w)
        qkv = qkv.reshape(B, N, 3, H, d)
        q = jnp.transpose(qkv[:, :, 0], (0, 2, 1, 3))
        k = jnp.transpose(qkv[:, :, 1], (0, 2, 1, 3))
        v = jnp.transpose(qkv[:, :, 2], (0, 2, 1, 3))
        q = jax.nn.elu(q) + 1.0
        k = jax.nn.elu(k) + 1.0
        kv = jnp.einsum('bhnd,bhne->bhde', k, v)
        ksum = jnp.sum(k, axis=2)
        z = 1.0 / (jnp.einsum('bhnd,bhd->bhn', q, ksum) + EPS_ATTN)
        attn_out = jnp.einsum('bhnd,bhde->bhne', q, kv) * z[..., None]
        attn_out = jnp.transpose(attn_out, (0, 2, 1, 3)).reshape(B, N, C)
        attn_out = jnp.einsum('bnc,oc->bno', attn_out, proj_w) + proj_b
        x = x + attn_out
        h = layer_norm(x, norm2_g, norm2_b)
        h = jax.nn.gelu(jnp.einsum('bnc,hc->bnh', h, fc1_w) + fc1_b, approximate=False)
        h = jnp.einsum('bnh,ch->bnc', h, fc2_w) + fc2_b
        return x + h

    def _L1_xattn_ref(xx, ee, ln1_g, ln1_b, ln2_g, ln2_b, a1_wq, a1_wk, a1_wv, a1_li1_w, a1_li1_b, a1_lnx_g, a1_lnx_b, a1_lny_g, a1_lny_b, a1_ln3_g, a1_ln3_b, a1_li2_w, a1_li2_b, a1_li3_w, a1_li3_b, a2_wq, a2_wk, a2_wv, a2_li1_w, a2_li1_b, a2_lnx_g, a2_lnx_b, a2_lny_g, a2_lny_b, a2_ln3_g, a2_ln3_b, a2_li2_w, a2_li2_b, a2_li3_w, a2_li3_b, training):
        import jax, jax.numpy as jnp
        import numpy as np
        H, D, C1, C2, S, M, B, W = (16, 32, 128, 64, 256, 64, 2, 4)

        def _ln(x, g, b):
            m = jnp.mean(x, -1, keepdims=True)
            v = jnp.var(x, -1, keepdims=True)
            return (x - m) * jax.lax.rsqrt(v + 1e-05) * g + b

        def _mha(x, y, wq, wk, wv, li1_w, li1_b, lnx_g, lnx_b, lny_g, lny_b, ln3_g, ln3_b, li2_w, li2_b, li3_w, li3_b, causal):
            xn = _ln(x, lnx_g, lnx_b)
            yn = _ln(y, lny_g, lny_b)
            q = jnp.einsum('bsc,hcd->bhsd', xn, wq)
            k = jnp.einsum('btc,hcd->bhtd', yn, wk)
            v = jnp.einsum('btc,hcd->bhtd', yn, wv)
            a = jax.nn.softmax(jnp.einsum('bhsd,bhtd->bhst', q, k) * D ** (-0.5), axis=-1)
            if causal:
                s, t = (a.shape[-2], a.shape[-1])
                mask = (jnp.arange(t)[None, :] > jnp.arange(s)[:, None]).astype(a.dtype)
                a = a * mask
            o = jnp.einsum('bhst,bhtd->bhsd', a, v)
            o = o.transpose(0, 2, 1, 3).reshape(x.shape[0], x.shape[1], H * D)
            x_out = x + o @ li1_w + li1_b
            h = jax.nn.gelu(_ln(x_out, ln3_g, ln3_b) @ li2_w + li2_b, approximate=False)
            return x_out + h @ li3_w + li3_b
        x = _ln(xx, ln1_g, ln1_b)
        x = x + _mha(x, x, a1_wq, a1_wk, a1_wv, a1_li1_w, a1_li1_b, a1_lnx_g, a1_lnx_b, a1_lny_g, a1_lny_b, a1_ln3_g, a1_ln3_b, a1_li2_w, a1_li2_b, a1_li3_w, a1_li3_b, causal=True)
        x = _ln(x, ln2_g, ln2_b)
        return x + _mha(x, ee, a2_wq, a2_wk, a2_wv, a2_li1_w, a2_li1_b, a2_lnx_g, a2_lnx_b, a2_lny_g, a2_lny_b, a2_ln3_g, a2_ln3_b, a2_li2_w, a2_li2_b, a2_li3_w, a2_li3_b, causal=False)

    def _L1_ffn_ref(x, q_node_w, q_node_b, q_w1, q_b1, q_w2, q_b2, k_node_w, k_node_b, k_w1, k_b1, k_w2, k_b2, v_node_w, v_node_b, v_w1, v_b1, v_w2, v_b2):
        import jax, jax.numpy as jnp
        import numpy as np
        LATENT = 128
        LEAF_W = 64
        DEPTH = 4
        N_LEAVES = 2 ** DEPTH
        N_NODES = 2 ** DEPTH - 1
        B, S = (4, 256)

        def _fff_params(key, prefix):
            ks = jax.random.split(key, 4)
            d, h, l, n = (LATENT, LEAF_W, N_LEAVES, N_NODES)
            s_in = 1.0 / np.sqrt(d).astype(np.float32)
            s_h = 1.0 / np.sqrt(h).astype(np.float32)
            return {f'{prefix}_node_w': jax.random.normal(ks[0], (n, d), jnp.float32) * s_in, f'{prefix}_node_b': jax.random.normal(ks[1], (n,), jnp.float32) * s_in, f'{prefix}_w1': jax.random.normal(ks[2], (l, d, h), jnp.float32) * s_in, f'{prefix}_b1': jnp.zeros((l, h), jnp.float32), f'{prefix}_w2': jax.random.normal(ks[3], (l, h, d), jnp.float32) * s_h, f'{prefix}_b2': jnp.zeros((l, d), jnp.float32)}

        def _fff(x, node_w, node_b, w1, b1, w2, b2):
            Bx, Sx, D = x.shape
            xf = x.reshape(-1, D)
            N = xf.shape[0]
            cur = jnp.zeros((N,), jnp.int32)
            for _ in range(DEPTH):
                pw = node_w[cur]
                score = jnp.einsum('nd,nd->n', xf, pw) + node_b[cur]
                cur = 2 * cur + 1 + (score >= 0).astype(jnp.int32)
            leaf = cur - N_NODES
            sel = jax.nn.one_hot(leaf, N_LEAVES, dtype=xf.dtype)
            hidden_all = jax.nn.relu(jnp.einsum('nd,ldh->lnh', xf, w1) + b1[:, None, :])
            hidden = hidden_all * sel.T[:, :, None]
            out = jnp.einsum('lnh,lho->no', hidden, w2) + sel @ b2
            return out.reshape(Bx, Sx, D)
        q = _fff(x, q_node_w, q_node_b, q_w1, q_b1, q_w2, q_b2)
        k = _fff(x, k_node_w, k_node_b, k_w1, k_b1, k_w2, k_b2)
        v = _fff(x, v_node_w, v_node_b, v_w1, v_b1, v_w2, v_b2)
        scale = 1.0 / np.sqrt(LATENT).astype(np.float32)
        attn = jax.nn.softmax(jnp.einsum('bqd,bkd->bqk', q, k) * scale, axis=-1)
        return jnp.einsum('bqk,bkd->bqd', attn, v)
    x = x + _L0_attn_ref(_layernorm(x, axis=-1), L0_attn_wq, L0_attn_w_down, L0_attn_wk_up, L0_attn_wv_up, L0_attn_wo)
    x = x + _L0_xattn_ref(_layernorm(x, axis=-1), ctx_512, L0_xattn_Wk, L0_xattn_bk, L0_xattn_Wq, L0_xattn_bq, L0_xattn_Wv, L0_xattn_bv, L0_xattn_Wck, L0_xattn_bck, L0_xattn_Wcq, L0_xattn_bcq, L0_xattn_Wcv, L0_xattn_bcv, L0_xattn_Wp, L0_xattn_bp)
    x = x + _L0_ffn_ref(_layernorm(x, axis=-1), L0_ffn_Wg, L0_ffn_W1, L0_ffn_b1, L0_ffn_W2, L0_ffn_b2)
    x = x + _L1_attn_ref(_layernorm(x, axis=-1), L1_attn_norm1_g, L1_attn_norm1_b, L1_attn_qkv_w, L1_attn_proj_w, L1_attn_proj_b, L1_attn_norm2_g, L1_attn_norm2_b, L1_attn_fc1_w, L1_attn_fc1_b, L1_attn_fc2_w, L1_attn_fc2_b)
    x = x + _L1_xattn_ref(_layernorm(x, axis=-1), ctx_512, L1_xattn_ln1_g, L1_xattn_ln1_b, L1_xattn_ln2_g, L1_xattn_ln2_b, L1_xattn_a1_wq, L1_xattn_a1_wk, L1_xattn_a1_wv, L1_xattn_a1_li1_w, L1_xattn_a1_li1_b, L1_xattn_a1_lnx_g, L1_xattn_a1_lnx_b, L1_xattn_a1_lny_g, L1_xattn_a1_lny_b, L1_xattn_a1_ln3_g, L1_xattn_a1_ln3_b, L1_xattn_a1_li2_w, L1_xattn_a1_li2_b, L1_xattn_a1_li3_w, L1_xattn_a1_li3_b, L1_xattn_a2_wq, L1_xattn_a2_wk, L1_xattn_a2_wv, L1_xattn_a2_li1_w, L1_xattn_a2_li1_b, L1_xattn_a2_lnx_g, L1_xattn_a2_lnx_b, L1_xattn_a2_lny_g, L1_xattn_a2_lny_b, L1_xattn_a2_ln3_g, L1_xattn_a2_ln3_b, L1_xattn_a2_li2_w, L1_xattn_a2_li2_b, L1_xattn_a2_li3_w, L1_xattn_a2_li3_b, 0)
    x = x + _L1_ffn_ref(_layernorm(x, axis=-1), L1_ffn_q_node_w, L1_ffn_q_node_b, L1_ffn_q_w1, L1_ffn_q_b1, L1_ffn_q_w2, L1_ffn_q_b2, L1_ffn_k_node_w, L1_ffn_k_node_b, L1_ffn_k_w1, L1_ffn_k_b1, L1_ffn_k_w2, L1_ffn_k_b2, L1_ffn_v_node_w, L1_ffn_v_node_b, L1_ffn_v_w1, L1_ffn_v_b1, L1_ffn_v_w2, L1_ffn_v_b2)
    return x

_drawn_inputs = setup_inputs


def setup_inputs(seed=0):
    import zlib

    import numpy as np

    out = dict(_drawn_inputs(seed))
    spreads = {'L0_xattn_bk': (0.0, 2.0),
     'L0_xattn_bq': (0.0, 0.461),
     'L0_xattn_bv': (0.0, 0.1),
     'L0_xattn_bck': (0.0, 2.0),
     'L0_xattn_bcq': (0.0, 0.39),
     'L0_xattn_bcv': (0.0, 0.1),
     'L0_xattn_bp': (0.0, 0.1),
     'L0_ffn_b1': (0.0, 0.8),
     'L0_ffn_b2': (0.0, 0.436),
     'L1_attn_norm1_g': (1.0, 0.6),
     'L1_attn_norm1_b': (0.0, 0.8),
     'L1_attn_proj_b': (0.0, 0.1),
     'L1_attn_norm2_g': (1.0, 0.6),
     'L1_attn_norm2_b': (0.0, 0.8),
     'L1_attn_fc1_b': (0.0, 0.761),
     'L1_attn_fc2_b': (0.0, 0.1),
     'L1_xattn_ln1_g': (1.0, 0.2),
     'L1_xattn_ln1_b': (0.0, 0.1),
     'L1_xattn_ln2_g': (1.0, 0.2),
     'L1_xattn_ln2_b': (0.0, 0.1),
     'L1_xattn_a1_li1_b': (0.0, 0.348),
     'L1_xattn_a1_lnx_g': (1.0, 0.6),
     'L1_xattn_a1_lnx_b': (0.0, 0.8),
     'L1_xattn_a1_lny_g': (1.0, 0.6),
     'L1_xattn_a1_lny_b': (0.0, 0.8),
     'L1_xattn_a1_ln3_g': (1.0, 0.6),
     'L1_xattn_a1_ln3_b': (0.0, 0.8),
     'L1_xattn_a1_li2_b': (0.0, 0.8),
     'L1_xattn_a1_li3_b': (0.0, 0.333),
     'L1_xattn_a2_li1_b': (0.0, 0.36),
     'L1_xattn_a2_lnx_g': (1.0, 0.6),
     'L1_xattn_a2_lnx_b': (0.0, 0.8),
     'L1_xattn_a2_lny_g': (1.0, 0.6),
     'L1_xattn_a2_lny_b': (0.0, 0.8),
     'L1_xattn_a2_ln3_g': (1.0, 0.6),
     'L1_xattn_a2_ln3_b': (0.0, 0.8),
     'L1_xattn_a2_li2_b': (0.0, 0.8),
     'L1_xattn_a2_li3_b': (0.0, 0.339),
     'L1_ffn_q_b1': (0.0, 0.8),
     'L1_ffn_q_b2': (0.0, 0.8),
     'L1_ffn_k_b1': (0.0, 0.8),
     'L1_ffn_k_b2': (0.0, 2.0),
     'L1_ffn_v_b1': (0.0, 0.8),
     'L1_ffn_v_b2': (0.0, 0.8)}
    factors = {'L0_ffn_Wg': 3.009,
     'L0_ffn_W1': 5.595,
     'L0_ffn_W2': 5.133,
     'L1_attn_qkv_w': 4.428,
     'L1_attn_proj_w': 4.596,
     'L1_xattn_a1_wq': 8.0,
     'L1_xattn_a1_wk': 8.0,
     'L1_xattn_a1_wv': 8.0,
     'L1_xattn_a1_li1_w': 7.772,
     'L1_xattn_a1_li2_w': 4.438,
     'L1_xattn_a1_li3_w': 4.067,
     'L1_xattn_a2_wq': 8.0,
     'L1_xattn_a2_wk': 8.0,
     'L1_xattn_a2_wv': 5.494,
     'L1_xattn_a2_li1_w': 5.652,
     'L1_xattn_a2_li2_w': 4.166,
     'L1_xattn_a2_li3_w': 3.828,
     'L1_ffn_q_node_w': 8.0,
     'L1_ffn_q_node_b': 8.0,
     'L1_ffn_q_w1': 8.0,
     'L1_ffn_q_w2': 8.0,
     'L1_ffn_k_node_w': 8.0,
     'L1_ffn_k_node_b': 8.0,
     'L1_ffn_k_w1': 8.0,
     'L1_ffn_k_w2': 8.0,
     'L1_ffn_v_node_b': 6.929}
    for name, (base, spread) in spreads.items():
        noise = np.random.default_rng([zlib.crc32(name.encode()), seed]).standard_normal(out[name].shape)
        drawn = base * np.exp(spread * noise) if base else spread * noise
        out[name] = jnp.asarray(drawn.astype(out[name].dtype))
    for name, factor in factors.items():
        out[name] = (out[name] * factor).astype(out[name].dtype)
    return out
```

```python
from contextlib import ExitStack

import concourse.bass as bass
from concourse import mybir

F32 = mybir.dt.float32
BF16 = mybir.dt.bfloat16
ACT = mybir.ActivationFunctionType
ALU = mybir.AluOpType
AX = mybir.AxisListType

P = 128
BATCH, SEQ, CTX = 8, 256, 64
TOKENS = BATCH * SEQ
HALF = 512
PASS = 1024
PASSES = TOKENS // PASS
HALVES = PASS // HALF
PB = PASS // SEQ
TILES = PASS // P
HEADS, GROUPS = 16, 4
EXPERTS, HID = 8, 512
CAPACITY = int(round(2 * TOKENS * 1.05 / EXPERTS))
LEAVES, NODES, LEAF = 16, 15, 64
EPS = 1e-5
MASKED = -1e30
OFF = 1e30


class Marks:

    def __init__(self, nc, ctx, known):
        self.nc, self.ctx, self.known = nc, ctx, known
        self.sems, self.count, self.where = {}, {}, "start"
        self.found = {}

    def sem(self, kind):
        if kind not in self.sems:
            self.sems[kind] = self.ctx.enter_context(self.nc.semaphore(kind))
        return self.sems[kind]

    def begin(self, where):
        self.where, self.count = where, {}

    def done(self, kind, *key, n=1):
        self.count[kind] = self.count.get(kind, 0) + n
        name = (self.where, kind) + key
        assert name not in self.found, name
        self.found[name] = self.count[kind]
        return self.sem(kind), n

    def since(self, kind, *key):
        name = (self.where, kind) + key
        if self.known is None:
            return self.sem(kind), 1
        return self.sem(kind), self.known[name]


class Ring:

    def __init__(self, marks, name, banks):
        self.marks, self.name, self.banks = marks, name, banks
        self.claimed, self.order = {}, []
        self.freed_count = 0

    def begin(self):
        self.claimed, self.freed_count = {}, 0

    def claim(self, *key):
        assert key not in self.claimed, key
        self.claimed[key] = len(self.claimed)
        return self.bank(*key)

    def bank(self, *key):
        n = len(self.banks)
        return self.banks[self.claimed[key] % n]

    def pair(self, key):
        assert self.claimed[key] % 2 == 0
        return self.claimed[key] % len(self.banks)

    def reused(self, *key):
        return self.claimed[key] >= len(self.banks)

    def room(self, *key):
        return self.marks.sem(self.name + "_freed"), self.claimed[key] - len(self.banks) + 1

    def fill(self, *key):
        return self.marks.sem(self.name + "_filled"), 1

    def full(self, *key):
        return self.marks.sem(self.name + "_filled"), self.claimed[key] + 1

    def free(self, *keys):
        for key in keys:
            assert self.claimed[key] == self.freed_count, (self.name, key, self.claimed[key], self.freed_count)
            self.freed_count += 1
        return self.marks.sem(self.name + "_freed"), len(keys)

    def freed(self, *key):
        return self.marks.sem(self.name + "_freed"), self.claimed[key] + 1


VECTORS = [
    ("x_bq", 4), ("x_bk", 4), ("x_bcq", 4), ("x_bck", 4), ("x_bp", 1),
    ("moe_b1", 32),
    ("n1_g", 1), ("n1_b", 1), ("proj_b", 1), ("n2_g", 1), ("n2_b", 1), ("fc1_b", 4), ("fc2_b", 1),
    ("ln1_g", 1), ("ln1_b", 1), ("ln2_g", 1), ("ln2_b", 1),
] + [(f"{a}_{v}", n) for a in ("a1", "a2") for v, n in (
    ("lnx_g", 1), ("lnx_b", 1), ("lny_g", 1), ("lny_b", 1), ("li1_b", 1), ("ln3_g", 1), ("ln3_b", 1),
    ("li2_b", 4), ("li3_b", 1))] + [("f_b1", 24), ("eps", 1)]
VCOL, _at = {}, 0
for _name, _n in VECTORS:
    VCOL[_name] = (_at, _n)
    _at += _n
NVEC = _at

CONSTS = [("ident", 128), ("center", 128), ("mean", 128), ("center64", 64), ("mean64", 64), ("ones", 128),
          ("page", 128), ("pageT", 128), ("causal", 128), ("causalT", 128), ("upper", 128),
          ("before", 128), ("blocks", 128), ("prio", 8), ("headrows", 4)]
TO_BF16 = ["ident", "page", "pageT", "causal", "causalT", "before", "ones"]
LAYER0 = [("wq", 512), ("wqs", 512), ("w_down", 64), ("wk", 512), ("wks", 512), ("wv", 128), ("wo", 512),
          ("xq", 512), ("xk", 512), ("xv", 128), ("cq", 512), ("ck", 512), ("cv", 128), ("wp", 512),
          ("cos", 256), ("sin", 256), ("bv", 128), ("bcv", 128)]
MOE = [("experts", EXPERTS * 2 * HID)]
FEED = [("f_w1", 3072), ("f_w2", 3072)]
LAYER1 = [("qkv", 384), ("proj", 128), ("fc1", 512), ("fc2", 512)] + [
    (f"{a}_{w}", 512) for a in ("a1", "a2") for w in ("q", "k", "v", "li1", "li2", "li3")] + [
    ("nodes", 45), ("node_b", 45)]


def columns(parts):
    at, out = 0, {}
    for name, n in parts:
        out[name] = (at, n)
        at += n
    return out, at


class Chip:

    def __init__(self, nc, ctx, marks):
        def sb(name, shape, dt=F32):
            return ctx.enter_context(nc.sbuf_tensor(name, shape, dt))
        self.m = marks
        self.vec = sb("vec", [P, NVEC])
        self.ccol, n = columns(CONSTS)
        self.const = sb("const", [P, n])
        self.bcol, n = columns([(x, P) for x in TO_BF16])
        self.bf = sb("bf", [P, n], BF16)
        self.l0col, n0 = columns(LAYER0)
        self.mcol, nm = columns(MOE)
        self.fcol, nf = columns(FEED)
        self.early = sb("early", [P, max(n0, nm)])
        self.l1col, n1 = columns(LAYER1)
        self.late = sb("late", [P, n1])
        self.n0, self.nm, self.n1, self.nf = n0, nm, n1, nf
        self.headsel = sb("headsel", [P, HEADS, P], BF16)
        self.leafsel = sb("leafsel", [48, 24, P], BF16)
        self.small = sb("small", [48, 3 * P + 8 * P + P])
        self.logits = sb("logits", [P, TOKENS // P, EXPERTS])
        self.weight = sb("weight", [P, TOKENS // P, EXPERTS])
        self.weight_now = sb("weight_now", [P, TILES, EXPERTS])
        self.xw = sb("xw", [P, PASS])
        self.ctx = sb("ctx", [CTX, PASS])
        self.xn = sb("xn", [P, PASS])
        self.sq = sb("sq", [P, PASS])
        self.rstd = self.sq
        self.ya = sb("ya", [P, PASS])
        self.yb = sb("yb", [P, PASS])
        self.yc = sb("yc", [P, PASS])
        self.q = sb("q", [P, GROUPS, PASS])
        self.k = sb("k", [P, GROUPS, PASS])
        self.qb = sb("qb", [P, GROUPS, PASS], BF16)
        self.kb = sb("kb", [P, GROUPS, PASS], BF16)
        self.v = sb("v", [P, TILES, HEADS, 32])
        self.prob = sb("prob", [P, 4, 2, HALF])
        self.kept = sb("kept", [P, 2, 2, 2, P])
        self.maxes = sb("maxes", [P, 2, HEADS, 3])
        self.negmax = sb("negmax", [P, 2, 2, HEADS])
        self.shift = sb("shift", [P, 2, SEQ], BF16)
        self.recip = sb("recip", [P, 2, SEQ])
        self.gate = self.q[:, 0:2, :].rearrange("p a t -> p (a t)")[:, 0:12 * P].rearrange(
            "p (a n e) -> p a n e", a=12, e=EXPERTS)
        self.gcol = sb("gcol", [P, 8, 16])
        self.onehot = sb("onehot", [P, 2, 16, EXPERTS], BF16)
        flat = self.prob.rearrange("p a i t -> p (a i t)")
        self.tree = flat[:, 0:2 * TILES * 48].rearrange("p (a t n) -> p a t n", a=2, n=48)
        self.treeb = flat[:, 2 * TILES * 48:3 * TILES * 48].rearrange("p (t n) -> p t n", n=48)
        self.lt = self.ctx[0:48, :]
        self.lm = sb("lm", [48, PASS], BF16)
        self.share = self.lt[0:EXPERTS, :]
        self.stat = sb("stat", [P, 2, 8])
        self.ps = ctx.enter_context(nc.psum_tensor("ps", [P, 8, HALF], F32))
        banks = [self.ps[:, i, :] for i in range(8)]
        self.rv = Ring(marks, "rv", banks[0:2])
        self.ro = Ring(marks, "ro", banks[2:4])
        self.ra = Ring(marks, "ra", banks[4:8])
        self.bands = None

    def begin(self, where):
        self.m.begin(where)
        for r in (self.rv, self.ro, self.ra):
            r.begin()

    def C(self, name, rows=P):
        a, n = self.ccol[name]
        return self.const[0:rows, a:a + n]

    def B(self, name):
        a, n = self.bcol[name]
        return self.bf[:, a:a + n]

    def W0(self, name, rows=P):
        a, n = self.l0col[name]
        return self.early[0:rows, a:a + n]

    def expert(self, e, which, m):
        at = (2 * e + which) * HID + m * P
        return self.early[:, at:at + P]

    def WF(self, name):
        a, n = self.fcol[name]
        return self.early[:, a:a + n]

    def W1(self, name, rows=P):
        a, n = self.l1col[name]
        return self.late[0:rows, a:a + n]

    def V(self, name, i=0, rows=P):
        a = VCOL[name][0]
        return self.vec[0:rows, a + i:a + i + 1]

    def ra_pair(self, *key):
        at = 4 + self.ra.pair(key)
        return self.ps[:, at:at + 2, :]


def half(s):
    return slice(s * HALF, (s + 1) * HALF)


def tile(t):
    return slice(t * P, (t + 1) * P)


def seq(b):
    return slice(b * SEQ, (b + 1) * SEQ)



def norm_pe(K, pe, name, src, ready, rows=P):
    c, m = ("center", "mean") if rows == P else ("center64", "mean64")
    for s in range(HALVES):
        bank = K.rv.claim(name, "c", s)
        for w in ready(s):
            pe.wait_ge(*w)
        if K.rv.reused(name, "c", s):
            pe.wait_ge(*K.rv.room(name, "c", s))
        pe.matmul(bank[0:rows, :], K.C(c, rows), src[0:rows, half(s)], start=True, stop=True).then_inc(
            *K.rv.fill(name, "c", s))
    for s in range(HALVES):
        bank = K.ra.claim(name, "v", s)
        pe.wait_ge(*K.m.since("squared", name, s))
        if K.ra.reused(name, "v", s):
            pe.wait_ge(*K.ra.room(name, "v", s))
        pe.matmul(bank[0:rows, :], K.C(m, rows), K.sq[0:rows, half(s)], start=True, stop=True).then_inc(
            *K.ra.fill(name, "v", s))


def both_tables(act):
    act.preload_act_table_set("natural_log_exp_and_others")


def norm_act(K, act, name, rows=P):
    for s in range(HALVES):
        act.wait_ge(*K.rv.full(name, "c", s))
        act.activation(K.sq[0:rows, half(s)], K.rv.bank(name, "c", s)[0:rows, :], ACT.Square).then_inc(
            *K.m.done("squared", name, s))
    for s in range(HALVES):
        act.wait_ge(*K.ra.full(name, "v", s))
        act.activation(K.rstd[0:rows, half(s)], K.ra.bank(name, "v", s)[0:rows, :], ACT.Ln,
                       bias=K.V("eps", rows=rows)).then_inc(*K.ra.free((name, "v", s)))
        act.wait_ge(*K.ra.freed(name, "v", s))
        act.activation(K.rstd[0:rows, half(s)], K.rstd[0:rows, half(s)], ACT.Exp, scale=-0.5).then_inc(
            *K.m.done("rstd", name, s))


def norm_dve(K, dve, name, dst, affine=None, second=None, rows=P):
    for s in range(HALVES):
        dve.wait_ge(*K.m.since("rstd", name, s))
        dve.tensor_tensor(dst[0:rows, half(s)], K.rv.bank(name, "c", s)[0:rows, :], K.rstd[0:rows, half(s)],
                          ALU.mult).then_inc(*K.rv.free((name, "c", s)))
    for s in range(HALVES):
        if second:
            other, g, b = second
            dve.wait_ge(*K.rv.freed(name, "c", s))
            dve.tensor_scalar(other[0:rows, half(s)], dst[0:rows, half(s)], K.V(g, rows=rows), K.V(b, rows=rows),
                              ALU.mult, ALU.add).then_inc(*K.m.done("affine", name, "second", s))
            dve.wait_ge(*K.m.since("affine", name, "second", s))
        if affine:
            g, b = affine
            dve.wait_ge(*K.rv.freed(name, "c", s))
            dve.tensor_scalar(dst[0:rows, half(s)], dst[0:rows, half(s)], K.V(g, rows=rows), K.V(b, rows=rows),
                              ALU.mult, ALU.add).then_inc(*K.m.done("affine", name, s))


def normed(K, name):
    return lambda s: [K.rv.freed(name, "c", s)]


def affined(K, name):
    return lambda s: [K.m.since("affine", name, s)]



def project_pe(K, pe, name, weights, src, ready, rows=P, outs=P):
    for g, w in enumerate(weights):
        for s in range(HALVES):
            bank = K.ra.claim(name, g, s)
            if g == 0:
                for x in ready(s):
                    pe.wait_ge(*x)
            if K.ra.reused(name, g, s):
                pe.wait_ge(*K.ra.room(name, g, s))
            pe.matmul(bank[0:outs, :], w, src[0:rows, half(s)], start=True, stop=True).then_inc(
                *K.ra.fill(name, g, s))


def project_act(K, act, name, count, dst, func, bias=None, after=None, outs=P):
    for g in range(count):
        if after:
            for w in after(g):
                act.wait_ge(*w)
        act.wait_ge(*K.ra.full(name, g, 1))
        pair = K.ra_pair(name, g, 0)
        act.activation(dst(g)[0:outs].rearrange("p (s t) -> p s t", s=HALVES), pair[0:outs], func,
                       bias=bias(g) if bias else 0.0).then_inc(*K.ra.free((name, g, 0), (name, g, 1)))


def projected(K, name, g):
    return [K.ra.freed(name, g, 1)]


def as_bf16(K, pool, name, count, src, dst):
    for g in range(count):
        pool.wait_ge(*K.ra.freed(name, g, 1))
        pool.tensor_copy(dst[:, g, :], src[:, g, :]).then_inc(*K.m.done("rounded", name, g))



def rope_pe(K, pe, name, w, ws, src, ready, rows):
    for g in range(GROUPS):
        for s in range(HALVES):
            for part, mat in (("plain", w), ("swapped", ws)):
                bank = K.rv.claim(name, g, s, part)
                if g == 0 and part == "plain":
                    for x in ready(s):
                        pe.wait_ge(*x)
                if K.rv.reused(name, g, s, part):
                    pe.wait_ge(*K.rv.room(name, g, s, part))
                pe.matmul(bank, mat[:, g * P:(g + 1) * P], src[0:rows, half(s)], start=True, stop=True).then_inc(
                    *K.rv.fill(name, g, s, part))


def rope_dve(K, dve, name, dst, before=None):
    cos = K.W0("cos").unsqueeze(1).broadcast_to((P, 2, SEQ))
    sin = K.W0("sin").unsqueeze(1).broadcast_to((P, 2, SEQ))
    for g in range(GROUPS):
        for s in range(HALVES):
            out = dst[:, g, half(s)].rearrange("p (b t) -> p b t", b=2)
            tmp = (K.ya, K.yb)[s][:, (g % 2) * HALF:(g % 2 + 1) * HALF].rearrange("p (b t) -> p b t", b=2)
            dve.wait_ge(*K.rv.full(name, g, s, "plain"))
            dve.tensor_tensor(out, K.rv.bank(name, g, s, "plain").rearrange("p (b t) -> p b t", b=2), cos,
                              ALU.mult).then_inc(*K.rv.free((name, g, s, "plain")))
            dve.wait_ge(*K.rv.full(name, g, s, "swapped"))
            if g >= 2:
                dve.wait_ge(*K.m.since("rotated", name, g - 2, s))
            elif before:
                dve.wait_ge(*K.m.since("rotated", before, g + 2, s))
            dve.tensor_tensor(tmp, K.rv.bank(name, g, s, "swapped").rearrange("p (b t) -> p b t", b=2), sin,
                              ALU.mult).then_inc(*K.rv.free((name, g, s, "swapped")))


def rope_pool(K, pool, name, dst, dstb):
    for g in range(GROUPS):
        for s in range(HALVES):
            tmp = (K.ya, K.yb)[s][:, (g % 2) * HALF:(g % 2 + 1) * HALF]
            pool.wait_ge(*K.rv.freed(name, g, s, "swapped"))
            pool.tensor_tensor(dst[:, g, half(s)], dst[:, g, half(s)], tmp, ALU.add).then_inc(
                *K.m.done("rotated", name, g, s))
        pool.wait_ge(*K.m.since("rotated", name, g, 1))
        pool.tensor_copy(dstb[:, g, :], dst[:, g, :]).then_inc(*K.m.done("rounded", name, g))



def values_pe(K, pe, name, w, src, ready, rows, wide):
    if wide:
        for t in range(TILES):
            bank = K.ra.claim(name, "v", t)
            for x in ready(t // 4):
                pe.wait_ge(*x)
            if K.ra.reused(name, "v", t):
                pe.wait_ge(*K.ra.room(name, "v", t))
            pe.matmul(bank, src[0:rows, tile(t)], w, start=True, stop=True).then_inc(*K.ra.fill(name, "v", t))
        return
    for s in range(HALVES):
        bank = K.rv.claim(name, "v", s)
        for x in ready(s):
            pe.wait_ge(*x)
        if K.rv.reused(name, "v", s):
            pe.wait_ge(*K.rv.room(name, "v", s))
        for i in range(4):
            mm = pe.matmul(bank[:, tile(i)], src[0:rows, tile(4 * s + i)], w, start=True, stop=True)
        mm.then_inc(*K.rv.fill(name, "v", s))


def values_act(K, act, name):
    for t in range(0, TILES, 2):
        act.wait_ge(*K.ra.full(name, "v", t + 1))
        act.activation(K.v[:, t:t + 2, :, :].rearrange("p a h d -> p a (h d)"), K.ra_pair(name, "v", t),
                       ACT.Copy).then_inc(*K.ra.free((name, "v", t), (name, "v", t + 1)))


def values_dve(K, dve, name, bias):
    for s in range(HALVES):
        src = K.rv.bank(name, "v", s).rearrange("p (a h d) -> p a h d", a=4, h=HEADS)
        dve.wait_ge(*K.rv.full(name, "v", s))
        for i in range(4):
            dst = K.v[:, 4 * s + i, :, 0:8]
            if bias is None:
                op = dve.tensor_copy(dst, src[:, i])
            else:
                op = dve.tensor_tensor(dst, src[:, i], bias.rearrange("p (h d) -> p h d", h=HEADS), ALU.add)
            if i < 3:
                op.then_inc(*K.m.done("value", name, 4 * s + i))
        op.then_inc(*K.rv.free((name, "v", s)))



def masked(kind):
    return kind in ("page", "causal")


def scores_pe(K, pe, name, b, g, j, dims, kind, ready):
    h, rows = 4 * g + j, slice(32 * j, 32 * j + dims)
    bank = K.rv.claim(name, "s", b, h)
    if b == 0 and j == 0:
        for w in ready(g):
            pe.wait_ge(*w)
    if K.rv.reused(name, "s", b, h):
        pe.wait_ge(*K.rv.room(name, "s", b, h))
    q0, q1 = slice(b * SEQ, b * SEQ + P), slice(b * SEQ + P, (b + 1) * SEQ)
    if masked(kind):
        diagonal = bank.rearrange("p (a k) -> p a k", a=4)[:, 0:3:2, :]
        pe.matmul(diagonal, K.B("ident"), K.B(kind).unsqueeze(1).broadcast_to((P, 2, P)), start=True, stop=False,
                  skip_group_check=True)
        pe.matmul(bank[:, 0:P], K.qb[rows, g, q0], K.kb[rows, g, q0], start=False, stop=False,
                  skip_group_check=True)
        mm = pe.matmul(bank[:, P:3 * P], K.qb[rows, g, q1], K.kb[rows, g, seq(b)], start=False, stop=True,
                       skip_group_check=True)
    else:
        pe.matmul(bank[:, 0:SEQ], K.qb[rows, g, q0], K.kb[rows, g, seq(b)], start=True, stop=False,
                  skip_group_check=True)
        mm = pe.matmul(bank[:, SEQ:], K.qb[rows, g, q1], K.kb[rows, g, seq(b)], start=False, stop=True,
                       skip_group_check=True)
    mm.then_inc(*K.rv.fill(name, "s", b, h))


def maxima_dve(K, dve, name, b, g, j, kind):
    h = 4 * g + j
    n, w = (3, P) if masked(kind) else (2, SEQ)
    src = K.rv.bank(name, "s", b, h)[:, 0:n * w].rearrange("p (a k) -> p a k", a=n)
    dve.wait_ge(*K.rv.full(name, "s", b, h))
    dve.tensor_reduce(K.maxes[:, b % 2, h, 0:n], src, AX.X, ALU.max).then_inc(*K.rv.free((name, "s", b, h)))


def shift_dve(K, dve, name, b, kind):
    m, out = K.maxes[:, b % 2], K.negmax[:, b % 2]
    dve.wait_ge(*K.rv.freed(name, "s", b, HEADS - 1))
    if masked(kind):
        dve.tensor_tensor(m[:, :, 1], m[:, :, 1], m[:, :, 2], ALU.max).then_inc(*K.m.done("joined", name, b))
        dve.wait_ge(*K.m.since("joined", name, b))
    dve.tensor_scalar(out, m[:, :, 0:2].rearrange("p h a -> p a h"), -1.0, None, ALU.mult).then_inc(
        *K.m.done("negated", name, b))


def turn_pe(K, pe, name, b):
    bank = K.ro.claim(name, "m", b)
    pe.wait_ge(*K.m.since("negated", name, b))
    if K.ro.reused(name, "m", b):
        pe.wait_ge(*K.ro.room(name, "m", b))
    for a in range(2):
        mm = pe.transpose(bank[0:HEADS, tile(a)], K.negmax[:, b % 2, a, :], K.C("ident"))
    mm.then_inc(*K.ro.fill(name, "m", b))


def turned_dve(K, dve, name, b):
    dve.wait_ge(*K.ro.full(name, "m", b))
    if b >= 2:
        dve.wait_ge(*K.ra.full(name, "t", b - 2, HEADS - 1))
    dve.tensor_copy(K.shift[0:HEADS, b % 2, :], K.ro.bank(name, "m", b)[0:HEADS, 0:SEQ]).then_inc(
        *K.ro.free((name, "m", b)))


BANDS = 4


def band_ring(where):
    return where[:, 0:BANDS * 4 * SEQ].rearrange("p (n j t) -> p n j t", n=BANDS, j=4)


def banded(j):
    return "banded_v" if j < 2 else "banded_p"


def bands(K, eng, name, b, g, heads, ready):
    u = GROUPS * b + g
    if b == 0:
        for w in ready(g):
            eng.wait_ge(*w)
    if u >= BANDS:
        ub, ug = divmod(u - BANDS, GROUPS)
        eng.wait_ge(*K.ra.full(name, "t", ub, 4 * ug + 3))
    for j in heads:
        eng.tensor_scalar(K.bands[:, u % BANDS, j, :], K.q[:, g, seq(b)], K.C("headrows")[:, j:j + 1], None,
                           ALU.mult).then_inc(*K.m.done(banded(j), name, b, g, j))


def exact_pe(K, pe, name, b, g, j, kind, ready):
    h = 4 * g + j
    query = K.bands[:, (GROUPS * b + g) % BANDS, j, :]
    bank = K.ra.claim(name, "t", b, h)
    pe.wait_ge(*K.m.since(banded(j), name, b, g, j))
    if h == 0:
        pe.wait_ge(*K.ro.freed(name, "m", b))
    if b == 0 and j == 0:
        for w in ready(g):
            pe.wait_ge(*w)
    if K.ra.reused(name, "t", b, h):
        pe.wait_ge(*K.ra.room(name, "t", b, h))
    k0, k1 = slice(b * SEQ, b * SEQ + P), slice(b * SEQ + P, (b + 1) * SEQ)
    shift = K.shift[:, b % 2, :]
    if masked(kind):
        pe.matmul(bank[:, 0:SEQ], K.headsel[:, h, :], shift, start=True, stop=False, skip_group_check=True)
        pe.matmul(bank[:, SEQ:3 * P], K.headsel[:, h, :], shift[:, P:], start=False, stop=False,
                  skip_group_check=True)
        diagonal = bank.rearrange("p (a k) -> p a k", a=4)[:, 0:3:2, :]
        pe.matmul(diagonal, K.B("ident"), K.B(kind + "T").unsqueeze(1).broadcast_to((P, 2, P)), start=False,
                  stop=False, skip_group_check=True)
        pe.matmul(bank[:, 0:SEQ], K.k[:, g, k0], query, start=False, stop=False,
                  skip_group_check=True)
        mm = pe.matmul(bank[:, SEQ:3 * P], K.k[:, g, k1], query[:, P:], start=False, stop=True,
                       skip_group_check=True)
    else:
        pe.matmul(bank, K.headsel[:, h, :], shift.unsqueeze(1).broadcast_to((P, 2, SEQ)), start=True, stop=False,
                  skip_group_check=True)
        pe.matmul(bank[:, 0:SEQ], K.k[:, g, k0], query, start=False, stop=False,
                  skip_group_check=True)
        mm = pe.matmul(bank[:, SEQ:], K.k[:, g, k1], query, start=False, stop=True,
                       skip_group_check=True)
    mm.then_inc(*K.ra.fill(name, "t", b, h))


def slot(b, g, i):
    return (2 * (GROUPS * b + g) + i) % 4


def exps_act(K, act, name, b, g, kind, scale):
    n = 3 * P if masked(kind) else HALF
    for i in range(2):
        h = 4 * g + 2 * i
        u = GROUPS * b + g
        if u >= 2:
            ub, ug = divmod(u - 2, GROUPS)
            act.wait_ge(*K.ro.full(name, "o", ub, ug))
        act.wait_ge(*K.ra.full(name, "t", b, h + 1))
        act.activation(K.prob[:, slot(b, g, i), :, 0:n], K.ra_pair(name, "t", b, h)[:, :, 0:n], ACT.Exp,
                       scale=scale).then_inc(*K.ra.free((name, "t", b, h), (name, "t", b, h + 1)))


def kept_pool(K, pool, name, b, g):
    u = GROUPS * b + g
    for i in range(2):
        for a in range(2):
            src = K.prob[:, slot(b, g, i), a, :].rearrange("p (c q) -> p c q", c=4)[:, 0:4:3, :]
            if i == 0 and a == 0 and u >= 1:
                ub, ug = divmod(u - 1, GROUPS)
                pool.wait_ge(*K.ro.full(name, "o", ub, ug))
            pool.wait_ge(*K.ra.freed(name, "t", b, 4 * g + 2 * i + 1))
            pool.tensor_tensor(K.kept[:, i, a, :, :], src, K.C("upper").unsqueeze(1).broadcast_to((P, 2, P)),
                               ALU.mult).then_inc(*K.m.done("kept", name, b, g, i, a))


def weigh_pe(K, pe, name, b, g, kind, ready):
    bank = K.ro.claim(name, "o", b, g)
    if b == 0 and g == 0:
        for w in ready:
            pe.wait_ge(*w)
    pe.wait_ge(*K.ra.freed(name, "t", b, 4 * g + 3))
    if kind == "upper":
        pe.wait_ge(*K.m.since("kept", name, b, g, 1, 1))
    if K.ro.reused(name, "o", b, g):
        pe.wait_ge(*K.ro.room(name, "o", b, g))

    def e(j, lo, hi):
        return K.prob[:, slot(b, g, j // 2), j % 2, lo:hi]

    ones = K.C("ones")[:, 0:32]
    steps = []
    if masked(kind):
        steps = [("v", 0, 0, SEQ, 0), ("v", 1, P, SEQ, SEQ), ("one", 0, 0, SEQ, 0), ("one", 1, P, SEQ, SEQ)]
    elif kind == "all":
        steps = [("v", 0, 0, SEQ, 0), ("v", 1, 0, SEQ, SEQ), ("one", 0, 0, SEQ, 0), ("one", 1, 0, SEQ, SEQ)]
    else:
        steps = [("keep", 0, 0, P, 0), ("v", 1, 0, P, SEQ), ("keep", 1, P, SEQ, 0),
                 ("one", 0, 0, SEQ, 0), ("one", 1, 0, SEQ, SEQ)]
    for n, (what, kc, q0, q1, col) in enumerate(steps):
        for j in range(4):
            h = 4 * g + j
            value = K.v[:, 2 * b + kc, h, :]
            if what == "keep":
                moving = K.kept[:, j // 2, j % 2, kc, :]
            else:
                moving = e(j, col, col + q1 - q0)
            at = SEQ if what == "one" else 0
            mm = pe.matmul(bank[32 * j:32 * j + 32, at + q0:at + q1], ones if what == "one" else value, moving,
                           start=(n == 0), stop=(n == len(steps) - 1), skip_group_check=True)
    mm.then_inc(*K.ro.fill(name, "o", b, g))


def divide_dve(K, dve, name, b, g):
    bank = K.ro.bank(name, "o", b, g)
    dve.wait_ge(*K.ro.full(name, "o", b, g))
    dve.reciprocal(K.recip[:, g % 2, :], bank[:, SEQ:]).then_inc(*K.m.done("recip", name, b, g))
    dve.wait_ge(*K.m.since("recip", name, b, g))
    dve.tensor_tensor(K.q[:, g, seq(b)], bank[:, 0:SEQ], K.recip[:, g % 2, :], ALU.mult).then_inc(
        *K.ro.free((name, "o", b, g)))


TURNS = [(b, g) for b in range(PB) for g in range(GROUPS)]
AHEAD = GROUPS + 1


def attention_pe(K, pe, name, dims, kind, rounded, exact, values):
    for u in range(AHEAD):
        if u == GROUPS:
            turn_pe(K, pe, name, 0)
        for j in range(4):
            scores_pe(K, pe, name, *TURNS[u], j, dims, kind, rounded)
    for u, (b, g) in enumerate(TURNS):
        if g == GROUPS - 1 and b + 1 < PB:
            turn_pe(K, pe, name, b + 1)
        for j in range(4):
            if u + AHEAD < len(TURNS):
                scores_pe(K, pe, name, *TURNS[u + AHEAD], j, dims, kind, rounded)
            exact_pe(K, pe, name, b, g, j, kind, exact)
        if u:
            weigh_pe(K, pe, name, *TURNS[u - 1], kind, values)
    weigh_pe(K, pe, name, *TURNS[-1], kind, values)


def attention_dve(K, dve, name, kind, ready):
    for u in range(AHEAD):
        if u == GROUPS:
            shift_dve(K, dve, name, 0, kind)
            turned_dve(K, dve, name, 0)
        for j in range(4):
            maxima_dve(K, dve, name, *TURNS[u], j, kind)
        if u < 2:
            bands(K, dve, name, *TURNS[u], (0, 1), ready)
    for u, (b, g) in enumerate(TURNS):
        if g == GROUPS - 1 and b + 1 < PB:
            shift_dve(K, dve, name, b + 1, kind)
        if u >= 2:
            divide_dve(K, dve, name, *TURNS[u - 2])
        if g == GROUPS - 1 and b + 1 < PB:
            turned_dve(K, dve, name, b + 1)
        for j in range(4):
            if u + AHEAD < len(TURNS):
                maxima_dve(K, dve, name, *TURNS[u + AHEAD], j, kind)
            if j == 1 and u + 2 < len(TURNS):
                bands(K, dve, name, *TURNS[u + 2], (0, 1), ready)
    for u in (-2, -1):
        divide_dve(K, dve, name, *TURNS[u])


def attention_act(K, act, name, kind, scale):
    for b in range(PB):
        for g in range(GROUPS):
            exps_act(K, act, name, b, g, kind, scale)


def attention_pool(K, pool, name, kind, ready):
    turns = [(b, g) for b in range(PB) for g in range(GROUPS)]
    for b, g in turns[:2]:
        bands(K, pool, name, b, g, (2, 3), ready)
    for u, (b, g) in enumerate(turns):
        if u + 2 < len(turns):
            bands(K, pool, name, *turns[u + 2], (2, 3), ready)
        if kind == "upper":
            kept_pool(K, pool, name, b, g)



def gather_pe(K, pe, name, weights, src, ready):
    for s in range(HALVES):
        bank = K.ro.claim(name, s)
        if K.ro.reused(name, s):
            pe.wait_ge(*K.ro.room(name, s))
        for i, w in enumerate(weights):
            for x in ready(i, s):
                pe.wait_ge(*x)
            mm = pe.matmul(bank, w, src(i, s), start=(i == 0), stop=(i == len(weights) - 1))
        mm.then_inc(*K.ro.fill(name, s))


def residual_dve(K, dve, name, dst, base, bias=None, ready=None):
    for s in range(HALVES):
        dve.wait_ge(*K.ro.full(name, s))
        if ready:
            for w in ready(s):
                dve.wait_ge(*w)
        if bias is None:
            op = dve.tensor_tensor(dst[:, half(s)], K.ro.bank(name, s), base[:, half(s)], ALU.add)
        else:
            op = dve.scalar_tensor_tensor(out=dst[:, half(s)], in0=K.ro.bank(name, s), scalar=bias,
                                          in1=base[:, half(s)], op0=ALU.add, op1=ALU.add)
        op.then_inc(*K.ro.free((name, s)))


def added(K, name):
    return lambda s: [K.ro.freed(name, s)]


def add_dve(K, dve, name, dst, a, after):
    for s in range(HALVES):
        for w in after(s):
            dve.wait_ge(*w)
        dve.tensor_tensor(dst[:, half(s)], dst[:, half(s)], a[:, half(s)], ALU.add).then_inc(
            *K.m.done("summed", name, s))


def summed(K, name):
    return lambda s: [K.m.since("summed", name, s)]


def blocks(w, n=4):
    return [w[:, i * P:(i + 1) * P] for i in range(n)]



def ffn_pe(K, pe, name, w1, w2, src, ready):
    project_pe(K, pe, name + "_up", blocks(w1), src, ready)
    gather_pe(K, pe, name + "_down", blocks(w2), lambda i, s: K.k[:, i, half(s)],
              lambda i, s: projected(K, name + "_up", i) if s == 0 else [])


def ffn_act(K, act, name, bias):
    project_act(K, act, name + "_up", 4, lambda g: K.k[:, g, :], ACT.Gelu, bias=lambda g: K.V(bias, g))
    both_tables(act)



def layer0_pe(K, pe):
    norm_pe(K, pe, "l0", K.xw, lambda s: [K.m.since("x_loaded", 0)])
    project_pe(K, pe, "lat", [K.W0("w_down")], K.xn, normed(K, "l0"), outs=64)
    rope_pe(K, pe, "rq", K.W0("wq"), K.W0("wqs"), K.xn, normed(K, "l0"), P)
    rope_pe(K, pe, "rk", K.W0("wk", 64), K.W0("wks", 64), K.yc, lambda s: projected(K, "lat", 0), 64)
    values_pe(K, pe, "lv", K.W0("wv", 64), K.yc, lambda s: projected(K, "lat", 0), 64, False)
    attention_pe(K, pe, "A", 8, "page",
                 lambda g: [K.m.since("rounded", "rq", g), K.m.since("rounded", "rk", g)],
                 lambda g: [], [K.rv.freed("lv", "v", 1)])
    gather_pe(K, pe, "wo", blocks(K.W0("wo")), lambda i, s: K.q[:, i, half(s)],
              lambda i, s: [K.ro.freed("A", "o", PB - 1, GROUPS - 1)] if i == 0 else [])

    norm_pe(K, pe, "l1", K.xw, added(K, "wo"))
    project_pe(K, pe, "xq", blocks(K.W0("xq")), K.xn, normed(K, "l1"))
    project_pe(K, pe, "xk", blocks(K.W0("xk")), K.xn, normed(K, "l1"))
    values_pe(K, pe, "xv", K.W0("xv"), K.xn, normed(K, "l1"), P, False)
    attention_pe(K, pe, "B", 8, "causal",
                 lambda g: [K.m.since("rounded", "xq", g), K.m.since("rounded", "xk", g)],
                 lambda g: projected(K, "xk", g), [K.rv.freed("xv", "v", 1)])
    gather_pe(K, pe, "wp_self", blocks(K.W0("wp")), lambda i, s: K.q[:, i, half(s)],
              lambda i, s: [K.ro.freed("B", "o", PB - 1, GROUPS - 1)] if i == 0 else [])

    project_pe(K, pe, "cq", blocks(K.W0("cq")), K.xn, lambda s: [])
    project_pe(K, pe, "ck", blocks(K.W0("ck", 64)), K.ctx, lambda s: [K.m.since("ctx_loaded", 0)], rows=64)
    values_pe(K, pe, "cv", K.W0("cv", 64), K.ctx, lambda s: [], 64, False)
    attention_pe(K, pe, "C", 8, "all",
                 lambda g: [K.m.since("rounded", "cq", g), K.m.since("rounded", "ck", g)],
                 lambda g: projected(K, "ck", g), [K.rv.freed("cv", "v", 1)])
    gather_pe(K, pe, "wp_cross", blocks(K.W0("wp")), lambda i, s: K.q[:, i, half(s)],
              lambda i, s: [K.ro.freed("C", "o", PB - 1, GROUPS - 1)] if i == 0 else [])
    norm_pe(K, pe, "l2", K.xw, added(K, "wp_cross"))
    bank = K.rv.claim("logits")
    pe.wait_ge(*K.rv.freed("l2", "c", 1))
    for t in range(TILES):
        mm = pe.matmul(bank[:, EXPERTS * t:EXPERTS * (t + 1)], K.xn[:, tile(t)], K.wg[:, :], start=True, stop=True)
    mm.then_inc(*K.rv.fill("logits"))


def layer0_act(K, act):
    both_tables(act)
    scale = 1.0 / 8 ** 0.5
    norm_act(K, act, "l0")
    project_act(K, act, "lat", 1, lambda g: K.yc[0:64, :], ACT.Copy, outs=64)
    attention_act(K, act, "A", "page", scale)
    norm_act(K, act, "l1")
    project_act(K, act, "xq", 4, lambda g: K.q[:, g, :], ACT.Identity, bias=lambda g: K.V("x_bq", g))
    project_act(K, act, "xk", 4, lambda g: K.k[:, g, :], ACT.Identity, bias=lambda g: K.V("x_bk", g))
    attention_act(K, act, "B", "causal", scale)
    project_act(K, act, "cq", 4, lambda g: K.q[:, g, :], ACT.Identity, bias=lambda g: K.V("x_bcq", g),
                after=lambda g: [K.ro.full("wp_self", 1)] if g == 0 else [])
    project_act(K, act, "ck", 4, lambda g: K.k[:, g, :], ACT.Identity, bias=lambda g: K.V("x_bck", g))
    attention_act(K, act, "C", "all", scale)
    norm_act(K, act, "l2")


def layer0_dve(K, dve, i):
    norm_dve(K, dve, "l0", K.xn)
    rope_dve(K, dve, "rq", K.q)
    rope_dve(K, dve, "rk", K.k, "rq")
    values_dve(K, dve, "lv", None)
    attention_dve(K, dve, "A", "page", lambda g: [K.m.since("rotated", "rq", g, 1)])
    residual_dve(K, dve, "wo", K.xw, K.xw)
    norm_dve(K, dve, "l1", K.xn)
    values_dve(K, dve, "xv", K.W0("bv"))
    attention_dve(K, dve, "B", "causal", lambda g: projected(K, "xq", g))
    residual_dve(K, dve, "wp_self", K.xw, K.xw, K.V("x_bp"))
    values_dve(K, dve, "cv", K.W0("bcv"))
    attention_dve(K, dve, "C", "all", lambda g: projected(K, "cq", g))
    residual_dve(K, dve, "wp_cross", K.xw, K.xw)
    norm_dve(K, dve, "l2", K.xn)
    dve.wait_ge(*K.rv.full("logits"))
    dve.tensor_copy(K.logits[:, bass.ds(i * TILES, TILES), :], K.rv.bank("logits")[:, 0:EXPERTS * TILES].rearrange(
        "p (t e) -> p t e", e=EXPERTS)).then_inc(*K.rv.free(("logits",)))
    dve.wait_ge(*K.rv.freed("logits"))


def layer0_pool(K, pool):
    rope_pool(K, pool, "rq", K.q, K.qb)
    rope_pool(K, pool, "rk", K.k, K.kb)
    attention_pool(K, pool, "A", "page", lambda g: [K.m.since("rotated", "rq", g, 1)])
    for x, name, kind in (("x", "B", "causal"), ("c", "C", "all")):
        as_bf16(K, pool, x + "q", 4, K.q, K.qb)
        as_bf16(K, pool, x + "k", 4, K.k, K.kb)
        attention_pool(K, pool, name, kind, lambda g: projected(K, x + "q", g))



def router_pe(K, pe):
    for c in range(2):
        bank = K.ro.claim("place", c)
        pe.wait_ge(*K.m.since("gate", f"choice{c}"))
        flat = K.onehot[:, c].rearrange("p n e -> p (n e)")
        pe.matmul(bank[:, 0:P], K.B("before"), flat, start=True, stop=False, skip_group_check=True)
        for n in range(15):
            pe.matmul(bank[:, 8 * (n + 1):P].rearrange("p (n e) -> p n e", e=EXPERTS), K.B("ones"),
                      K.onehot[:, c, n, :].unsqueeze(1).broadcast_to((P, 15 - n, EXPERTS)), start=False,
                      stop=False, skip_group_check=True)
        if c:
            for n in range(16):
                pe.matmul(bank[:, 0:P].rearrange("p (n e) -> p n e", e=EXPERTS), K.B("ones"),
                          K.onehot[:, 0, n, :].unsqueeze(1).broadcast_to((P, 16, EXPERTS)), start=False,
                          stop=False, skip_group_check=True)
        pe.matmul(bank[:, 0:8], K.B("ones"), K.zeros[:, :], start=False, stop=True,
                  skip_group_check=True).then_inc(*K.ro.fill("place", c))


def router_act(K, act):
    act.wait_ge(*K.m.since("gate", "less"))
    act.activation(K.gate[:, 1], K.gate[:, 0], ACT.Exp).then_inc(*K.m.done("gate_exp", 0))


def router_dve(K, dve):
    g, col = K.gate, K.gcol

    def wide(i):
        return col[:, i, :].unsqueeze(2).broadcast_to((P, 16, EXPERTS))

    prio = K.C("prio").unsqueeze(1).broadcast_to((P, 16, EXPERTS))

    def step(op, key):
        op.then_inc(*K.m.done("gate", key))
        dve.wait_ge(*K.m.since("gate", key))

    logits = K.logits[:, :, :]
    step(dve.tensor_reduce(col[:, 0, :], logits, AX.X, ALU.max), "max")
    dve.tensor_tensor(g[:, 0], logits, wide(0), ALU.subtract).then_inc(*K.m.done("gate", "less"))
    dve.wait_ge(*K.m.since("gate_exp", 0))
    step(dve.tensor_reduce(col[:, 1, :], g[:, 1], AX.X, ALU.add), "sum")
    step(dve.reciprocal(col[:, 2, :], col[:, 1, :]), "recip")
    step(dve.tensor_tensor(g[:, 2], g[:, 1], wide(2), ALU.mult), "gates")
    for c in range(2):
        src, eq, pri, oh = g[:, 2 + 4 * c], g[:, 3 + 4 * c], g[:, 4 + 4 * c], g[:, 5 + 4 * c]
        step(dve.tensor_reduce(col[:, 3 + c, :], src, AX.X, ALU.max), f"top{c}")
        step(dve.tensor_tensor(eq, src, wide(3 + c), ALU.is_equal), f"equal{c}")
        step(dve.tensor_tensor(pri, eq, prio, ALU.mult), f"ranked{c}")
        step(dve.tensor_reduce(col[:, 5 + c, :], pri, AX.X, ALU.max), f"first{c}")
        step(dve.tensor_tensor(oh, pri, wide(5 + c), ALU.is_equal), f"hot{c}")
        step(dve.tensor_copy(K.onehot[:, c], oh), f"choice{c}")
        if c == 0:
            step(dve.scalar_tensor_tensor(out=g[:, 6], in0=oh, scalar=-2.0, in1=src, op0=ALU.mult, op1=ALU.add),
                 "rest")
    for c in range(2):
        oh, a = g[:, 5 + 4 * c], g[:, 3 + 4 * c]
        place = K.ro.bank("place", c)[:, 0:P].rearrange("p (n e) -> p n e", e=EXPERTS)
        dve.wait_ge(*K.ro.full("place", c))
        step(dve.scalar_tensor_tensor(out=a, in0=place, scalar=float(CAPACITY), in1=oh, op0=ALU.is_lt,
                                      op1=ALU.mult), f"within{c}")
        step(dve.tensor_tensor(a, a, wide(3 + c), ALU.mult), f"weight{c}")
    step(dve.tensor_tensor(K.weight[:, :, :], g[:, 3], g[:, 7], ALU.add), "share")



def experts_pe(K, pe):
    rows = K.small[0:EXPERTS, 3 * P:11 * P].rearrange("p (e m) -> p e m", e=EXPERTS)
    b2 = K.small[0:EXPERTS, 11 * P:12 * P]
    for s in range(HALVES):
        bank = K.rv.claim("share", s)
        pe.wait_ge(*K.m.since("restored", "weight"))
        for i in range(4):
            mm = pe.transpose(bank[0:EXPERTS, tile(i)], K.weight_now[:, 4 * s + i, :], K.C("ident"))
        mm.then_inc(*K.rv.fill("share", s))
    for s in range(HALVES):
        bank = K.ro.claim("moe", s)
        pe.wait_ge(*K.rv.freed("share", s))
        pe.matmul(bank, b2, K.share[:, half(s)], start=True, stop=False, skip_group_check=True)

    def down(e):
        for s in range(HALVES):
            pe.wait_ge(*K.rv.freed("moe", e, s))
            for m in range(4):
                mm = pe.matmul(K.ro.bank("moe", s), K.expert(e, 1, m), hidden(K, e)[:, m, half(s)],
                               start=False, stop=(e == EXPERTS - 1 and m == 3), skip_group_check=True)
            if e == EXPERTS - 1:
                mm.then_inc(*K.ro.fill("moe", s))
            else:
                mm.then_inc(*K.m.done("hidden_used", e, s))

    for e in range(EXPERTS):
        project_pe(K, pe, f"up{e}", [K.expert(e, 0, m) for m in range(4)], K.xn,
                   lambda s: [K.m.since("xn_loaded", 0), K.m.since(f"expert{e}_loaded", 0)])
        for s in range(HALVES):
            bank = K.rv.claim("moe", e, s)
            if K.rv.reused("moe", e, s):
                pe.wait_ge(*K.rv.room("moe", e, s))
            pe.matmul(bank, rows[:, e, :], K.share[:, half(s)], start=True, stop=True).then_inc(
                *K.rv.fill("moe", e, s))
        if e:
            down(e - 1)
    down(EXPERTS - 1)


def hidden(K, e):
    return K.q if e % 2 else K.k


def experts_act(K, act):
    for e in range(EXPERTS):
        project_act(K, act, f"up{e}", 4, lambda g: hidden(K, e)[:, g, :], ACT.Gelu,
                    bias=lambda g: K.V("moe_b1", 4 * e + g),
                    after=lambda g: [K.m.since("hidden_used", e - 2, 1)] if e >= 2 and g == 0 else [])
    both_tables(act)


def experts_dve(K, dve):
    for s in range(HALVES):
        dve.wait_ge(*K.rv.full("share", s))
        dve.tensor_copy(K.share[:, half(s)], K.rv.bank("share", s)[0:EXPERTS, :]).then_inc(*K.rv.free(("share", s)))
    for e in range(EXPERTS):
        for s in range(HALVES):
            h = hidden(K, e)[:, :, half(s)]
            dve.wait_ge(*K.ra.freed(f"up{e}", 3, 1))
            dve.wait_ge(*K.rv.full("moe", e, s))
            dve.tensor_tensor(h, h, K.rv.bank("moe", e, s).unsqueeze(1).broadcast_to((P, 4, HALF)),
                              ALU.mult).then_inc(*K.rv.free(("moe", e, s)))
    residual_dve(K, dve, "moe", K.xw, K.xw, ready=lambda s: [K.m.since("x_loaded", 0)])


def linear_pe(K, pe):
    kv = K.W1("qkv")[:, P:3 * P]
    for c in range(4):
        bank = K.ra.claim("kv", c)
        for w in affined(K, "n1")(c // 2):
            pe.wait_ge(*w)
        if K.ra.reused("kv", c):
            pe.wait_ge(*K.ra.room("kv", c))
        for i in range(2):
            mm = pe.matmul(bank[:, i * SEQ:(i + 1) * SEQ], K.xn[:, tile(2 * c + i)], kv, start=True, stop=True)
        mm.then_inc(*K.ra.fill("kv", c))
    project_pe(K, pe, "lq", [K.W1("qkv")[:, 0:P]], K.xn, lambda s: [])
    for b in range(PB):
        bank = K.ro.claim("outer", b)
        pe.wait_ge(*K.m.since("elu", "k", b))
        if K.ro.reused("outer", b):
            pe.wait_ge(*K.ro.room("outer", b))
        for i in range(2):
            key = K.q[:, 0, tile(2 * b + i)]
            pe.matmul(bank[:, 0:P], key, K.q[:, 1, tile(2 * b + i)], start=(i == 0), stop=False,
                      skip_group_check=True)
            mm = pe.matmul(bank[:, P:2 * P], key, K.C("ones"), start=False, stop=(i == 1), skip_group_check=True)
        mm.then_inc(*K.ro.fill("outer", b))
    for b in range(PB):
        bank = K.rv.claim("linear", b)
        pe.wait_ge(*K.m.since("elu", "q", b // 2))
        pe.wait_ge(*K.ro.freed("outer", b))
        if K.rv.reused("linear", b):
            pe.wait_ge(*K.rv.room("linear", b))
        for i in range(2):
            mm = pe.matmul(bank[:, i * SEQ:(i + 1) * SEQ], K.q[:, 3, b * SEQ + i * P:b * SEQ + (i + 1) * P],
                           K.yb[:, seq(b)], start=True, stop=True)
        mm.then_inc(*K.rv.fill("linear", b))
    gather_pe(K, pe, "proj", [K.W1("proj")], lambda i, s: K.q[:, 2, half(s)],
              lambda i, s: [K.rv.freed("linear", 2 * s + 1)])


def linear_act(K, act):
    for c in range(4):
        bank = K.ra.bank("kv", c).rearrange("p (i w) -> p i w", i=2)
        at = slice(2 * c * P, 2 * (c + 1) * P)
        act.wait_ge(*K.ra.full("kv", c))
        act.activation(K.q[:, 0, at].rearrange("p (i w) -> p i w", i=2), bank[:, :, 0:P], ACT.Relu).then_inc(
            *K.m.done("elu_part", "relu", c))
        act.activation(K.q[:, 1, at].rearrange("p (i w) -> p i w", i=2), bank[:, :, P:2 * P], ACT.Copy).then_inc(
            *K.m.done("elu_part", "v", c))
        act.activation(K.q[:, 2, at].rearrange("p (i w) -> p i w", i=2), bank[:, :, 0:P], ACT.Exp).then_inc(
            *K.ra.free(("kv", c)))
    act.wait_ge(*K.ra.full("lq", 0, 1))
    pair = K.ra_pair("lq", 0, 0)
    act.activation(K.yb[:, :].rearrange("p (s t) -> p s t", s=2), pair, ACT.Relu).then_inc(
        *K.m.done("elu_part", "relu", "q"))
    act.activation(K.yc[:, :].rearrange("p (s t) -> p s t", s=2), pair, ACT.Exp).then_inc(
        *K.ra.free(("lq", 0, 0), ("lq", 0, 1)))


def linear_dve(K, dve):
    for c in range(4):
        at = slice(2 * c * P, 2 * (c + 1) * P)
        dve.wait_ge(*K.ra.freed("kv", c))
        dve.wait_ge(*K.m.since("elu_part", "v", c))
        dve.scalar_tensor_tensor(out=K.q[:, 0, at], in0=K.q[:, 2, at], scalar=1.0, in1=K.q[:, 0, at], op0=ALU.min,
                                 op1=ALU.add).then_inc(*K.m.done("elu", "k", c))
    for s in range(HALVES):
        dve.wait_ge(*K.ra.freed("lq", 0, 1))
        dve.wait_ge(*K.m.since("elu_part", "relu", "q"))
        dve.scalar_tensor_tensor(out=K.yb[:, half(s)], in0=K.yc[:, half(s)], scalar=1.0, in1=K.yb[:, half(s)],
                                 op0=ALU.min, op1=ALU.add).then_inc(*K.m.done("elu", "q", s))
    for b in range(PB):
        dve.wait_ge(*K.ro.full("outer", b))
        dve.tensor_tensor(K.q[:, 3, seq(b)].rearrange("p (i w) -> p i w", i=2),
                          K.ro.bank("outer", b)[:, 0:SEQ].rearrange("p (i w) -> p i w", i=2),
                          K.C("blocks").unsqueeze(1).broadcast_to((P, 2, P)), ALU.mult).then_inc(
            *K.ro.free(("outer", b)))
    for b in range(PB):
        bank, r = K.rv.bank("linear", b), K.recip[:, b % 2, :]
        dve.wait_ge(*K.rv.full("linear", b))
        dve.tensor_scalar(r, bank[:, SEQ:], 1e-6, None, ALU.add).then_inc(*K.m.done("zsum", b))
        dve.wait_ge(*K.m.since("zsum", b))
        dve.reciprocal(r, r).then_inc(*K.m.done("z", b))
        dve.wait_ge(*K.m.since("z", b))
        dve.tensor_tensor(K.q[:, 2, seq(b)], bank[:, 0:SEQ], r, ALU.mult).then_inc(*K.rv.free(("linear", b)))
    residual_dve(K, dve, "proj", K.ya, K.ya, K.V("proj_b"))


def mixed_pe(K, pe, a, kind, kv_src, kv_ready, kv_rows):
    project_pe(K, pe, a + "q", blocks(K.W1(a + "_q")), K.xn, affined(K, a + "x"))
    project_pe(K, pe, a + "k", blocks(K.W1(a + "_k", kv_rows)), kv_src, kv_ready, rows=kv_rows)
    values_pe(K, pe, a + "v", K.W1(a + "_v", kv_rows), kv_src, lambda s: [], kv_rows, True)
    attention_pe(K, pe, a, 32, kind,
                 lambda g: [K.m.since("rounded", a + "q", g), K.m.since("rounded", a + "k", g)],
                 lambda g: projected(K, a + "k", g), [K.ra.freed(a + "v", "v", TILES - 1)])
    gather_pe(K, pe, a + "o", blocks(K.W1(a + "_li1")), lambda i, s: K.q[:, i, half(s)],
              lambda i, s: [K.ro.freed(a, "o", PB - 1, GROUPS - 1)] if i == 0 else [])
    norm_pe(K, pe, a + "3", K.yc, added(K, a + "o"))
    ffn_pe(K, pe, a + "f", K.W1(a + "_li2"), K.W1(a + "_li3"), K.xn, affined(K, a + "3"))


def mixed_act(K, act, a, kind):
    project_act(K, act, a + "q", 4, lambda g: K.q[:, g, :], ACT.Copy)
    project_act(K, act, a + "k", 4, lambda g: K.k[:, g, :], ACT.Copy)
    values_act(K, act, a + "v")
    attention_act(K, act, a, kind, 32 ** -0.5)
    norm_act(K, act, a + "3")
    ffn_act(K, act, a + "f", a + "_li2_b")


def mixed_dve(K, dve, a, kind):
    attention_dve(K, dve, a, kind, lambda g: projected(K, a + "q", g))
    residual_dve(K, dve, a + "o", K.yc, K.ya, K.V(a + "_li1_b"))
    norm_dve(K, dve, a + "3", K.xn, affine=(a + "_ln3_g", a + "_ln3_b"))
    residual_dve(K, dve, a + "f_down", K.yc, K.yc, K.V(a + "_li3_b"))
    add_dve(K, dve, a + "out", K.ya, K.yc, added(K, a + "f_down"))


def leaves_pe(K, pe):
    bank = K.rv.claim("nodes")
    for t in range(TILES):
        for w in normed(K, "l5")(t // 4):
            pe.wait_ge(*w)
        if t == 0 and K.rv.reused("nodes"):
            pe.wait_ge(*K.rv.room("nodes"))
        mm = pe.matmul(bank[:, 45 * t:45 * t + 45], K.xn[:, tile(t)], K.W1("nodes"), start=True, stop=True)
    mm.then_inc(*K.rv.fill("nodes"))
    for s in range(HALVES):
        bank = K.rv.claim("leaf", s)
        pe.wait_ge(*K.m.since("tree", "chosen"))
        if K.rv.reused("leaf", s):
            pe.wait_ge(*K.rv.room("leaf", s))
        for i in range(4):
            mm = pe.transpose(bank[0:48, tile(i)], K.tree[:, 1, 4 * s + i, :], K.C("ident"))
        mm.then_inc(*K.rv.fill("leaf", s))
    w1, w2 = K.WF("f_w1"), K.WF("f_w2")
    pe.wait_ge(*K.m.since("feed_loaded", 0))
    for r in range(3):
        outs = [K.ro.claim("leaves", r, s) for s in range(HALVES)]

        def up(m):
            for s in range(HALVES):
                bank = K.ra.claim("hid", r, m, s)
                if K.ra.reused("hid", r, m, s):
                    pe.wait_ge(*K.ra.room("hid", r, m, s))
                if r == 0 and m == 0:
                    pe.wait_ge(*K.rv.freed("leaf", s))
                pe.matmul(bank, w1[:, r * PASS + m * P:r * PASS + (m + 1) * P], K.xn[:, half(s)], start=True,
                          stop=False, skip_group_check=True)
                pe.matmul(bank, K.leafsel[:, 8 * r + m, :], K.lm[:, half(s)], start=False, stop=True,
                          skip_group_check=True).then_inc(*K.ra.fill("hid", r, m, s))

        def down(m):
            w = w2[:, r * PASS + m * P:r * PASS + (m + 1) * P]
            if m == 0:
                for s in range(HALVES):
                    if K.ro.reused("leaves", r, s):
                        pe.wait_ge(*K.ro.room("leaves", r, s))
            pe.wait_ge(*K.ra.freed("hid", r, m, 1))
            h = (K.q if m < 4 else K.k)[:, m % 4, :]
            b2 = K.small[:, r * P:(r + 1) * P]
            for s in range(HALVES):
                if r < 2:
                    if m == 0:
                        pe.matmul(outs[s], b2, K.lt[:, half(s)], start=True, stop=False, skip_group_check=True)
                    mm = pe.matmul(outs[s], w, h[:, half(s)], start=False, stop=(m == 7), skip_group_check=True)
                else:
                    for i in range(4):
                        t = 4 * s + i
                        if m == 0:
                            pe.matmul(outs[s][:, tile(i)], K.lt[:, tile(t)], b2, start=(i == 0), stop=False,
                                      skip_group_check=True)
                    for i in range(4):
                        t = 4 * s + i
                        mm = pe.matmul(outs[s][:, tile(i)], h[:, tile(t)], w, start=False, stop=(m == 7),
                                       skip_group_check=True)
                if m == 7:
                    mm.then_inc(*K.ro.fill("leaves", r, s))
                elif s == 1:
                    mm.then_inc(*K.m.done("hid_used", r, m))

        for m in range(8):
            up(m)
            if m >= 2:
                down(m - 2)
        down(6)
        down(7)
    for b in range(PB):
        bank = K.ra.claim("fs", b)
        pe.wait_ge(*K.ro.freed("leaves", 1, 1))
        if K.ra.reused("fs", b):
            pe.wait_ge(*K.ra.room("fs", b))
        for i in range(2):
            mm = pe.matmul(bank[:, i * SEQ:(i + 1) * SEQ], K.ya[:, b * SEQ + i * P:b * SEQ + (i + 1) * P],
                           K.yb[:, seq(b)], start=True, stop=True)
        mm.then_inc(*K.ra.fill("fs", b))
    for b in range(PB):
        bank = K.ro.claim("ft", b)
        pe.wait_ge(*K.m.since("fnorm", b, 1))
        if K.ro.reused("ft", b):
            pe.wait_ge(*K.ro.room("ft", b))
        for kc in range(2):
            for i in range(2):
                mm = pe.transpose(bank[:, kc * SEQ + i * P:kc * SEQ + (i + 1) * P],
                                  K.prob[:, b, i, kc * P:(kc + 1) * P], K.C("ident"))
        mm.then_inc(*K.ro.fill("ft", b))
        bank = K.rv.claim("fo", b)
        pe.wait_ge(*K.ro.freed("ft", b))
        pe.wait_ge(*K.ro.freed("leaves", 2, 1))
        if K.rv.reused("fo", b):
            pe.wait_ge(*K.rv.room("fo", b))
        for kc in range(2):
            mm = pe.matmul(bank[:, 0:SEQ], K.yc[:, tile(2 * b + kc)], K.q[:, b, kc * SEQ:(kc + 1) * SEQ],
                           start=(kc == 0), stop=(kc == 1))
        mm.then_inc(*K.rv.fill("fo", b))


def leaves_act(K, act):
    for r in range(3):
        for m in range(8):
            if r:
                if m < 7:
                    act.wait_ge(*K.m.since("hid_used", r - 1, m))
                else:
                    act.wait_ge(*K.ro.full("leaves", r - 1, 1))
            act.wait_ge(*K.ra.full("hid", r, m, 1))
            h = (K.q if m < 4 else K.k)[:, m % 4, :]
            act.activation(h.rearrange("p (s t) -> p s t", s=2), K.ra_pair("hid", r, m, 0), ACT.Relu,
                           bias=K.V("f_b1", 8 * r + m)).then_inc(*K.ra.free(("hid", r, m, 0), ("hid", r, m, 1)))
    for b in range(PB):
        for i in range(2):
            act.wait_ge(*K.m.since("fmax", "scaled", b))
            op = act.activation(K.prob[:, b, i, 0:SEQ], K.ra.bank("fs", b)[:, i * SEQ:(i + 1) * SEQ], ACT.Exp,
                                bias=K.stat[:, 0, 2 * b + i:2 * b + i + 1], scale=P ** -0.5,
                                accum_out=K.stat[:, 1, 2 * b + i:2 * b + i + 1])
            if i:
                op.then_inc(*K.ra.free(("fs", b)))
            else:
                op.then_inc(*K.m.done("fexp", b))


def leaves_dve(K, dve):
    d, c = K.tree[:, 0], K.tree[:, 1]

    def step(op, *key):
        op.then_inc(*K.m.done("tree", *key))
        dve.wait_ge(*K.m.since("tree", *key))

    score = K.rv.bank("nodes")[:, 0:45 * TILES].rearrange("p (t n) -> p t n", t=TILES)
    dve.wait_ge(*K.rv.full("nodes"))
    dve.tensor_tensor(d[:, :, 0:45], score, K.W1("node_b").unsqueeze(1).broadcast_to((P, TILES, 45)),
                      ALU.add).then_inc(*K.rv.free(("nodes",)))
    dve.wait_ge(*K.rv.freed("nodes"))
    step(dve.tensor_scalar(d[:, :, 0:45], d[:, :, 0:45], 0.0, None, ALU.is_ge), "right")
    turn = d[:, :, 0:45].rearrange("p t (r n) -> p t r n", r=3)
    a, b = c.rearrange("p t (r n) -> p t r n", r=3), K.treeb[:, :, :].rearrange("p t (r n) -> p t r n", r=3)
    level = [b, a, b, a]
    step(dve.tensor_copy(b[:, :, :, 1], turn[:, :, :, 0]), "one", 0)
    step(dve.tensor_scalar(b[:, :, :, 0], turn[:, :, :, 0], -1.0, 1.0, ALU.mult, ALU.add), "zero", 0)
    for n in (1, 2, 3):
        w = 2 ** n
        old, new = level[n - 1], level[n]
        for r in range(3):
            step(dve.tensor_tensor(new[:, :, r, 1:2 * w:2], old[:, :, r, 0:w], turn[:, :, r, w - 1:2 * w - 1],
                                   ALU.mult), "one", n, r)
            step(dve.tensor_tensor(new[:, :, r, 0:2 * w:2], old[:, :, r, 0:w], new[:, :, r, 1:2 * w:2],
                                   ALU.subtract), "chosen" if (n, r) == (3, 2) else "zero", *(
                                       () if (n, r) == (3, 2) else (n, r)))
    for s in range(HALVES):
        bank = K.rv.bank("leaf", s)[0:48, :]
        dve.wait_ge(*K.rv.full("leaf", s))
        dve.tensor_scalar(K.lm[:, half(s)], bank, -1.0, None, ALU.add)
        dve.tensor_copy(K.lt[:, half(s)], bank).then_inc(*K.rv.free(("leaf", s)))
    for r, dst in enumerate((K.ya, K.yb, K.yc)):
        for s in range(HALVES):
            dve.wait_ge(*K.ro.full("leaves", r, s))
            dve.tensor_copy(dst[:, half(s)], K.ro.bank("leaves", r, s)).then_inc(*K.ro.free(("leaves", r, s)))
    for b in range(PB):
        at = slice(2 * b, 2 * b + 2)
        dve.wait_ge(*K.ra.full("fs", b))
        dve.tensor_reduce(K.stat[:, 0, at], K.ra.bank("fs", b).rearrange("p (i k) -> p i k", i=2), AX.X,
                          ALU.max).then_inc(*K.m.done("fmax", "raw", b))
        dve.wait_ge(*K.m.since("fmax", "raw", b))
        dve.tensor_scalar(K.stat[:, 0, at], K.stat[:, 0, at], -(P ** -0.5), None, ALU.mult).then_inc(
            *K.m.done("fmax", "scaled", b))
    for b in range(PB):
        at = slice(2 * b, 2 * b + 2)
        dve.wait_ge(*K.ra.freed("fs", b))
        dve.wait_ge(*K.m.since("fexp", b))
        dve.reciprocal(K.stat[:, 1, at], K.stat[:, 1, at]).then_inc(*K.m.done("frecip", b))
        dve.wait_ge(*K.m.since("frecip", b))
        for i in range(2):
            e = K.prob[:, b, i, 0:SEQ]
            dve.tensor_scalar(e, e, K.stat[:, 1, 2 * b + i:2 * b + i + 1], None, ALU.mult).then_inc(
                *K.m.done("fnorm", b, i))
        dve.wait_ge(*K.ro.full("ft", b))
        dve.tensor_copy(K.q[:, b, 0:HALF], K.ro.bank("ft", b)).then_inc(*K.ro.free(("ft", b)))
        dve.wait_ge(*K.rv.full("fo", b))
        dve.tensor_tensor(K.xw[:, seq(b)], K.rv.bank("fo", b)[:, 0:SEQ], K.xw[:, seq(b)], ALU.add).then_inc(
            *K.rv.free(("fo", b)))


def layer1_pe(K, pe):
    experts_pe(K, pe)
    norm_pe(K, pe, "l3", K.xw, added(K, "moe"))
    norm_pe(K, pe, "n1", K.ya, normed(K, "l3"))
    linear_pe(K, pe)
    norm_pe(K, pe, "n2", K.ya, added(K, "proj"))
    ffn_pe(K, pe, "fc", K.W1("fc1"), K.W1("fc2"), K.xn, affined(K, "n2"))

    norm_pe(K, pe, "l4", K.xw, summed(K, "linear"))
    norm_pe(K, pe, "ln1", K.ya, normed(K, "l4"))
    norm_pe(K, pe, "a1x", K.ya, affined(K, "ln1"))
    mixed_pe(K, pe, "a1", "upper", K.yb, lambda s: [K.m.since("affine", "a1x", "second", s)], P)
    norm_pe(K, pe, "ln2", K.ya, summed(K, "a1out"))
    norm_pe(K, pe, "a2x", K.ya, affined(K, "ln2"))
    norm_pe(K, pe, "a2y", K.ctx, lambda s: [K.m.since("ctx_loaded", 0)], rows=CTX)
    mixed_pe(K, pe, "a2", "all", K.yb, affined(K, "a2y"), CTX)

    norm_pe(K, pe, "l5", K.xw, summed(K, "cross"))
    leaves_pe(K, pe)


def layer1_act(K, act):
    experts_act(K, act)
    norm_act(K, act, "l3")
    norm_act(K, act, "n1")
    linear_act(K, act)
    norm_act(K, act, "n2")
    ffn_act(K, act, "fc", "fc1_b")
    norm_act(K, act, "l4")
    norm_act(K, act, "ln1")
    norm_act(K, act, "a1x")
    mixed_act(K, act, "a1", "upper")
    norm_act(K, act, "ln2")
    norm_act(K, act, "a2x")
    norm_act(K, act, "a2y", rows=CTX)
    mixed_act(K, act, "a2", "all")
    norm_act(K, act, "l5")
    leaves_act(K, act)


def layer1_dve(K, dve):
    experts_dve(K, dve)
    norm_dve(K, dve, "l3", K.ya)
    norm_dve(K, dve, "n1", K.xn, affine=("n1_g", "n1_b"))
    linear_dve(K, dve)
    norm_dve(K, dve, "n2", K.xn, affine=("n2_g", "n2_b"))
    residual_dve(K, dve, "fc_down", K.ya, K.ya, K.V("fc2_b"))
    add_dve(K, dve, "linear", K.xw, K.ya, added(K, "fc_down"))

    norm_dve(K, dve, "l4", K.ya)
    norm_dve(K, dve, "ln1", K.ya, affine=("ln1_g", "ln1_b"))
    norm_dve(K, dve, "a1x", K.xn, affine=("a1_lnx_g", "a1_lnx_b"), second=(K.yb, "a1_lny_g", "a1_lny_b"))
    mixed_dve(K, dve, "a1", "upper")
    norm_dve(K, dve, "ln2", K.ya, affine=("ln2_g", "ln2_b"))
    norm_dve(K, dve, "a2x", K.xn, affine=("a2_lnx_g", "a2_lnx_b"))
    norm_dve(K, dve, "a2y", K.yb, affine=("a2_lny_g", "a2_lny_b"), rows=CTX)
    mixed_dve(K, dve, "a2", "all")
    add_dve(K, dve, "cross", K.xw, K.ya, summed(K, "a2out"))
    norm_dve(K, dve, "l5", K.xn)
    leaves_dve(K, dve)


def layer1_pool(K, pool, i):
    pool.tensor_copy(K.weight_now[:, :, :], K.weight[:, bass.ds(i * TILES, TILES), :]).then_inc(
        *K.m.done("restored", "weight"))
    pool.wait_ge(*K.ro.full("moe", 1))
    for a, kind in (("a1", "upper"), ("a2", "all")):
        as_bf16(K, pool, a + "q", 4, K.q, K.qb)
        as_bf16(K, pool, a + "k", 4, K.k, K.kb)
        attention_pool(K, pool, a, kind, lambda g: projected(K, a + "q", g))


def build(nc, known, args):
    (xT, ctxT, vec, const, early, moe, feed, late, wgT, headsel, leafsel, small, out) = args
    with ExitStack() as ctx:
        marks = Marks(nc, ctx, known)
        for kind in KINDS:
            marks.sem(kind)
        lo = min(sem_number(s) for s in marks.sems.values())
        hi = max(sem_number(s) for s in marks.sems.values())
        assert hi - lo + 1 == len(marks.sems)
        K = Chip(nc, ctx, marks)
        x_kept = nc.dram_tensor("x_kept", (P, TOKENS), F32, kind="Internal").ap()
        xn_kept = nc.dram_tensor("xn_kept", (P, TOKENS), F32, kind="Internal").ap()
        K.wg = ctx.enter_context(nc.sbuf_tensor("wg", [P, EXPERTS], F32))
        K.zeros = ctx.enter_context(nc.sbuf_tensor("zeros", [P, 8], BF16))

        def clear():
            with nc.Block() as block:
                @block.gpsimd
                def _(pool):
                    pool.sem_clear(range(lo, hi + 1))

        K.begin("setup")
        K.bands = band_ring(K.late)
        with nc.Block() as block:
            @block.sync
            def _(sp):
                for n, (dst, src) in enumerate((
                        (K.const[:, :], const), (K.vec[:, :], vec), (K.early[:, 0:K.n0], early),
                        (K.wg[:, :], wgT), (K.small[:, :], small))):
                    sp.dma_start(dst, src).then_inc(*K.m.done("weights", n, n=16))
                sp.wait_ge(*K.m.since("weights", 4))

            @block.scalar
            def _(act):
                act.dma_start(K.q[:, 0:2, :].rearrange("p a t -> p (a t)"), headsel).then_inc(
                    *K.m.done("selectors", 0, n=16))
                act.dma_start(K.k[0:48, 0:3, :].rearrange("p a t -> p (a t)"), leafsel).then_inc(
                    *K.m.done("selectors", 1, n=16))

            @block.vector
            def _(dve):
                dve.memset(K.zeros[:, :], 0.0).then_inc(*K.m.done("setup", "zeros"))
                dve.memset(K.shift[:, :, :], 0.0).then_inc(*K.m.done("setup", "shift"))
                dve.wait_ge(*K.m.since("selectors", 1))
                dve.tensor_copy(K.headsel[:, :, :], K.q[:, 0:2, :].rearrange("p a (h m) -> p (a h) m", m=P)).then_inc(
                    *K.m.done("setup", "headsel"))
                dve.tensor_copy(K.leafsel[:, :, :], K.k[0:48, 0:3, :].rearrange("p a (h m) -> p (a h) m", m=P)
                                ).then_inc(*K.m.done("setup", "leafsel"))
                dve.wait_ge(*K.m.since("weights", 4))
                for name in TO_BF16:
                    dve.tensor_copy(K.B(name), K.C(name)).then_inc(*K.m.done("setup", name))
                dve.wait_ge(*K.m.since("setup", TO_BF16[-1]))

            @block.gpsimd
            def _(pool):
                pool.memset(K.v[:, :, :, :], 0.0).then_inc(*K.m.done("padding", 0))
                pool.wait_ge(*K.m.since("padding", 0))
        clear()

        with nc.Fori(0, PASSES) as i:
            K.begin("first")
            with nc.Block() as block:
                @block.tensor
                def _(pe):
                    layer0_pe(K, pe)

                @block.sync
                def _(sp):
                    sp.dma_start(K.xw[:, :], xT[:, bass.ds(i * PASS, PASS)]).then_inc(
                        *K.m.done("x_loaded", 0, n=16))
                    sp.dma_start(K.ctx[:, :], ctxT[:, bass.ds(i * PASS, PASS)]).then_inc(
                        *K.m.done("ctx_loaded", 0, n=16))
                    sp.wait_ge(*K.ro.freed("wp_cross", 1))
                    sp.dma_start(x_kept[:, bass.ds(i * PASS, PASS)], K.xw[:, :]).then_inc(
                        *K.m.done("x_stored", 0, n=16))
                    sp.wait_ge(*K.rv.freed("l2", "c", 1))
                    sp.dma_start(xn_kept[:, bass.ds(i * PASS, PASS)], K.xn[:, :]).then_inc(
                        *K.m.done("xn_stored", 0, n=16))
                    sp.wait_ge(*K.m.since("x_stored", 0))
                    sp.wait_ge(*K.m.since("xn_stored", 0))

                @block.scalar
                def _(act):
                    layer0_act(K, act)

                @block.vector
                def _(dve):
                    layer0_dve(K, dve, i)

                @block.gpsimd
                def _(pool):
                    layer0_pool(K, pool)
            clear()

        K.begin("router")
        with nc.Block() as block:
            @block.tensor
            def _(pe):
                router_pe(K, pe)

            @block.scalar
            def _(act):
                router_act(K, act)

            @block.vector
            def _(dve):
                router_dve(K, dve)

            @block.sync
            def _(sp):
                sp.dma_start(K.late[:, :], late).then_inc(*K.m.done("later_loaded", 0, n=16))
                sp.wait_ge(*K.m.since("later_loaded", 0))
        clear()
        K.bands = band_ring(K.early)

        with nc.Fori(0, PASSES) as i:
            K.begin("second")
            with nc.Block() as block:
                @block.tensor
                def _(pe):
                    layer1_pe(K, pe)

                @block.sync
                def _(sp):
                    sp.dma_start(K.xn[:, :], xn_kept[:, bass.ds(i * PASS, PASS)]).then_inc(
                        *K.m.done("xn_loaded", 0, n=16))
                    for e in range(EXPERTS):
                        at = slice(2 * HID * e, 2 * HID * (e + 1))
                        sp.dma_start(K.early[:, at], moe[:, at]).then_inc(*K.m.done(f"expert{e}_loaded", 0, n=16))
                    sp.dma_start(K.xw[:, :], x_kept[:, bass.ds(i * PASS, PASS)]).then_inc(
                        *K.m.done("x_loaded", 0, n=16))
                    sp.wait_ge(*K.ro.full("moe", 1))
                    sp.dma_start(K.ctx[:, :], ctxT[:, bass.ds(i * PASS, PASS)]).then_inc(
                        *K.m.done("ctx_loaded", 0, n=16))
                    sp.wait_ge(*K.ra.full("a2", "t", PB - 1, HEADS - 1))
                    sp.dma_start(K.early[:, 0:K.nf], feed).then_inc(*K.m.done("feed_loaded", 0, n=16))
                    sp.wait_ge(*K.rv.freed("fo", PB - 1))
                    sp.dma_start(out[:, bass.ds(i * PASS, PASS)], K.xw[:, :]).then_inc(
                        *K.m.done("stored", 0, n=16))
                    sp.wait_ge(*K.m.since("stored", 0))
                    sp.wait_ge(*K.m.since("ctx_loaded", 0))

                @block.scalar
                def _(act):
                    layer1_act(K, act)

                @block.vector
                def _(dve):
                    layer1_dve(K, dve)

                @block.gpsimd
                def _(pool):
                    layer1_pool(K, pool, i)
            clear()
        return marks.found


KINDS = ["rv_filled", "rv_freed", "ro_filled", "ro_freed", "ra_filled", "ra_freed", "squared", "rstd", "affine",
         "rounded", "rotated", "banded_v", "banded_p", "later_loaded", "value", "joined", "negated", "kept", "recip", "summed", "weights", "selectors",
         "setup", "padding", "x_loaded", "ctx_loaded", "gate", "gate_exp", "x_stored",
         "xn_stored", "xn_loaded", "feed_loaded", "restored", "hidden_used", "elu", "elu_part", "zsum", "z", "tree", "hid_used", "fmax", "fexp",
         "frecip", "fnorm", "stored"] + [f"expert{e}_loaded" for e in range(EXPERTS)]


def sem_number(s):
    return s.num



def _layout(a):
    import numpy as np
    f = {n: np.asarray(v) for n, v in a.items()}

    def rows(m, r=P):
        m = np.asarray(m, np.float32) if m.dtype != np.float32 else m
        out = np.zeros((r, m.shape[1]), np.float32)
        out[:m.shape[0]] = m
        return out

    def pad_out(w):
        out = np.zeros((w.shape[0], HEADS, 32), np.float32)
        out[:, :, 0:8] = w.reshape(w.shape[0], HEADS, 8)
        return out.reshape(w.shape[0], 512)

    def pad_in(w):
        out = np.zeros((HEADS, 32, w.shape[1]), np.float32)
        out[:, 0:8] = w.reshape(HEADS, 8, w.shape[1])
        return out.reshape(4, P, w.shape[1]).transpose(1, 0, 2).reshape(P, -1)

    def swap(w):
        return w.reshape(w.shape[0], -1, 2)[:, :, ::-1].reshape(w.shape)

    def fold(w):
        return w.reshape(-1, P, w.shape[1]).transpose(1, 0, 2).reshape(P, -1)

    def vpad(v):
        return pad_out(v.reshape(1, P)).reshape(4, P).T

    def cols(v):
        return v.reshape(-1, P).T

    def heads(w):
        return w.transpose(1, 0, 2).reshape(w.shape[1], -1)

    vec = np.zeros((P, NVEC), np.float32)

    def put(name, m):
        at, n = VCOL[name]
        assert m.shape[1] == n
        vec[:m.shape[0], at:at + n] = m
    for name, key in (("x_bq", "bq"), ("x_bk", "bk"), ("x_bcq", "bcq"), ("x_bck", "bck")):
        put(name, vpad(f["L0_xattn_" + key]))
    put("x_bp", cols(f["L0_xattn_bp"]))
    put("moe_b1", cols(f["L0_ffn_b1"]))
    for name, key in (("n1_g", "norm1_g"), ("n1_b", "norm1_b"), ("proj_b", "proj_b"), ("n2_g", "norm2_g"),
                      ("n2_b", "norm2_b"), ("fc1_b", "fc1_b"), ("fc2_b", "fc2_b")):
        put(name, cols(f["L1_attn_" + key]))
    for name in ("ln1_g", "ln1_b", "ln2_g", "ln2_b"):
        put(name, cols(f["L1_xattn_" + name]))
    for b in ("a1", "a2"):
        for name in ("lnx_g", "lnx_b", "lny_g", "lny_b", "li1_b", "ln3_g", "ln3_b", "li2_b", "li3_b"):
            v = f[f"L1_xattn_{b}_{name}"]
            put(f"{b}_{name}", cols(v) if v.size >= P else v.reshape(-1, 1))
    put("f_b1", np.concatenate([cols(f[f"L1_ffn_{r}_b1"]) for r in "qkv"], 1))
    vec[:, VCOL["eps"][0]] = EPS

    eye = np.eye(P, dtype=np.float32)
    i = np.arange(P)
    page = np.where(i[None] // 32 <= i[:, None] // 32, 0.0, MASKED).astype(np.float32)
    causal = np.where(i[None] <= i[:, None], 0.0, MASKED).astype(np.float32)
    consts = {"ident": eye, "center": eye - 1.0 / P, "mean": np.full((P, P), 1.0 / P),
              "center64": rows((np.eye(64) - 1.0 / 64).astype(np.float32)),
              "mean64": rows(np.full((64, 64), 1 / 64, np.float32)), "ones": np.ones((P, P)),
              "page": page, "pageT": page.T, "causal": causal, "causalT": causal.T,
              "upper": (i[:, None] > i[None]).astype(np.float32),
              "before": (i[:, None] < i[None]).astype(np.float32),
              "blocks": (i[:, None] // 8 == i[None] // 8).astype(np.float32),
              "headrows": (i[:, None] // 32 == np.arange(4)[None]).astype(np.float32),
              "prio": np.broadcast_to(8.0 - np.arange(8), (P, 8))}
    const = np.concatenate([np.asarray(consts[n], np.float32) for n, _ in CONSTS], 1)

    inv = 1.0 / 10000.0 ** (np.arange(0, 8, 2, dtype=np.float32) / 8)
    ang = np.outer(np.arange(SEQ, dtype=np.float32), inv.astype(np.float32))
    cos, sin = np.zeros((4, 32, SEQ), np.float32), np.zeros((4, 32, SEQ), np.float32)
    for d in range(8):
        cos[:, d] = np.cos(ang[:, d // 2]).astype(np.float32)
        sin[:, d] = (np.sin(ang[:, d // 2]) * (-1.0 if d % 2 == 0 else 1.0)).astype(np.float32)
    l0 = {"wq": pad_out(f["L0_attn_wq"]), "wqs": pad_out(swap(f["L0_attn_wq"])), "w_down": f["L0_attn_w_down"],
          "wk": pad_out(f["L0_attn_wk_up"]), "wks": pad_out(swap(f["L0_attn_wk_up"])), "wv": f["L0_attn_wv_up"],
          "wo": pad_in(f["L0_attn_wo"]), "xq": pad_out(f["L0_xattn_Wq"]), "xk": pad_out(f["L0_xattn_Wk"]),
          "xv": f["L0_xattn_Wv"], "cq": pad_out(f["L0_xattn_Wcq"]), "ck": pad_out(f["L0_xattn_Wck"]),
          "cv": f["L0_xattn_Wcv"], "wp": pad_in(f["L0_xattn_Wp"]), "cos": cos.reshape(P, SEQ),
          "sin": sin.reshape(P, SEQ), "bv": np.broadcast_to(f["L0_xattn_bv"], (P, P)),
          "bcv": np.broadcast_to(f["L0_xattn_bcv"], (P, P))}
    early = np.concatenate([rows(l0[n]) for n, _ in LAYER0], 1)
    moe = np.concatenate([np.concatenate([f["L0_ffn_W1"][e], fold(f["L0_ffn_W2"][e])], 1)
                          for e in range(EXPERTS)], 1)
    l1 = {"qkv": f["L1_attn_qkv_w"].T, "proj": f["L1_attn_proj_w"].T, "fc1": f["L1_attn_fc1_w"].T,
          "fc2": fold(f["L1_attn_fc2_w"].T)}
    for b in ("a1", "a2"):
        for w in "qkv":
            l1[f"{b}_{w}"] = heads(f[f"L1_xattn_{b}_w{w}"])
        l1[f"{b}_li1"] = fold(f[f"L1_xattn_{b}_li1_w"])
        l1[f"{b}_li2"] = f[f"L1_xattn_{b}_li2_w"]
        l1[f"{b}_li3"] = fold(f[f"L1_xattn_{b}_li3_w"])
    feed = np.concatenate([f[f"L1_ffn_{r}_w1"].transpose(1, 0, 2).reshape(P, -1) for r in "qkv"]
                          + [fold(f[f"L1_ffn_{r}_w2"].reshape(-1, P)) for r in "qkv"], 1)
    l1["nodes"] = np.concatenate([f[f"L1_ffn_{r}_node_w"].T for r in "qkv"], 1)
    l1["node_b"] = np.broadcast_to(np.concatenate([f[f"L1_ffn_{r}_node_b"] for r in "qkv"]), (P, 45))
    late = np.concatenate([rows(l1[n]) for n, _ in LAYER1], 1)

    headsel = np.zeros((P, HEADS, P), np.float32)
    for h in range(HEADS):
        headsel[h, h] = 1.0
    leafsel = np.zeros((48, 24, P), np.float32)
    for r in range(3):
        for leaf in range(LEAVES):
            leafsel[16 * r + leaf, 8 * r + leaf // 2, 64 * (leaf % 2):64 * (leaf % 2) + 64] = OFF
    small = np.zeros((48, 12 * P), np.float32)
    for n, r in enumerate("qkv"):
        small[16 * n:16 * n + 16, n * P:(n + 1) * P] = f[f"L1_ffn_{r}_b2"]
    for e in range(EXPERTS):
        small[e, (3 + e) * P:(4 + e) * P] = 1.0
    small[0:EXPERTS, 11 * P:] = f["L0_ffn_b2"]
    return {"xT": f["x"].reshape(TOKENS, P).T, "ctxT": f["ctx_512"].reshape(TOKENS, CTX).T, "vec": vec,
            "const": const, "early": early, "moe": moe, "feed": feed, "late": late, "wgT": f["L0_ffn_Wg"].T,
            "headsel": headsel.reshape(P, -1), "leafsel": leafsel.reshape(48, -1), "small": small}


def kernel(**inputs):
    import numpy as _np
    import concourse.bacc as _bacc
    from concourse import mybir as _mybir
    from concourse.bass_utils import run_bass_kernel_spmd as _run

    laid = {n: _np.ascontiguousarray(v) for n, v in _layout(inputs).items()}
    known = None
    for _ in range(2):
        nc = _bacc.Bacc("TRN2", target_bir_lowering=False, num_devices=1)
        args = [nc.dram_tensor(f"in_{n}", v.shape, _mybir.dt.from_np(v.dtype), kind="ExternalInput").ap()
                for n, v in laid.items()]
        args.append(nc.dram_tensor("out_0", (P, TOKENS), F32, kind="ExternalOutput").ap())
        known = build(nc, known, args)
    r = _run(nc, [{f"in_{n}": v for n, v in laid.items()}], core_ids=[0])
    return r.results[0]["out_0"].T.reshape(BATCH, SEQ, P)
```

```python
from contextlib import ExitStack

import concourse.bass as bass
from concourse import mybir

F32 = mybir.dt.float32
BF16 = mybir.dt.bfloat16
ACT = mybir.ActivationFunctionType
ALU = mybir.AluOpType
AX = mybir.AxisListType

P = 128
BATCH, SEQ, CTX = 8, 256, 64
TOKENS = BATCH * SEQ
HALF = 512
PASS = 1024
PASSES = TOKENS // PASS
HALVES = PASS // HALF
PB = PASS // SEQ
TILES = PASS // P
HEADS, GROUPS = 16, 4
EXPERTS, HID = 8, 512
CAPACITY = int(round(2 * TOKENS * 1.05 / EXPERTS))
LEAVES, NODES, LEAF = 16, 15, 64
EPS = 1e-5
MASKED = -1e30
OFF = 1e30


class Marks:

    def __init__(self, nc, ctx, known):
        self.nc, self.ctx, self.known = nc, ctx, known
        self.sems, self.count, self.where = {}, {}, "start"
        self.found = {}

    def sem(self, kind):
        if kind not in self.sems:
            self.sems[kind] = self.ctx.enter_context(self.nc.semaphore(kind))
        return self.sems[kind]

    def begin(self, where):
        self.where, self.count = where, {}

    def done(self, kind, *key, n=1):
        self.count[kind] = self.count.get(kind, 0) + n
        name = (self.where, kind) + key
        assert name not in self.found, name
        self.found[name] = self.count[kind]
        return self.sem(kind), n

    def since(self, kind, *key):
        name = (self.where, kind) + key
        if self.known is None:
            return self.sem(kind), 1
        return self.sem(kind), self.known[name]


class Ring:

    def __init__(self, marks, name, banks, shared=False):
        self.marks, self.name, self.banks, self.shared = marks, name, banks, shared
        self.claimed, self.order = {}, []
        self.freed_count = 0

    def begin(self):
        self.claimed, self.freed_count = {}, 0

    def claim(self, *key):
        assert key not in self.claimed, key
        self.claimed[key] = len(self.claimed)
        return self.bank(*key)

    def bank(self, *key):
        n = len(self.banks)
        return self.banks[self.claimed[key] % n]

    def pair(self, key):
        assert self.claimed[key] % 2 == 0
        return self.claimed[key] % len(self.banks)

    def reused(self, *key):
        return self.claimed[key] >= len(self.banks)

    def room(self, *key):
        return self.marks.sem(self.name + "_freed"), self.claimed[key] - len(self.banks) + 1

    def fill(self, *key):
        return self.marks.sem(self.name + "_filled"), 1

    def full(self, *key):
        return self.marks.sem(self.name + "_filled"), self.claimed[key] + 1

    def free(self, *keys):
        for key in keys:
            assert self.shared or self.claimed[key] == self.freed_count, (self.name, key)
            self.freed_count += 1
        return self.marks.sem(self.name + "_freed"), len(keys)

    def freed(self, *key):
        return self.marks.sem(self.name + "_freed"), self.claimed[key] + 1


VECTORS = [
    ("x_bq", 1), ("x_bk", 1), ("x_bcq", 1), ("x_bck", 1), ("x_bp", 1),
    ("moe_b1", 32),
    ("n1_g", 1), ("n1_b", 1), ("proj_b", 1), ("n2_g", 1), ("n2_b", 1), ("fc1_b", 4), ("fc2_b", 1),
    ("ln1_g", 1), ("ln1_b", 1), ("ln2_g", 1), ("ln2_b", 1),
] + [(f"{a}_{v}", n) for a in ("a1", "a2") for v, n in (
    ("lnx_g", 1), ("lnx_b", 1), ("lny_g", 1), ("lny_b", 1), ("li1_b", 1), ("ln3_g", 1), ("ln3_b", 1),
    ("li2_b", 4), ("li3_b", 1))] + [("f_b1", 24), ("eps", 1)]
VCOL, _at = {}, 0
for _name, _n in VECTORS:
    VCOL[_name] = (_at, _n)
    _at += _n
NVEC = _at

CONSTS = [("ident", 128), ("center", 128), ("mean", 128), ("center64", 64), ("mean64", 64), ("ones", 128),
          ("page", 128), ("pageT", 128), ("causal", 128), ("causalT", 128), ("upper", 128),
          ("before", 128), ("blocks", 128), ("prio", 8), ("headrows", 4)]
TO_BF16 = ["ident", "page", "pageT", "causal", "causalT", "before", "ones"]
LAYER0 = [("wq", 128), ("wqs", 128), ("w_down", 64), ("wk", 128), ("wks", 128), ("wv", 128), ("wo", 512),
          ("xq", 128), ("xk", 128), ("xv", 128), ("cq", 128), ("ck", 128), ("cv", 128), ("wp", 512),
          ("cos", 256), ("sin", 256), ("bv", 128), ("bcv", 128)]
MOE = [("experts", EXPERTS * 2 * HID)]
FEED = [("f_w1", 3072), ("f_w2", 3072)]
LAYER1 = [("qkv", 384), ("proj", 128), ("fc1", 512), ("fc2", 512)] + [
    (f"{a}_{w}", 512) for a in ("a1", "a2") for w in ("q", "k", "v", "li1", "li2", "li3")] + [
    ("nodes", 45), ("node_b", 45)]


def columns(parts):
    at, out = 0, {}
    for name, n in parts:
        out[name] = (at, n)
        at += n
    return out, at


class Chip:

    def __init__(self, nc, ctx, marks):
        def sb(name, shape, dt=F32):
            return ctx.enter_context(nc.sbuf_tensor(name, shape, dt))
        self.m = marks
        self.vec = sb("vec", [P, NVEC])
        self.ccol, n = columns(CONSTS)
        self.const = sb("const", [P, n])
        self.bcol, n = columns([(x, P) for x in TO_BF16])
        self.bf = sb("bf", [P, n], BF16)
        self.l0col, n0 = columns(LAYER0)
        self.mcol, nm = columns(MOE)
        self.fcol, nf = columns(FEED)
        self.early = sb("early", [P, max(n0, nm)])
        self.l1col, n1 = columns(LAYER1)
        self.late = sb("late", [P, n1])
        self.n0, self.nm, self.n1, self.nf = n0, nm, n1, nf
        self.headsel = sb("headsel", [P, HEADS, P], BF16)
        self.leafsel = sb("leafsel", [48, 24, P], BF16)
        self.small = sb("small", [48, 3 * P + 8 * P + P])
        self.logits = sb("logits", [P, TOKENS // P, EXPERTS])
        self.weight = sb("weight", [P, TOKENS // P, EXPERTS])
        self.weight_now = sb("weight_now", [P, TILES, EXPERTS])
        self.xw = sb("xw", [P, PASS])
        self.ctx = sb("ctx", [CTX, PASS])
        self.xn = sb("xn", [P, PASS])
        self.sq = sb("sq", [P, PASS])
        self.rstd = self.sq
        self.ya = sb("ya", [P, PASS])
        self.yb = sb("yb", [P, PASS])
        self.yc = sb("yc", [P, PASS])
        self.q = sb("q", [P, GROUPS, PASS])
        self.k = sb("k", [P, GROUPS, PASS])
        both = sb("rounded_qk", [P, 2 * GROUPS, PASS], BF16)
        self.qb, self.kb = both[:, 0:GROUPS, :], both[:, GROUPS:, :]
        self.stack = {"k": both, "q": self.k.rearrange("p g t -> p (g t)").bitcast(BF16).rearrange(
            "p (n t) -> p n t", t=PASS)}
        room = self.late.rearrange("p n -> p n")
        self.sel = room[:, 0:6 * 8 * P // 2].bitcast(BF16).rearrange("p (x n m) -> p x n m", x=6, m=P)
        self.part = room[:, 3 * PASS:6 * PASS].bitcast(BF16).rearrange("p (x t) -> p x t", t=PASS)
        self.turned = room[:, 6 * PASS:7 * PASS]
        self.v = sb("v", [P, TILES, HEADS, 32])
        self.prob = sb("prob", [P, 4, 2, HALF])
        self.kept = sb("kept", [P, 2, 2, 2, P])
        self.maxes = sb("maxes", [P, 2, HEADS, 3])
        self.negmax = sb("negmax", [P, 2, 2, HEADS])
        self.shift = sb("shift", [P, 2, SEQ], BF16)
        self.weighed = sb("weighed", [P, 2, 2 * SEQ])
        self.recip = self.weighed[:, :, SEQ:]
        self.gate = self.q[:, 0:2, :].rearrange("p a t -> p (a t)")[:, 0:12 * P].rearrange(
            "p (a n e) -> p a n e", a=12, e=EXPERTS)
        self.gcol = sb("gcol", [P, 8, 16])
        self.onehot = sb("onehot", [P, 2, 16, EXPERTS], BF16)
        flat = self.prob.rearrange("p a i t -> p (a i t)")
        self.tree = flat[:, 0:2 * TILES * 48].rearrange("p (a t n) -> p a t n", a=2, n=48)
        self.treeb = flat[:, 2 * TILES * 48:3 * TILES * 48].rearrange("p (t n) -> p t n", n=48)
        self.lt = self.ctx[0:48, :]
        self.lm = self.weighed[0:48, 0, :].bitcast(BF16)
        self.share = self.lt[0:EXPERTS, :]
        self.stat = sb("stat", [P, 2, 8])
        self.ps = ctx.enter_context(nc.psum_tensor("ps", [P, 8, HALF], F32))
        banks = [self.ps[:, i, :] for i in range(8)]
        self.rv = Ring(marks, "rv", banks[0:2])
        self.ro = Ring(marks, "ro", banks[2:4], shared=True)
        self.ra = Ring(marks, "ra", banks[4:8])
        self.bands = None

    def begin(self, where):
        self.m.begin(where)
        for r in (self.rv, self.ro, self.ra):
            r.begin()

    def C(self, name, rows=P):
        a, n = self.ccol[name]
        return self.const[0:rows, a:a + n]

    def B(self, name):
        a, n = self.bcol[name]
        return self.bf[:, a:a + n]

    def W0(self, name, rows=P):
        a, n = self.l0col[name]
        return self.early[0:rows, a:a + n]

    def expert(self, e, which, m):
        at = (2 * e + which) * HID + m * P
        return self.early[:, at:at + P]

    def WF(self, name):
        a, n = self.fcol[name]
        return self.early[:, a:a + n]

    def W1(self, name, rows=P):
        a, n = self.l1col[name]
        return self.late[0:rows, a:a + n]

    def V(self, name, i=0, rows=P):
        a = VCOL[name][0]
        return self.vec[0:rows, a + i:a + i + 1]

    def ra_pair(self, *key):
        at = 4 + self.ra.pair(key)
        return self.ps[:, at:at + 2, :]


def half(s):
    return slice(s * HALF, (s + 1) * HALF)


def tile(t):
    return slice(t * P, (t + 1) * P)


def seq(b):
    return slice(b * SEQ, (b + 1) * SEQ)



def norm_pe(K, pe, name, src, ready, rows=P):
    c, m = ("center", "mean") if rows == P else ("center64", "mean64")
    for s in range(HALVES):
        bank = K.rv.claim(name, "c", s)
        for w in ready(s):
            pe.wait_ge(*w)
        if K.rv.reused(name, "c", s):
            pe.wait_ge(*K.rv.room(name, "c", s))
        pe.matmul(bank[0:rows, :], K.C(c, rows), src[0:rows, half(s)], start=True, stop=True).then_inc(
            *K.rv.fill(name, "c", s))
    for s in range(HALVES):
        bank = K.ra.claim(name, "v", s)
        pe.wait_ge(*K.m.since("squared", name, s))
        if K.ra.reused(name, "v", s):
            pe.wait_ge(*K.ra.room(name, "v", s))
        pe.matmul(bank[0:rows, :], K.C(m, rows), K.sq[0:rows, half(s)], start=True, stop=True).then_inc(
            *K.ra.fill(name, "v", s))


def both_tables(act):
    act.preload_act_table_set("natural_log_exp_and_others")


def norm_act(K, act, name, rows=P):
    for s in range(HALVES):
        act.wait_ge(*K.rv.full(name, "c", s))
        act.activation(K.sq[0:rows, half(s)], K.rv.bank(name, "c", s)[0:rows, :], ACT.Square).then_inc(
            *K.m.done("squared", name, s))
    for s in range(HALVES):
        act.wait_ge(*K.ra.full(name, "v", s))
        act.activation(K.rstd[0:rows, half(s)], K.ra.bank(name, "v", s)[0:rows, :], ACT.Ln,
                       bias=K.V("eps", rows=rows)).then_inc(*K.ra.free((name, "v", s)))
        act.wait_ge(*K.ra.freed(name, "v", s))
        act.activation(K.rstd[0:rows, half(s)], K.rstd[0:rows, half(s)], ACT.Exp, scale=-0.5).then_inc(
            *K.m.done("rstd", name, s))


def norm_dve(K, dve, name, dst, affine=None, second=None, rows=P):
    for s in range(HALVES):
        dve.wait_ge(*K.m.since("rstd", name, s))
        dve.tensor_tensor(dst[0:rows, half(s)], K.rv.bank(name, "c", s)[0:rows, :], K.rstd[0:rows, half(s)],
                          ALU.mult).then_inc(*K.rv.free((name, "c", s)))
    for s in range(HALVES):
        if second:
            other, g, b = second
            dve.wait_ge(*K.rv.freed(name, "c", s))
            dve.tensor_scalar(other[0:rows, half(s)], dst[0:rows, half(s)], K.V(g, rows=rows), K.V(b, rows=rows),
                              ALU.mult, ALU.add).then_inc(*K.m.done("affine", name, "second", s))
            dve.wait_ge(*K.m.since("affine", name, "second", s))
        if affine:
            g, b = affine
            dve.wait_ge(*K.rv.freed(name, "c", s))
            dve.tensor_scalar(dst[0:rows, half(s)], dst[0:rows, half(s)], K.V(g, rows=rows), K.V(b, rows=rows),
                              ALU.mult, ALU.add).then_inc(*K.m.done("affine", name, s))


def normed(K, name):
    return lambda s: [K.rv.freed(name, "c", s)]


def affined(K, name):
    return lambda s: [K.m.since("affine", name, s)]



def project_pe(K, pe, name, weights, src, ready, rows=P, outs=P):
    for g, w in enumerate(weights):
        for s in range(HALVES):
            bank = K.ra.claim(name, g, s)
            if g == 0:
                for x in ready(s):
                    pe.wait_ge(*x)
            if K.ra.reused(name, g, s):
                pe.wait_ge(*K.ra.room(name, g, s))
            pe.matmul(bank[0:outs, :], w, src[0:rows, half(s)], start=True, stop=True).then_inc(
                *K.ra.fill(name, g, s))


def project_act(K, act, name, count, dst, func, bias=None, after=None, outs=P):
    for g in range(count):
        if after:
            for w in after(g):
                act.wait_ge(*w)
        act.wait_ge(*K.ra.full(name, g, 1))
        pair = K.ra_pair(name, g, 0)
        act.activation(dst(g)[0:outs].rearrange("p (s t) -> p s t", s=HALVES), pair[0:outs], func,
                       bias=bias(g) if bias else 0.0).then_inc(*K.ra.free((name, g, 0), (name, g, 1)))


def projected(K, name, g):
    return [K.ra.freed(name, g, 1)]


def as_bf16(K, pool, name, count, src, dst):
    for g in range(count):
        pool.wait_ge(*K.ra.freed(name, g, 1))
        pool.tensor_copy(dst[:, g, :], src[:, g, :]).then_inc(*K.m.done("rounded", name, g))



def rope_pe(K, pe, name, w, ws, src, ready, rows):
    for s in range(HALVES):
        for part, mat in (("plain", w), ("swapped", ws)):
            bank = K.rv.claim(name, s, part)
            if part == "plain":
                for x in ready(s):
                    pe.wait_ge(*x)
            if K.rv.reused(name, s, part):
                pe.wait_ge(*K.rv.room(name, s, part))
            pe.matmul(bank, mat, src[0:rows, half(s)], start=True, stop=True).then_inc(*K.rv.fill(name, s, part))


def rope_dve(K, dve, name, dst):
    cos = K.W0("cos").unsqueeze(1).broadcast_to((P, 2, SEQ))
    sin = K.W0("sin").unsqueeze(1).broadcast_to((P, 2, SEQ))
    for s in range(HALVES):
        out = dst[:, half(s)].rearrange("p (b t) -> p b t", b=2)
        tmp = K.turned[:, half(s)].rearrange("p (b t) -> p b t", b=2)
        dve.wait_ge(*K.rv.full(name, s, "plain"))
        dve.tensor_tensor(out, K.rv.bank(name, s, "plain").rearrange("p (b t) -> p b t", b=2), cos,
                          ALU.mult).then_inc(*K.rv.free((name, s, "plain")))
        dve.wait_ge(*K.rv.full(name, s, "swapped"))
        dve.tensor_tensor(tmp, K.rv.bank(name, s, "swapped").rearrange("p (b t) -> p b t", b=2), sin,
                          ALU.mult).then_inc(*K.rv.free((name, s, "swapped")))
        dve.wait_ge(*K.rv.freed(name, s, "swapped"))
        dve.tensor_tensor(out, out, tmp, ALU.add).then_inc(*K.m.done("rotated", name, s))



LEVELS = {"q": (0, 0, 1, 1, 0, 2), "k": (0, 1, 0, 1, 2, 0)}


def selectors_dve(K, dve):
    dve.memset(K.sel[:, :, :, :], 0.0).then_inc(*K.m.done("setup", "sel"))
    dve.wait_ge(*K.m.since("setup", "sel"))
    ident = K.B("ident").rearrange("k (n i d) -> k n i d", i=2, d=8)
    for x, t in enumerate("qk"):
        for c, level in enumerate(LEVELS[t]):
            rows = K.sel[:, 3 * x + level, :, :].rearrange("k n (i m) -> k n i m", i=2)
            dve.tensor_copy(rows[:, :, :, 8 * c:8 * c + 8], ident).then_inc(*K.m.done("setup", "sel", t, c))
    dve.wait_ge(*K.m.since("setup", "sel", "k", 5))


def level(K, t, n):
    return K.part[:, 3 * "qk".index(t) + n, :]


def split_act(K, act, name, t, src, ready):
    for s in range(HALVES):
        for w in ready(s):
            act.wait_ge(*w)
        act.activation(level(K, t, 0)[:, half(s)], src[:, half(s)], ACT.Copy).then_inc(
            *K.m.done("coarse", name, t, 0, s))
    for s in range(HALVES):
        act.wait_ge(*K.m.since("fine", name, t, 1, s))
        act.activation(level(K, t, 1)[:, half(s)], src[:, half(s)], ACT.Copy).then_inc(
            *K.m.done("coarse", name, t, 1, s))


def split_dve(K, dve, name, t, src):
    for s in range(HALVES):
        dve.wait_ge(*K.m.since("coarse", name, t, 0, s))
        dve.tensor_tensor(src[:, half(s)], src[:, half(s)], level(K, t, 0)[:, half(s)], ALU.subtract).then_inc(
            *K.m.done("fine", name, t, 1, s))
    for s in range(HALVES):
        dve.wait_ge(*K.m.since("coarse", name, t, 1, s))
        dve.tensor_tensor(level(K, t, 2)[:, half(s)], src[:, half(s)], level(K, t, 1)[:, half(s)],
                          ALU.subtract).then_inc(*K.m.done("fine", name, t, 2, s))


def stack_pe(K, pe, name):
    for x, t in enumerate("qk"):
        for n in range(HEADS // 2):
            for s in range(HALVES):
                bank = K.ra.claim(name, t, n, s)
                if n == 0:
                    pe.wait_ge(*K.m.since("coarse", name, t, 1, s))
                    pe.wait_ge(*K.m.since("fine", name, t, 2, s))
                if K.ra.reused(name, t, n, s):
                    pe.wait_ge(*K.ra.room(name, t, n, s))
                for i in range(3):
                    mm = pe.matmul(bank, K.sel[:, 3 * x + i, n, :], level(K, t, i)[:, half(s)], start=(i == 0),
                                   stop=(i == 2))
                mm.then_inc(*K.ra.fill(name, t, n, s))


def stack_act(K, act, name):
    for t in "qk":
        for n in range(HEADS // 2):
            act.wait_ge(*K.ra.full(name, t, n, 1))
            act.activation(K.stack[t][:, n, :].rearrange("p (s t) -> p s t", s=HALVES), K.ra_pair(name, t, n, 0),
                           ACT.Copy).then_inc(*K.ra.free((name, t, n, 0), (name, t, n, 1)))


def stacked(K, name):
    return lambda g: [K.ra.freed(name, "k", HEADS // 2 - 1, 1)]



def values_pe(K, pe, name, w, src, ready, rows, wide):
    if wide:
        for t in range(TILES):
            bank = K.ra.claim(name, "v", t)
            for x in ready(t // 4):
                pe.wait_ge(*x)
            if K.ra.reused(name, "v", t):
                pe.wait_ge(*K.ra.room(name, "v", t))
            pe.matmul(bank, src[0:rows, tile(t)], w, start=True, stop=True).then_inc(*K.ra.fill(name, "v", t))
        return
    for s in range(HALVES):
        bank = K.rv.claim(name, "v", s)
        for x in ready(s):
            pe.wait_ge(*x)
        if K.rv.reused(name, "v", s):
            pe.wait_ge(*K.rv.room(name, "v", s))
        for i in range(4):
            mm = pe.matmul(bank[:, tile(i)], src[0:rows, tile(4 * s + i)], w, start=True, stop=True)
        mm.then_inc(*K.rv.fill(name, "v", s))


def values_act(K, act, name):
    for t in range(0, TILES, 2):
        act.wait_ge(*K.ra.full(name, "v", t + 1))
        act.activation(K.v[:, t:t + 2, :, :].rearrange("p a h d -> p a (h d)"), K.ra_pair(name, "v", t),
                       ACT.Copy).then_inc(*K.ra.free((name, "v", t), (name, "v", t + 1)))


def values_dve(K, dve, name, bias):
    for s in range(HALVES):
        src = K.rv.bank(name, "v", s).rearrange("p (a h d) -> p a h d", a=4, h=HEADS)
        dve.wait_ge(*K.rv.full(name, "v", s))
        for i in range(4):
            dst = K.v[:, 4 * s + i, :, 0:8]
            if bias is None:
                op = dve.tensor_copy(dst, src[:, i])
            else:
                op = dve.tensor_tensor(dst, src[:, i], bias.rearrange("p (h d) -> p h d", h=HEADS), ALU.add)
            if i < 3:
                op.then_inc(*K.m.done("value", name, 4 * s + i))
        op.then_inc(*K.rv.free((name, "v", s)))



def masked(kind):
    return kind in ("page", "causal")


def operands(K, dims, b, g, j):
    h = 4 * g + j
    if dims == 8:
        rows = slice(64 * (h % 2), 64 * (h % 2) + 64)
        q, k = (K.stack[t][rows, h // 2, seq(b)] for t in "qk")
        return q, k, q, k
    rows = slice(32 * j, 32 * j + 32)
    return (K.qb[rows, g, seq(b)], K.kb[rows, g, seq(b)], K.bands[:, (GROUPS * b + g) % BANDS, j, :],
            K.k[:, g, seq(b)])


def scores_pe(K, pe, name, b, g, j, dims, kind, ready):
    h = 4 * g + j
    query, key = operands(K, dims, b, g, j)[0:2]
    bank = K.rv.claim(name, "s", b, h)
    if b == 0 and j == 0:
        for w in ready(g):
            pe.wait_ge(*w)
    if K.rv.reused(name, "s", b, h):
        pe.wait_ge(*K.rv.room(name, "s", b, h))
    if masked(kind):
        diagonal = bank.rearrange("p (a k) -> p a k", a=4)[:, 0:3:2, :]
        pe.matmul(diagonal, K.B("ident"), K.B(kind).unsqueeze(1).broadcast_to((P, 2, P)), start=True, stop=False,
                  skip_group_check=True)
        pe.matmul(bank[:, 0:P], query[:, 0:P], key[:, 0:P], start=False, stop=False,
                  skip_group_check=True)
        mm = pe.matmul(bank[:, P:3 * P], query[:, P:], key, start=False, stop=True,
                       skip_group_check=True)
    else:
        pe.matmul(bank[:, 0:SEQ], query[:, 0:P], key, start=True, stop=False,
                  skip_group_check=True)
        mm = pe.matmul(bank[:, SEQ:], query[:, P:], key, start=False, stop=True,
                       skip_group_check=True)
    mm.then_inc(*K.rv.fill(name, "s", b, h))


def maxima_dve(K, dve, name, b, g, j, kind):
    h = 4 * g + j
    n, w = (3, P) if masked(kind) else (2, SEQ)
    src = K.rv.bank(name, "s", b, h)[:, 0:n * w].rearrange("p (a k) -> p a k", a=n)
    dve.wait_ge(*K.rv.full(name, "s", b, h))
    dve.tensor_reduce(K.maxes[:, b % 2, h, 0:n], src, AX.X, ALU.max).then_inc(*K.rv.free((name, "s", b, h)))


def shift_dve(K, dve, name, b, kind):
    m, out = K.maxes[:, b % 2], K.negmax[:, b % 2]
    dve.wait_ge(*K.rv.freed(name, "s", b, HEADS - 1))
    if masked(kind):
        dve.tensor_tensor(m[:, :, 1], m[:, :, 1], m[:, :, 2], ALU.max).then_inc(*K.m.done("joined", name, b))
        dve.wait_ge(*K.m.since("joined", name, b))
    dve.tensor_scalar(out, m[:, :, 0:2].rearrange("p h a -> p a h"), -1.0, None, ALU.mult).then_inc(
        *K.m.done("negated", name, b))


def turn_pe(K, pe, name, b):
    bank = K.rv.claim(name, "m", b)
    pe.wait_ge(*K.m.since("negated", name, b))
    if K.rv.reused(name, "m", b):
        pe.wait_ge(*K.rv.room(name, "m", b))
    for a in range(2):
        mm = pe.transpose(bank[0:HEADS, tile(a)], K.negmax[:, b % 2, a, :], K.C("ident"))
    mm.then_inc(*K.rv.fill(name, "m", b))


def turned_dve(K, dve, name, b):
    dve.wait_ge(*K.rv.full(name, "m", b))
    if b >= 2:
        dve.wait_ge(*K.ra.full(name, "t", b - 2, HEADS - 1))
    dve.tensor_copy(K.shift[0:HEADS, b % 2, :], K.rv.bank(name, "m", b)[0:HEADS, 0:SEQ]).then_inc(
        *K.rv.free((name, "m", b)))


BANDS = 4


def band_ring(where):
    return where[:, 0:BANDS * 4 * SEQ].rearrange("p (n j t) -> p n j t", n=BANDS, j=4)


def banded(j):
    return "banded_v" if j < 2 else "banded_p"


def bands(K, eng, name, b, g, heads, ready):
    u = GROUPS * b + g
    if b == 0:
        for w in ready(g):
            eng.wait_ge(*w)
    if u >= BANDS:
        ub, ug = divmod(u - BANDS, GROUPS)
        eng.wait_ge(*K.ra.full(name, "t", ub, 4 * ug + 3))
    for j in heads:
        eng.tensor_scalar(K.bands[:, u % BANDS, j, :], K.q[:, g, seq(b)], K.C("headrows")[:, j:j + 1], None,
                           ALU.mult).then_inc(*K.m.done(banded(j), name, b, g, j))


def exact_pe(K, pe, name, b, g, j, dims, kind, ready):
    h = 4 * g + j
    query, key = operands(K, dims, b, g, j)[2:4]
    bank = K.ra.claim(name, "t", b, h)
    if dims == 32:
        pe.wait_ge(*K.m.since(banded(j), name, b, g, j))
    if h == 0:
        pe.wait_ge(*K.rv.freed(name, "m", b))
    if b == 0 and j == 0:
        for w in ready(g):
            pe.wait_ge(*w)
    if K.ra.reused(name, "t", b, h):
        pe.wait_ge(*K.ra.room(name, "t", b, h))
    shift = K.shift[:, b % 2, :]
    if masked(kind):
        pe.matmul(bank[:, 0:SEQ], K.headsel[:, h, :], shift, start=True, stop=False, skip_group_check=True)
        pe.matmul(bank[:, SEQ:3 * P], K.headsel[:, h, :], shift[:, P:], start=False, stop=False,
                  skip_group_check=True)
        diagonal = bank.rearrange("p (a k) -> p a k", a=4)[:, 0:3:2, :]
        pe.matmul(diagonal, K.B("ident"), K.B(kind + "T").unsqueeze(1).broadcast_to((P, 2, P)), start=False,
                  stop=False, skip_group_check=True)
        pe.matmul(bank[:, 0:SEQ], key[:, 0:P], query, start=False, stop=False,
                  skip_group_check=True)
        mm = pe.matmul(bank[:, SEQ:3 * P], key[:, P:], query[:, P:], start=False, stop=True,
                       skip_group_check=True)
    else:
        pe.matmul(bank, K.headsel[:, h, :], shift.unsqueeze(1).broadcast_to((P, 2, SEQ)), start=True, stop=False,
                  skip_group_check=True)
        pe.matmul(bank[:, 0:SEQ], key[:, 0:P], query, start=False, stop=False,
                  skip_group_check=True)
        mm = pe.matmul(bank[:, SEQ:], key[:, P:], query, start=False, stop=True,
                       skip_group_check=True)
    mm.then_inc(*K.ra.fill(name, "t", b, h))


def slot(b, g, i):
    return (2 * (GROUPS * b + g) + i) % 4


def exps_act(K, act, name, b, g, kind, scale):
    n = 3 * P if masked(kind) else HALF
    for i in range(2):
        h = 4 * g + 2 * i
        u = GROUPS * b + g
        if u >= 2:
            ub, ug = divmod(u - 2, GROUPS)
            act.wait_ge(*K.ro.full(name, "o", ub, ug))
        act.wait_ge(*K.ra.full(name, "t", b, h + 1))
        act.activation(K.prob[:, slot(b, g, i), :, 0:n], K.ra_pair(name, "t", b, h)[:, :, 0:n], ACT.Exp,
                       scale=scale).then_inc(*K.ra.free((name, "t", b, h), (name, "t", b, h + 1)))


def kept_pool(K, pool, name, b, g):
    u = GROUPS * b + g
    for i in range(2):
        for a in range(2):
            src = K.prob[:, slot(b, g, i), a, :].rearrange("p (c q) -> p c q", c=4)[:, 0:4:3, :]
            if i == 0 and a == 0 and u >= 1:
                ub, ug = divmod(u - 1, GROUPS)
                pool.wait_ge(*K.ro.full(name, "o", ub, ug))
            pool.wait_ge(*K.ra.freed(name, "t", b, 4 * g + 2 * i + 1))
            pool.tensor_tensor(K.kept[:, i, a, :, :], src, K.C("upper").unsqueeze(1).broadcast_to((P, 2, P)),
                               ALU.mult).then_inc(*K.m.done("kept", name, b, g, i, a))


def weigh_pe(K, pe, name, b, g, kind, ready):
    bank = K.ro.claim(name, "o", b, g)
    if b == 0 and g == 0:
        for w in ready:
            pe.wait_ge(*w)
    pe.wait_ge(*K.ra.freed(name, "t", b, 4 * g + 3))
    if kind == "upper":
        pe.wait_ge(*K.m.since("kept", name, b, g, 1, 1))
    if K.ro.reused(name, "o", b, g):
        pe.wait_ge(*K.ro.room(name, "o", b, g))

    def e(j, lo, hi):
        return K.prob[:, slot(b, g, j // 2), j % 2, lo:hi]

    ones = K.C("ones")[:, 0:32]
    steps = []
    if masked(kind):
        steps = [("v", 0, 0, SEQ, 0), ("v", 1, P, SEQ, SEQ), ("one", 0, 0, SEQ, 0), ("one", 1, P, SEQ, SEQ)]
    elif kind == "all":
        steps = [("v", 0, 0, SEQ, 0), ("v", 1, 0, SEQ, SEQ), ("one", 0, 0, SEQ, 0), ("one", 1, 0, SEQ, SEQ)]
    else:
        steps = [("keep", 0, 0, P, 0), ("v", 1, 0, P, SEQ), ("keep", 1, P, SEQ, 0),
                 ("one", 0, 0, SEQ, 0), ("one", 1, 0, SEQ, SEQ)]
    for n, (what, kc, q0, q1, col) in enumerate(steps):
        for j in range(4):
            h = 4 * g + j
            value = K.v[:, 2 * b + kc, h, :]
            if what == "keep":
                moving = K.kept[:, j // 2, j % 2, kc, :]
            else:
                moving = e(j, col, col + q1 - q0)
            at = SEQ if what == "one" else 0
            mm = pe.matmul(bank[32 * j:32 * j + 32, at + q0:at + q1], ones if what == "one" else value, moving,
                           start=(n == 0), stop=(n == len(steps) - 1), skip_group_check=True)
    mm.then_inc(*K.ro.fill(name, "o", b, g))


def weighed_act(K, act, name, b, g):
    u = GROUPS * b + g
    act.wait_ge(*K.ro.full(name, "o", b, g))
    if u >= 2:
        act.wait_ge(*K.m.since("divided", name, *TURNS[u - 2]))
    act.activation(K.weighed[:, u % 2, :], K.ro.bank(name, "o", b, g), ACT.Copy).then_inc(
        *K.ro.free((name, "o", b, g)))


def divide_dve(K, dve, name, b, g):
    w = K.weighed[:, (GROUPS * b + g) % 2, :]
    dve.wait_ge(*K.ro.freed(name, "o", b, g))
    dve.reciprocal(w[:, SEQ:], w[:, SEQ:]).then_inc(*K.m.done("recip", name, b, g))
    dve.wait_ge(*K.m.since("recip", name, b, g))
    dve.tensor_tensor(K.q[:, g, seq(b)], w[:, 0:SEQ], w[:, SEQ:], ALU.mult).then_inc(
        *K.m.done("divided", name, b, g))


TURNS = [(b, g) for b in range(PB) for g in range(GROUPS)]
AHEAD = GROUPS + 1


def attention_pe(K, pe, name, dims, kind, rounded, exact, values):
    for u in range(AHEAD):
        for j in range(4):
            if u == GROUPS and j == 1:
                turn_pe(K, pe, name, 0)
            scores_pe(K, pe, name, *TURNS[u], j, dims, kind, rounded)
    for u, (b, g) in enumerate(TURNS):
        for j in range(4):
            if j == 1 and g == GROUPS - 1 and b + 1 < PB:
                turn_pe(K, pe, name, b + 1)
            if u + AHEAD < len(TURNS):
                scores_pe(K, pe, name, *TURNS[u + AHEAD], j, dims, kind, rounded)
            exact_pe(K, pe, name, b, g, j, dims, kind, exact)
        if u:
            weigh_pe(K, pe, name, *TURNS[u - 1], kind, values)
    weigh_pe(K, pe, name, *TURNS[-1], kind, values)


def attention_dve(K, dve, name, dims, kind, ready=None):
    for u in range(AHEAD):
        if u == GROUPS:
            shift_dve(K, dve, name, 0, kind)
        for j in range(4):
            if u == GROUPS and j == 1:
                turned_dve(K, dve, name, 0)
            maxima_dve(K, dve, name, *TURNS[u], j, kind)
        if u < 2 and dims == 32:
            bands(K, dve, name, *TURNS[u], (0, 1), ready)
    for u, (b, g) in enumerate(TURNS):
        turn = g == GROUPS - 1 and b + 1 < PB
        if turn:
            shift_dve(K, dve, name, b + 1, kind)
        for j in range(4):
            if turn and j == 1:
                turned_dve(K, dve, name, b + 1)
            if u + AHEAD < len(TURNS):
                maxima_dve(K, dve, name, *TURNS[u + AHEAD], j, kind)
            if j == 1 and u >= 2:
                divide_dve(K, dve, name, *TURNS[u - 2])
            if j == 1 and u + 2 < len(TURNS) and dims == 32:
                bands(K, dve, name, *TURNS[u + 2], (0, 1), ready)
    for u in (-2, -1):
        divide_dve(K, dve, name, *TURNS[u])


def attention_act(K, act, name, kind, scale):
    for u, (b, g) in enumerate(TURNS):
        exps_act(K, act, name, b, g, kind, scale)
        if u:
            weighed_act(K, act, name, *TURNS[u - 1])
    weighed_act(K, act, name, *TURNS[-1])


def attention_pool(K, pool, name, kind, ready):
    turns = [(b, g) for b in range(PB) for g in range(GROUPS)]
    for b, g in turns[:2]:
        bands(K, pool, name, b, g, (2, 3), ready)
    for u, (b, g) in enumerate(turns):
        if u + 2 < len(turns):
            bands(K, pool, name, *turns[u + 2], (2, 3), ready)
        if kind == "upper":
            kept_pool(K, pool, name, b, g)



def gather_pe(K, pe, name, weights, src, ready):
    for s in range(HALVES):
        bank = K.ro.claim(name, s)
        if K.ro.reused(name, s):
            pe.wait_ge(*K.ro.room(name, s))
        for i, w in enumerate(weights):
            for x in ready(i, s):
                pe.wait_ge(*x)
            mm = pe.matmul(bank, w, src(i, s), start=(i == 0), stop=(i == len(weights) - 1))
        mm.then_inc(*K.ro.fill(name, s))


def residual_dve(K, dve, name, dst, base, bias=None, ready=None):
    for s in range(HALVES):
        dve.wait_ge(*K.ro.full(name, s))
        if ready:
            for w in ready(s):
                dve.wait_ge(*w)
        if bias is None:
            op = dve.tensor_tensor(dst[:, half(s)], K.ro.bank(name, s), base[:, half(s)], ALU.add)
        else:
            op = dve.scalar_tensor_tensor(out=dst[:, half(s)], in0=K.ro.bank(name, s), scalar=bias,
                                          in1=base[:, half(s)], op0=ALU.add, op1=ALU.add)
        op.then_inc(*K.ro.free((name, s)))


def added(K, name):
    return lambda s: [K.ro.freed(name, s)]


def add_dve(K, dve, name, dst, a, after):
    for s in range(HALVES):
        for w in after(s):
            dve.wait_ge(*w)
        dve.tensor_tensor(dst[:, half(s)], dst[:, half(s)], a[:, half(s)], ALU.add).then_inc(
            *K.m.done("summed", name, s))


def summed(K, name):
    return lambda s: [K.m.since("summed", name, s)]


def blocks(w, n=4):
    return [w[:, i * P:(i + 1) * P] for i in range(n)]



def ffn_pe(K, pe, name, w1, w2, src, ready):
    project_pe(K, pe, name + "_up", blocks(w1), src, ready)
    gather_pe(K, pe, name + "_down", blocks(w2), lambda i, s: K.k[:, i, half(s)],
              lambda i, s: projected(K, name + "_up", i) if s == 0 else [])


def ffn_act(K, act, name, bias):
    project_act(K, act, name + "_up", 4, lambda g: K.k[:, g, :], ACT.Gelu, bias=lambda g: K.V(bias, g))
    both_tables(act)



def layer0_pe(K, pe):
    norm_pe(K, pe, "l0", K.xw, lambda s: [K.m.since("x_loaded", 0)])
    project_pe(K, pe, "lat", [K.W0("w_down")], K.xn, normed(K, "l0"), outs=64)
    rope_pe(K, pe, "rq", K.W0("wq"), K.W0("wqs"), K.xn, normed(K, "l0"), P)
    rope_pe(K, pe, "rk", K.W0("wk", 64), K.W0("wks", 64), K.yc, lambda s: projected(K, "lat", 0), 64)
    values_pe(K, pe, "lv", K.W0("wv", 64), K.yc, lambda s: projected(K, "lat", 0), 64, False)
    stack_pe(K, pe, "sA")
    attention_pe(K, pe, "A", 8, "page", stacked(K, "sA"), lambda g: [], [K.rv.freed("lv", "v", 1)])
    gather_pe(K, pe, "wo", blocks(K.W0("wo")), lambda i, s: K.q[:, i, half(s)],
              lambda i, s: [K.m.since("divided", "A", PB - 1, GROUPS - 1)] if i == 0 else [])

    norm_pe(K, pe, "l1", K.xw, added(K, "wo"))
    project_pe(K, pe, "xq", [K.W0("xq")], K.xn, normed(K, "l1"))
    project_pe(K, pe, "xk", [K.W0("xk")], K.xn, normed(K, "l1"))
    values_pe(K, pe, "xv", K.W0("xv"), K.xn, normed(K, "l1"), P, False)
    stack_pe(K, pe, "sB")
    project_pe(K, pe, "cq", [K.W0("cq")], K.xn, lambda s: [])
    project_pe(K, pe, "ck", [K.W0("ck", 64)], K.ctx, lambda s: [K.m.since("ctx_loaded", 0)], rows=64)
    attention_pe(K, pe, "B", 8, "causal", stacked(K, "sB"), lambda g: [], [K.rv.freed("xv", "v", 1)])
    gather_pe(K, pe, "wp_self", blocks(K.W0("wp")), lambda i, s: K.q[:, i, half(s)],
              lambda i, s: [K.m.since("divided", "B", PB - 1, GROUPS - 1)] if i == 0 else [])

    values_pe(K, pe, "cv", K.W0("cv", 64), K.ctx, lambda s: [], 64, False)
    stack_pe(K, pe, "sC")
    attention_pe(K, pe, "C", 8, "all", stacked(K, "sC"), lambda g: [], [K.rv.freed("cv", "v", 1)])
    gather_pe(K, pe, "wp_cross", blocks(K.W0("wp")), lambda i, s: K.q[:, i, half(s)],
              lambda i, s: [K.m.since("divided", "C", PB - 1, GROUPS - 1)] if i == 0 else [])
    norm_pe(K, pe, "l2", K.xw, added(K, "wp_cross"))
    bank = K.rv.claim("logits")
    pe.wait_ge(*K.rv.freed("l2", "c", 1))
    for t in range(TILES):
        mm = pe.matmul(bank[:, EXPERTS * t:EXPERTS * (t + 1)], K.xn[:, tile(t)], K.wg[:, :], start=True, stop=True)
    mm.then_inc(*K.rv.fill("logits"))


def layer0_act(K, act):
    both_tables(act)
    scale = 1.0 / 8 ** 0.5
    norm_act(K, act, "l0")
    project_act(K, act, "lat", 1, lambda g: K.yc[0:64, :], ACT.Copy, outs=64)
    split_act(K, act, "sA", "q", K.ya, lambda s: [K.m.since("rotated", "rq", s)])
    split_act(K, act, "sA", "k", K.yb, lambda s: [K.m.since("rotated", "rk", s)])
    stack_act(K, act, "sA")
    attention_act(K, act, "A", "page", scale)
    norm_act(K, act, "l1")
    project_act(K, act, "xq", 1, lambda g: K.ya, ACT.Identity, bias=lambda g: K.V("x_bq"))
    project_act(K, act, "xk", 1, lambda g: K.yb, ACT.Identity, bias=lambda g: K.V("x_bk"))
    split_act(K, act, "sB", "q", K.ya, lambda s: projected(K, "xq", 0))
    split_act(K, act, "sB", "k", K.yb, lambda s: projected(K, "xk", 0))
    stack_act(K, act, "sB")
    project_act(K, act, "cq", 1, lambda g: K.ya, ACT.Identity, bias=lambda g: K.V("x_bcq"))
    project_act(K, act, "ck", 1, lambda g: K.yb, ACT.Identity, bias=lambda g: K.V("x_bck"))
    split_act(K, act, "sC", "q", K.ya, lambda s: projected(K, "cq", 0))
    split_act(K, act, "sC", "k", K.yb, lambda s: projected(K, "ck", 0))
    attention_act(K, act, "B", "causal", scale)
    stack_act(K, act, "sC")
    attention_act(K, act, "C", "all", scale)
    norm_act(K, act, "l2")


def layer0_dve(K, dve, i):
    norm_dve(K, dve, "l0", K.xn)
    rope_dve(K, dve, "rq", K.ya)
    split_dve(K, dve, "sA", "q", K.ya)
    rope_dve(K, dve, "rk", K.yb)
    split_dve(K, dve, "sA", "k", K.yb)
    values_dve(K, dve, "lv", None)
    attention_dve(K, dve, "A", 8, "page")
    residual_dve(K, dve, "wo", K.xw, K.xw)
    norm_dve(K, dve, "l1", K.xn)
    split_dve(K, dve, "sB", "q", K.ya)
    split_dve(K, dve, "sB", "k", K.yb)
    values_dve(K, dve, "xv", K.W0("bv"))
    split_dve(K, dve, "sC", "q", K.ya)
    split_dve(K, dve, "sC", "k", K.yb)
    attention_dve(K, dve, "B", 8, "causal")
    residual_dve(K, dve, "wp_self", K.xw, K.xw, K.V("x_bp"))
    values_dve(K, dve, "cv", K.W0("bcv"))
    attention_dve(K, dve, "C", 8, "all")
    residual_dve(K, dve, "wp_cross", K.xw, K.xw)
    norm_dve(K, dve, "l2", K.xn)
    dve.wait_ge(*K.rv.full("logits"))
    dve.tensor_copy(K.logits[:, bass.ds(i * TILES, TILES), :], K.rv.bank("logits")[:, 0:EXPERTS * TILES].rearrange(
        "p (t e) -> p t e", e=EXPERTS)).then_inc(*K.rv.free(("logits",)))
    dve.wait_ge(*K.rv.freed("logits"))



def router_pe(K, pe):
    for c in range(2):
        bank = K.ro.claim("place", c)
        pe.wait_ge(*K.m.since("gate", f"choice{c}"))
        flat = K.onehot[:, c].rearrange("p n e -> p (n e)")
        pe.matmul(bank[:, 0:P], K.B("before"), flat, start=True, stop=False, skip_group_check=True)
        for n in range(15):
            pe.matmul(bank[:, 8 * (n + 1):P].rearrange("p (n e) -> p n e", e=EXPERTS), K.B("ones"),
                      K.onehot[:, c, n, :].unsqueeze(1).broadcast_to((P, 15 - n, EXPERTS)), start=False,
                      stop=False, skip_group_check=True)
        if c:
            for n in range(16):
                pe.matmul(bank[:, 0:P].rearrange("p (n e) -> p n e", e=EXPERTS), K.B("ones"),
                          K.onehot[:, 0, n, :].unsqueeze(1).broadcast_to((P, 16, EXPERTS)), start=False,
                          stop=False, skip_group_check=True)
        pe.matmul(bank[:, 0:8], K.B("ones"), K.zeros[:, :], start=False, stop=True,
                  skip_group_check=True).then_inc(*K.ro.fill("place", c))


def router_act(K, act):
    act.wait_ge(*K.m.since("gate", "less"))
    act.activation(K.gate[:, 1], K.gate[:, 0], ACT.Exp).then_inc(*K.m.done("gate_exp", 0))


def router_dve(K, dve):
    g, col = K.gate, K.gcol

    def wide(i):
        return col[:, i, :].unsqueeze(2).broadcast_to((P, 16, EXPERTS))

    prio = K.C("prio").unsqueeze(1).broadcast_to((P, 16, EXPERTS))

    def step(op, key):
        op.then_inc(*K.m.done("gate", key))
        dve.wait_ge(*K.m.since("gate", key))

    logits = K.logits[:, :, :]
    step(dve.tensor_reduce(col[:, 0, :], logits, AX.X, ALU.max), "max")
    dve.tensor_tensor(g[:, 0], logits, wide(0), ALU.subtract).then_inc(*K.m.done("gate", "less"))
    dve.wait_ge(*K.m.since("gate_exp", 0))
    step(dve.tensor_reduce(col[:, 1, :], g[:, 1], AX.X, ALU.add), "sum")
    step(dve.reciprocal(col[:, 2, :], col[:, 1, :]), "recip")
    step(dve.tensor_tensor(g[:, 2], g[:, 1], wide(2), ALU.mult), "gates")
    for c in range(2):
        src, eq, pri, oh = g[:, 2 + 4 * c], g[:, 3 + 4 * c], g[:, 4 + 4 * c], g[:, 5 + 4 * c]
        step(dve.tensor_reduce(col[:, 3 + c, :], src, AX.X, ALU.max), f"top{c}")
        step(dve.tensor_tensor(eq, src, wide(3 + c), ALU.is_equal), f"equal{c}")
        step(dve.tensor_tensor(pri, eq, prio, ALU.mult), f"ranked{c}")
        step(dve.tensor_reduce(col[:, 5 + c, :], pri, AX.X, ALU.max), f"first{c}")
        step(dve.tensor_tensor(oh, pri, wide(5 + c), ALU.is_equal), f"hot{c}")
        step(dve.tensor_copy(K.onehot[:, c], oh), f"choice{c}")
        if c == 0:
            step(dve.scalar_tensor_tensor(out=g[:, 6], in0=oh, scalar=-2.0, in1=src, op0=ALU.mult, op1=ALU.add),
                 "rest")
    for c in range(2):
        oh, a = g[:, 5 + 4 * c], g[:, 3 + 4 * c]
        place = K.ro.bank("place", c)[:, 0:P].rearrange("p (n e) -> p n e", e=EXPERTS)
        dve.wait_ge(*K.ro.full("place", c))
        step(dve.scalar_tensor_tensor(out=a, in0=place, scalar=float(CAPACITY), in1=oh, op0=ALU.is_lt,
                                      op1=ALU.mult), f"within{c}")
        step(dve.tensor_tensor(a, a, wide(3 + c), ALU.mult), f"weight{c}")
    step(dve.tensor_tensor(K.weight[:, :, :], g[:, 3], g[:, 7], ALU.add), "share")



def experts_pe(K, pe):
    rows = K.small[0:EXPERTS, 3 * P:11 * P].rearrange("p (e m) -> p e m", e=EXPERTS)
    b2 = K.small[0:EXPERTS, 11 * P:12 * P]
    for s in range(HALVES):
        bank = K.rv.claim("share", s)
        pe.wait_ge(*K.m.since("restored", "weight"))
        for i in range(4):
            mm = pe.transpose(bank[0:EXPERTS, tile(i)], K.weight_now[:, 4 * s + i, :], K.C("ident"))
        mm.then_inc(*K.rv.fill("share", s))
    for s in range(HALVES):
        bank = K.ro.claim("moe", s)
        pe.wait_ge(*K.rv.freed("share", s))
        pe.matmul(bank, b2, K.share[:, half(s)], start=True, stop=False, skip_group_check=True)

    def down(e):
        for s in range(HALVES):
            pe.wait_ge(*K.rv.freed("moe", e, s))
            for m in range(4):
                mm = pe.matmul(K.ro.bank("moe", s), K.expert(e, 1, m), hidden(K, e)[:, m, half(s)],
                               start=False, stop=(e == EXPERTS - 1 and m == 3), skip_group_check=True)
            if e == EXPERTS - 1:
                mm.then_inc(*K.ro.fill("moe", s))
            else:
                mm.then_inc(*K.m.done("hidden_used", e, s))

    for e in range(EXPERTS):
        project_pe(K, pe, f"up{e}", [K.expert(e, 0, m) for m in range(4)], K.xn,
                   lambda s: [K.m.since("xn_loaded", 0), K.m.since(f"expert{e}_loaded", 0)])
        for s in range(HALVES):
            bank = K.rv.claim("moe", e, s)
            if K.rv.reused("moe", e, s):
                pe.wait_ge(*K.rv.room("moe", e, s))
            pe.matmul(bank, rows[:, e, :], K.share[:, half(s)], start=True, stop=True).then_inc(
                *K.rv.fill("moe", e, s))
        if e:
            down(e - 1)
    down(EXPERTS - 1)


def hidden(K, e):
    return K.q if e % 2 else K.k


def experts_act(K, act):
    for e in range(EXPERTS):
        project_act(K, act, f"up{e}", 4, lambda g: hidden(K, e)[:, g, :], ACT.Gelu,
                    bias=lambda g: K.V("moe_b1", 4 * e + g),
                    after=lambda g: [K.m.since("hidden_used", e - 2, 1)] if e >= 2 and g == 0 else [])
    both_tables(act)


def experts_dve(K, dve):
    for s in range(HALVES):
        dve.wait_ge(*K.rv.full("share", s))
        dve.tensor_copy(K.share[:, half(s)], K.rv.bank("share", s)[0:EXPERTS, :]).then_inc(*K.rv.free(("share", s)))
    for e in range(EXPERTS):
        for s in range(HALVES):
            h = hidden(K, e)[:, :, half(s)]
            dve.wait_ge(*K.ra.freed(f"up{e}", 3, 1))
            dve.wait_ge(*K.rv.full("moe", e, s))
            dve.tensor_tensor(h, h, K.rv.bank("moe", e, s).unsqueeze(1).broadcast_to((P, 4, HALF)),
                              ALU.mult).then_inc(*K.rv.free(("moe", e, s)))
    residual_dve(K, dve, "moe", K.xw, K.xw, ready=lambda s: [K.m.since("x_loaded", 0)])


def linear_pe(K, pe):
    kv = K.W1("qkv")[:, P:3 * P]
    for c in range(4):
        bank = K.ra.claim("kv", c)
        for w in affined(K, "n1")(c // 2):
            pe.wait_ge(*w)
        if K.ra.reused("kv", c):
            pe.wait_ge(*K.ra.room("kv", c))
        for i in range(2):
            mm = pe.matmul(bank[:, i * SEQ:(i + 1) * SEQ], K.xn[:, tile(2 * c + i)], kv, start=True, stop=True)
        mm.then_inc(*K.ra.fill("kv", c))
    project_pe(K, pe, "lq", [K.W1("qkv")[:, 0:P]], K.xn, lambda s: [])
    for b in range(PB):
        bank = K.ro.claim("outer", b)
        pe.wait_ge(*K.m.since("elu", "k", b))
        if K.ro.reused("outer", b):
            pe.wait_ge(*K.ro.room("outer", b))
        for i in range(2):
            key = K.q[:, 0, tile(2 * b + i)]
            pe.matmul(bank[:, 0:P], key, K.q[:, 1, tile(2 * b + i)], start=(i == 0), stop=False,
                      skip_group_check=True)
            mm = pe.matmul(bank[:, P:2 * P], key, K.C("ones"), start=False, stop=(i == 1), skip_group_check=True)
        mm.then_inc(*K.ro.fill("outer", b))
    for b in range(PB):
        bank = K.rv.claim("linear", b)
        pe.wait_ge(*K.m.since("elu", "q", b // 2))
        pe.wait_ge(*K.ro.freed("outer", b))
        if K.rv.reused("linear", b):
            pe.wait_ge(*K.rv.room("linear", b))
        for i in range(2):
            mm = pe.matmul(bank[:, i * SEQ:(i + 1) * SEQ], K.q[:, 3, b * SEQ + i * P:b * SEQ + (i + 1) * P],
                           K.yb[:, seq(b)], start=True, stop=True)
        mm.then_inc(*K.rv.fill("linear", b))
    gather_pe(K, pe, "proj", [K.W1("proj")], lambda i, s: K.q[:, 2, half(s)],
              lambda i, s: [K.rv.freed("linear", 2 * s + 1)])


def linear_act(K, act):
    for c in range(4):
        bank = K.ra.bank("kv", c).rearrange("p (i w) -> p i w", i=2)
        at = slice(2 * c * P, 2 * (c + 1) * P)
        act.wait_ge(*K.ra.full("kv", c))
        act.activation(K.q[:, 0, at].rearrange("p (i w) -> p i w", i=2), bank[:, :, 0:P], ACT.Relu).then_inc(
            *K.m.done("elu_part", "relu", c))
        act.activation(K.q[:, 1, at].rearrange("p (i w) -> p i w", i=2), bank[:, :, P:2 * P], ACT.Copy).then_inc(
            *K.m.done("elu_part", "v", c))
        act.activation(K.q[:, 2, at].rearrange("p (i w) -> p i w", i=2), bank[:, :, 0:P], ACT.Exp).then_inc(
            *K.ra.free(("kv", c)))
    act.wait_ge(*K.ra.full("lq", 0, 1))
    pair = K.ra_pair("lq", 0, 0)
    act.activation(K.yb[:, :].rearrange("p (s t) -> p s t", s=2), pair, ACT.Relu).then_inc(
        *K.m.done("elu_part", "relu", "q"))
    act.activation(K.yc[:, :].rearrange("p (s t) -> p s t", s=2), pair, ACT.Exp).then_inc(
        *K.ra.free(("lq", 0, 0), ("lq", 0, 1)))


def linear_dve(K, dve):
    for c in range(4):
        at = slice(2 * c * P, 2 * (c + 1) * P)
        dve.wait_ge(*K.ra.freed("kv", c))
        dve.wait_ge(*K.m.since("elu_part", "v", c))
        dve.scalar_tensor_tensor(out=K.q[:, 0, at], in0=K.q[:, 2, at], scalar=1.0, in1=K.q[:, 0, at], op0=ALU.min,
                                 op1=ALU.add).then_inc(*K.m.done("elu", "k", c))
    for s in range(HALVES):
        dve.wait_ge(*K.ra.freed("lq", 0, 1))
        dve.wait_ge(*K.m.since("elu_part", "relu", "q"))
        dve.scalar_tensor_tensor(out=K.yb[:, half(s)], in0=K.yc[:, half(s)], scalar=1.0, in1=K.yb[:, half(s)],
                                 op0=ALU.min, op1=ALU.add).then_inc(*K.m.done("elu", "q", s))
    for b in range(PB):
        dve.wait_ge(*K.ro.full("outer", b))
        dve.tensor_tensor(K.q[:, 3, seq(b)].rearrange("p (i w) -> p i w", i=2),
                          K.ro.bank("outer", b)[:, 0:SEQ].rearrange("p (i w) -> p i w", i=2),
                          K.C("blocks").unsqueeze(1).broadcast_to((P, 2, P)), ALU.mult).then_inc(
            *K.ro.free(("outer", b)))
    for b in range(PB):
        bank, r = K.rv.bank("linear", b), K.recip[:, b % 2, :]
        dve.wait_ge(*K.rv.full("linear", b))
        dve.tensor_scalar(r, bank[:, SEQ:], 1e-6, None, ALU.add).then_inc(*K.m.done("zsum", b))
        dve.wait_ge(*K.m.since("zsum", b))
        dve.reciprocal(r, r).then_inc(*K.m.done("z", b))
        dve.wait_ge(*K.m.since("z", b))
        dve.tensor_tensor(K.q[:, 2, seq(b)], bank[:, 0:SEQ], r, ALU.mult).then_inc(*K.rv.free(("linear", b)))
    residual_dve(K, dve, "proj", K.ya, K.ya, K.V("proj_b"))


def mixed_pe(K, pe, a, kind, kv_src, kv_ready, kv_rows):
    project_pe(K, pe, a + "q", blocks(K.W1(a + "_q")), K.xn, affined(K, a + "x"))
    project_pe(K, pe, a + "k", blocks(K.W1(a + "_k", kv_rows)), kv_src, kv_ready, rows=kv_rows)
    values_pe(K, pe, a + "v", K.W1(a + "_v", kv_rows), kv_src, lambda s: [], kv_rows, True)
    attention_pe(K, pe, a, 32, kind,
                 lambda g: [K.m.since("rounded", a + "q", g), K.m.since("rounded", a + "k", g)],
                 lambda g: projected(K, a + "k", g), [K.ra.freed(a + "v", "v", TILES - 1)])
    gather_pe(K, pe, a + "o", blocks(K.W1(a + "_li1")), lambda i, s: K.q[:, i, half(s)],
              lambda i, s: [K.m.since("divided", a, PB - 1, GROUPS - 1)] if i == 0 else [])
    norm_pe(K, pe, a + "3", K.yc, added(K, a + "o"))
    ffn_pe(K, pe, a + "f", K.W1(a + "_li2"), K.W1(a + "_li3"), K.xn, affined(K, a + "3"))


def mixed_act(K, act, a, kind):
    project_act(K, act, a + "q", 4, lambda g: K.q[:, g, :], ACT.Copy)
    project_act(K, act, a + "k", 4, lambda g: K.k[:, g, :], ACT.Copy)
    values_act(K, act, a + "v")
    attention_act(K, act, a, kind, 32 ** -0.5)
    norm_act(K, act, a + "3")
    ffn_act(K, act, a + "f", a + "_li2_b")


def mixed_dve(K, dve, a, kind):
    attention_dve(K, dve, a, 32, kind, lambda g: projected(K, a + "q", g))
    residual_dve(K, dve, a + "o", K.yc, K.ya, K.V(a + "_li1_b"))
    norm_dve(K, dve, a + "3", K.xn, affine=(a + "_ln3_g", a + "_ln3_b"))
    residual_dve(K, dve, a + "f_down", K.yc, K.yc, K.V(a + "_li3_b"))
    add_dve(K, dve, a + "out", K.ya, K.yc, added(K, a + "f_down"))


def leaves_pe(K, pe):
    bank = K.rv.claim("nodes")
    for t in range(TILES):
        for w in normed(K, "l5")(t // 4):
            pe.wait_ge(*w)
        if t == 0 and K.rv.reused("nodes"):
            pe.wait_ge(*K.rv.room("nodes"))
        mm = pe.matmul(bank[:, 45 * t:45 * t + 45], K.xn[:, tile(t)], K.W1("nodes"), start=True, stop=True)
    mm.then_inc(*K.rv.fill("nodes"))
    for s in range(HALVES):
        bank = K.rv.claim("leaf", s)
        pe.wait_ge(*K.m.since("tree", "chosen"))
        if K.rv.reused("leaf", s):
            pe.wait_ge(*K.rv.room("leaf", s))
        for i in range(4):
            mm = pe.transpose(bank[0:48, tile(i)], K.tree[:, 1, 4 * s + i, :], K.C("ident"))
        mm.then_inc(*K.rv.fill("leaf", s))
    w1, w2 = K.WF("f_w1"), K.WF("f_w2")
    pe.wait_ge(*K.m.since("feed_loaded", 0))
    for r in range(3):
        outs = [K.ro.claim("leaves", r, s) for s in range(HALVES)]

        def up(m):
            for s in range(HALVES):
                bank = K.ra.claim("hid", r, m, s)
                if K.ra.reused("hid", r, m, s):
                    pe.wait_ge(*K.ra.room("hid", r, m, s))
                if r == 0 and m == 0:
                    pe.wait_ge(*K.rv.freed("leaf", s))
                pe.matmul(bank, w1[:, r * PASS + m * P:r * PASS + (m + 1) * P], K.xn[:, half(s)], start=True,
                          stop=False, skip_group_check=True)
                pe.matmul(bank, K.leafsel[:, 8 * r + m, :], K.lm[:, half(s)], start=False, stop=True,
                          skip_group_check=True).then_inc(*K.ra.fill("hid", r, m, s))

        def down(m):
            w = w2[:, r * PASS + m * P:r * PASS + (m + 1) * P]
            if m == 0:
                for s in range(HALVES):
                    if K.ro.reused("leaves", r, s):
                        pe.wait_ge(*K.ro.room("leaves", r, s))
            pe.wait_ge(*K.ra.freed("hid", r, m, 1))
            h = (K.q if m < 4 else K.k)[:, m % 4, :]
            b2 = K.small[:, r * P:(r + 1) * P]
            for s in range(HALVES):
                if r < 2:
                    if m == 0:
                        pe.matmul(outs[s], b2, K.lt[:, half(s)], start=True, stop=False, skip_group_check=True)
                    mm = pe.matmul(outs[s], w, h[:, half(s)], start=False, stop=(m == 7), skip_group_check=True)
                else:
                    for i in range(4):
                        t = 4 * s + i
                        if m == 0:
                            pe.matmul(outs[s][:, tile(i)], K.lt[:, tile(t)], b2, start=(i == 0), stop=False,
                                      skip_group_check=True)
                    for i in range(4):
                        t = 4 * s + i
                        mm = pe.matmul(outs[s][:, tile(i)], h[:, tile(t)], w, start=False, stop=(m == 7),
                                       skip_group_check=True)
                if m == 7:
                    mm.then_inc(*K.ro.fill("leaves", r, s))
                elif s == 1:
                    mm.then_inc(*K.m.done("hid_used", r, m))

        for m in range(8):
            up(m)
            if m >= 2:
                down(m - 2)
        down(6)
        down(7)
    for b in range(PB):
        bank = K.ra.claim("fs", b)
        pe.wait_ge(*K.ro.freed("leaves", 1, 1))
        if K.ra.reused("fs", b):
            pe.wait_ge(*K.ra.room("fs", b))
        for i in range(2):
            mm = pe.matmul(bank[:, i * SEQ:(i + 1) * SEQ], K.ya[:, b * SEQ + i * P:b * SEQ + (i + 1) * P],
                           K.yb[:, seq(b)], start=True, stop=True)
        mm.then_inc(*K.ra.fill("fs", b))
    for b in range(PB):
        bank = K.ro.claim("ft", b)
        pe.wait_ge(*K.m.since("fnorm", b, 1))
        if K.ro.reused("ft", b):
            pe.wait_ge(*K.ro.room("ft", b))
        for kc in range(2):
            for i in range(2):
                mm = pe.transpose(bank[:, kc * SEQ + i * P:kc * SEQ + (i + 1) * P],
                                  K.prob[:, b, i, kc * P:(kc + 1) * P], K.C("ident"))
        mm.then_inc(*K.ro.fill("ft", b))
        bank = K.rv.claim("fo", b)
        pe.wait_ge(*K.ro.freed("ft", b))
        pe.wait_ge(*K.ro.freed("leaves", 2, 1))
        if K.rv.reused("fo", b):
            pe.wait_ge(*K.rv.room("fo", b))
        for kc in range(2):
            mm = pe.matmul(bank[:, 0:SEQ], K.yc[:, tile(2 * b + kc)], K.q[:, b, kc * SEQ:(kc + 1) * SEQ],
                           start=(kc == 0), stop=(kc == 1))
        mm.then_inc(*K.rv.fill("fo", b))


def leaves_act(K, act):
    for r in range(3):
        for m in range(8):
            if r:
                if m < 7:
                    act.wait_ge(*K.m.since("hid_used", r - 1, m))
                else:
                    act.wait_ge(*K.ro.full("leaves", r - 1, 1))
            act.wait_ge(*K.ra.full("hid", r, m, 1))
            h = (K.q if m < 4 else K.k)[:, m % 4, :]
            act.activation(h.rearrange("p (s t) -> p s t", s=2), K.ra_pair("hid", r, m, 0), ACT.Relu,
                           bias=K.V("f_b1", 8 * r + m)).then_inc(*K.ra.free(("hid", r, m, 0), ("hid", r, m, 1)))
    for b in range(PB):
        for i in range(2):
            act.wait_ge(*K.m.since("fmax", "scaled", b))
            op = act.activation(K.prob[:, b, i, 0:SEQ], K.ra.bank("fs", b)[:, i * SEQ:(i + 1) * SEQ], ACT.Exp,
                                bias=K.stat[:, 0, 2 * b + i:2 * b + i + 1], scale=P ** -0.5,
                                accum_out=K.stat[:, 1, 2 * b + i:2 * b + i + 1])
            if i:
                op.then_inc(*K.ra.free(("fs", b)))
            else:
                op.then_inc(*K.m.done("fexp", b))


def leaves_dve(K, dve):
    d, c = K.tree[:, 0], K.tree[:, 1]

    def step(op, *key):
        op.then_inc(*K.m.done("tree", *key))
        dve.wait_ge(*K.m.since("tree", *key))

    score = K.rv.bank("nodes")[:, 0:45 * TILES].rearrange("p (t n) -> p t n", t=TILES)
    dve.wait_ge(*K.rv.full("nodes"))
    dve.tensor_tensor(d[:, :, 0:45], score, K.W1("node_b").unsqueeze(1).broadcast_to((P, TILES, 45)),
                      ALU.add).then_inc(*K.rv.free(("nodes",)))
    dve.wait_ge(*K.rv.freed("nodes"))
    step(dve.tensor_scalar(d[:, :, 0:45], d[:, :, 0:45], 0.0, None, ALU.is_ge), "right")
    turn = d[:, :, 0:45].rearrange("p t (r n) -> p t r n", r=3)
    a, b = c.rearrange("p t (r n) -> p t r n", r=3), K.treeb[:, :, :].rearrange("p t (r n) -> p t r n", r=3)
    level = [b, a, b, a]
    step(dve.tensor_copy(b[:, :, :, 1], turn[:, :, :, 0]), "one", 0)
    step(dve.tensor_scalar(b[:, :, :, 0], turn[:, :, :, 0], -1.0, 1.0, ALU.mult, ALU.add), "zero", 0)
    for n in (1, 2, 3):
        w = 2 ** n
        old, new = level[n - 1], level[n]
        for r in range(3):
            step(dve.tensor_tensor(new[:, :, r, 1:2 * w:2], old[:, :, r, 0:w], turn[:, :, r, w - 1:2 * w - 1],
                                   ALU.mult), "one", n, r)
            step(dve.tensor_tensor(new[:, :, r, 0:2 * w:2], old[:, :, r, 0:w], new[:, :, r, 1:2 * w:2],
                                   ALU.subtract), "chosen" if (n, r) == (3, 2) else "zero", *(
                                       () if (n, r) == (3, 2) else (n, r)))
    for s in range(HALVES):
        bank = K.rv.bank("leaf", s)[0:48, :]
        dve.wait_ge(*K.rv.full("leaf", s))
        dve.tensor_scalar(K.lm[:, half(s)], bank, -1.0, None, ALU.add)
        dve.tensor_copy(K.lt[:, half(s)], bank).then_inc(*K.rv.free(("leaf", s)))
    for r, dst in enumerate((K.ya, K.yb, K.yc)):
        for s in range(HALVES):
            dve.wait_ge(*K.ro.full("leaves", r, s))
            dve.tensor_copy(dst[:, half(s)], K.ro.bank("leaves", r, s)).then_inc(*K.ro.free(("leaves", r, s)))
    for b in range(PB):
        at = slice(2 * b, 2 * b + 2)
        dve.wait_ge(*K.ra.full("fs", b))
        dve.tensor_reduce(K.stat[:, 0, at], K.ra.bank("fs", b).rearrange("p (i k) -> p i k", i=2), AX.X,
                          ALU.max).then_inc(*K.m.done("fmax", "raw", b))
        dve.wait_ge(*K.m.since("fmax", "raw", b))
        dve.tensor_scalar(K.stat[:, 0, at], K.stat[:, 0, at], -(P ** -0.5), None, ALU.mult).then_inc(
            *K.m.done("fmax", "scaled", b))
    for b in range(PB):
        at = slice(2 * b, 2 * b + 2)
        dve.wait_ge(*K.ra.freed("fs", b))
        dve.wait_ge(*K.m.since("fexp", b))
        dve.reciprocal(K.stat[:, 1, at], K.stat[:, 1, at]).then_inc(*K.m.done("frecip", b))
        dve.wait_ge(*K.m.since("frecip", b))
        for i in range(2):
            e = K.prob[:, b, i, 0:SEQ]
            dve.tensor_scalar(e, e, K.stat[:, 1, 2 * b + i:2 * b + i + 1], None, ALU.mult).then_inc(
                *K.m.done("fnorm", b, i))
        dve.wait_ge(*K.ro.full("ft", b))
        dve.tensor_copy(K.q[:, b, 0:HALF], K.ro.bank("ft", b)).then_inc(*K.ro.free(("ft", b)))
        dve.wait_ge(*K.rv.full("fo", b))
        dve.tensor_tensor(K.xw[:, seq(b)], K.rv.bank("fo", b)[:, 0:SEQ], K.xw[:, seq(b)], ALU.add).then_inc(
            *K.rv.free(("fo", b)))


def layer1_pe(K, pe):
    experts_pe(K, pe)
    norm_pe(K, pe, "l3", K.xw, added(K, "moe"))
    norm_pe(K, pe, "n1", K.ya, normed(K, "l3"))
    linear_pe(K, pe)
    norm_pe(K, pe, "n2", K.ya, added(K, "proj"))
    ffn_pe(K, pe, "fc", K.W1("fc1"), K.W1("fc2"), K.xn, affined(K, "n2"))

    norm_pe(K, pe, "l4", K.xw, summed(K, "linear"))
    norm_pe(K, pe, "ln1", K.ya, normed(K, "l4"))
    norm_pe(K, pe, "a1x", K.ya, affined(K, "ln1"))
    mixed_pe(K, pe, "a1", "upper", K.yb, lambda s: [K.m.since("affine", "a1x", "second", s)], P)
    norm_pe(K, pe, "ln2", K.ya, summed(K, "a1out"))
    norm_pe(K, pe, "a2x", K.ya, affined(K, "ln2"))
    norm_pe(K, pe, "a2y", K.ctx, lambda s: [K.m.since("ctx_loaded", 0)], rows=CTX)
    mixed_pe(K, pe, "a2", "all", K.yb, affined(K, "a2y"), CTX)

    norm_pe(K, pe, "l5", K.xw, summed(K, "cross"))
    leaves_pe(K, pe)


def layer1_act(K, act):
    experts_act(K, act)
    norm_act(K, act, "l3")
    norm_act(K, act, "n1")
    linear_act(K, act)
    norm_act(K, act, "n2")
    ffn_act(K, act, "fc", "fc1_b")
    norm_act(K, act, "l4")
    norm_act(K, act, "ln1")
    norm_act(K, act, "a1x")
    mixed_act(K, act, "a1", "upper")
    norm_act(K, act, "ln2")
    norm_act(K, act, "a2x")
    norm_act(K, act, "a2y", rows=CTX)
    mixed_act(K, act, "a2", "all")
    norm_act(K, act, "l5")
    leaves_act(K, act)


def layer1_dve(K, dve):
    experts_dve(K, dve)
    norm_dve(K, dve, "l3", K.ya)
    norm_dve(K, dve, "n1", K.xn, affine=("n1_g", "n1_b"))
    linear_dve(K, dve)
    norm_dve(K, dve, "n2", K.xn, affine=("n2_g", "n2_b"))
    residual_dve(K, dve, "fc_down", K.ya, K.ya, K.V("fc2_b"))
    add_dve(K, dve, "linear", K.xw, K.ya, added(K, "fc_down"))

    norm_dve(K, dve, "l4", K.ya)
    norm_dve(K, dve, "ln1", K.ya, affine=("ln1_g", "ln1_b"))
    norm_dve(K, dve, "a1x", K.xn, affine=("a1_lnx_g", "a1_lnx_b"), second=(K.yb, "a1_lny_g", "a1_lny_b"))
    mixed_dve(K, dve, "a1", "upper")
    norm_dve(K, dve, "ln2", K.ya, affine=("ln2_g", "ln2_b"))
    norm_dve(K, dve, "a2x", K.xn, affine=("a2_lnx_g", "a2_lnx_b"))
    norm_dve(K, dve, "a2y", K.yb, affine=("a2_lny_g", "a2_lny_b"), rows=CTX)
    mixed_dve(K, dve, "a2", "all")
    add_dve(K, dve, "cross", K.xw, K.ya, summed(K, "a2out"))
    norm_dve(K, dve, "l5", K.xn)
    leaves_dve(K, dve)


def layer1_pool(K, pool, i):
    pool.tensor_copy(K.weight_now[:, :, :], K.weight[:, bass.ds(i * TILES, TILES), :]).then_inc(
        *K.m.done("restored", "weight"))
    pool.wait_ge(*K.ro.full("moe", 1))
    for a, kind in (("a1", "upper"), ("a2", "all")):
        as_bf16(K, pool, a + "q", 4, K.q, K.qb)
        as_bf16(K, pool, a + "k", 4, K.k, K.kb)
        attention_pool(K, pool, a, kind, lambda g: projected(K, a + "q", g))


def build(nc, known, args):
    (xT, ctxT, vec, const, early, moe, feed, late, wgT, headsel, leafsel, small, out) = args
    with ExitStack() as ctx:
        marks = Marks(nc, ctx, known)
        for kind in KINDS:
            marks.sem(kind)
        lo = min(sem_number(s) for s in marks.sems.values())
        hi = max(sem_number(s) for s in marks.sems.values())
        assert hi - lo + 1 == len(marks.sems)
        K = Chip(nc, ctx, marks)
        x_kept = nc.dram_tensor("x_kept", (P, TOKENS), F32, kind="Internal").ap()
        xn_kept = nc.dram_tensor("xn_kept", (P, TOKENS), F32, kind="Internal").ap()
        K.wg = ctx.enter_context(nc.sbuf_tensor("wg", [P, EXPERTS], F32))
        K.zeros = ctx.enter_context(nc.sbuf_tensor("zeros", [P, 8], BF16))

        def clear():
            with nc.Block() as block:
                @block.gpsimd
                def _(pool):
                    pool.sem_clear(range(lo, hi + 1))

        K.begin("setup")
        with nc.Block() as block:
            @block.sync
            def _(sp):
                for n, (dst, src) in enumerate((
                        (K.const[:, :], const), (K.vec[:, :], vec), (K.early[:, 0:K.n0], early),
                        (K.wg[:, :], wgT), (K.small[:, :], small))):
                    sp.dma_start(dst, src).then_inc(*K.m.done("weights", n, n=16))
                sp.wait_ge(*K.m.since("weights", 4))

            @block.scalar
            def _(act):
                act.dma_start(K.q[:, 0:2, :].rearrange("p a t -> p (a t)"), headsel).then_inc(
                    *K.m.done("selectors", 0, n=16))
                act.dma_start(K.k[0:48, 0:3, :].rearrange("p a t -> p (a t)"), leafsel).then_inc(
                    *K.m.done("selectors", 1, n=16))

            @block.vector
            def _(dve):
                dve.memset(K.zeros[:, :], 0.0).then_inc(*K.m.done("setup", "zeros"))
                dve.memset(K.shift[:, :, :], 0.0).then_inc(*K.m.done("setup", "shift"))
                dve.wait_ge(*K.m.since("selectors", 1))
                dve.tensor_copy(K.headsel[:, :, :], K.q[:, 0:2, :].rearrange("p a (h m) -> p (a h) m", m=P)).then_inc(
                    *K.m.done("setup", "headsel"))
                dve.tensor_copy(K.leafsel[:, :, :], K.k[0:48, 0:3, :].rearrange("p a (h m) -> p (a h) m", m=P)
                                ).then_inc(*K.m.done("setup", "leafsel"))
                dve.wait_ge(*K.m.since("weights", 4))
                for name in TO_BF16:
                    dve.tensor_copy(K.B(name), K.C(name)).then_inc(*K.m.done("setup", name))
                dve.wait_ge(*K.m.since("setup", TO_BF16[-1]))
                selectors_dve(K, dve)

            @block.gpsimd
            def _(pool):
                pool.memset(K.v[:, :, :, :], 0.0).then_inc(*K.m.done("padding", 0))
                pool.wait_ge(*K.m.since("padding", 0))
        clear()

        with nc.Fori(0, PASSES) as i:
            K.begin("first")
            with nc.Block() as block:
                @block.tensor
                def _(pe):
                    layer0_pe(K, pe)

                @block.sync
                def _(sp):
                    sp.dma_start(K.xw[:, :], xT[:, bass.ds(i * PASS, PASS)]).then_inc(
                        *K.m.done("x_loaded", 0, n=16))
                    sp.dma_start(K.ctx[:, :], ctxT[:, bass.ds(i * PASS, PASS)]).then_inc(
                        *K.m.done("ctx_loaded", 0, n=16))
                    sp.wait_ge(*K.ro.freed("wp_cross", 1))
                    sp.dma_start(x_kept[:, bass.ds(i * PASS, PASS)], K.xw[:, :]).then_inc(
                        *K.m.done("x_stored", 0, n=16))
                    sp.wait_ge(*K.rv.freed("l2", "c", 1))
                    sp.dma_start(xn_kept[:, bass.ds(i * PASS, PASS)], K.xn[:, :]).then_inc(
                        *K.m.done("xn_stored", 0, n=16))
                    sp.wait_ge(*K.m.since("x_stored", 0))
                    sp.wait_ge(*K.m.since("xn_stored", 0))

                @block.scalar
                def _(act):
                    layer0_act(K, act)

                @block.vector
                def _(dve):
                    layer0_dve(K, dve, i)
            clear()

        K.begin("router")
        with nc.Block() as block:
            @block.tensor
            def _(pe):
                router_pe(K, pe)

            @block.scalar
            def _(act):
                router_act(K, act)

            @block.vector
            def _(dve):
                router_dve(K, dve)

            @block.sync
            def _(sp):
                sp.dma_start(K.late[:, :], late).then_inc(*K.m.done("later_loaded", 0, n=16))
                sp.wait_ge(*K.m.since("later_loaded", 0))
        clear()
        K.bands = band_ring(K.early)

        with nc.Fori(0, PASSES) as i:
            K.begin("second")
            with nc.Block() as block:
                @block.tensor
                def _(pe):
                    layer1_pe(K, pe)

                @block.sync
                def _(sp):
                    sp.dma_start(K.xn[:, :], xn_kept[:, bass.ds(i * PASS, PASS)]).then_inc(
                        *K.m.done("xn_loaded", 0, n=16))
                    for e in range(EXPERTS):
                        at = slice(2 * HID * e, 2 * HID * (e + 1))
                        sp.dma_start(K.early[:, at], moe[:, at]).then_inc(*K.m.done(f"expert{e}_loaded", 0, n=16))
                    sp.dma_start(K.xw[:, :], x_kept[:, bass.ds(i * PASS, PASS)]).then_inc(
                        *K.m.done("x_loaded", 0, n=16))
                    sp.wait_ge(*K.ro.full("moe", 1))
                    sp.dma_start(K.ctx[:, :], ctxT[:, bass.ds(i * PASS, PASS)]).then_inc(
                        *K.m.done("ctx_loaded", 0, n=16))
                    sp.wait_ge(*K.ra.full("a2", "t", PB - 1, HEADS - 1))
                    sp.dma_start(K.early[:, 0:K.nf], feed).then_inc(*K.m.done("feed_loaded", 0, n=16))
                    sp.wait_ge(*K.rv.freed("fo", PB - 1))
                    sp.dma_start(out[:, bass.ds(i * PASS, PASS)], K.xw[:, :]).then_inc(
                        *K.m.done("stored", 0, n=16))
                    sp.wait_ge(*K.m.since("stored", 0))
                    sp.wait_ge(*K.m.since("ctx_loaded", 0))

                @block.scalar
                def _(act):
                    layer1_act(K, act)

                @block.vector
                def _(dve):
                    layer1_dve(K, dve)

                @block.gpsimd
                def _(pool):
                    layer1_pool(K, pool, i)
            clear()
        return marks.found


KINDS = ["rv_filled", "rv_freed", "ro_filled", "ro_freed", "ra_filled", "ra_freed", "squared", "rstd", "affine",
         "rounded", "rotated", "coarse", "fine", "banded_v", "banded_p", "later_loaded", "value", "joined", "negated", "kept", "recip", "divided", "summed", "weights", "selectors",
         "setup", "padding", "x_loaded", "ctx_loaded", "gate", "gate_exp", "x_stored",
         "xn_stored", "xn_loaded", "feed_loaded", "restored", "hidden_used", "elu", "elu_part", "zsum", "z", "tree", "hid_used", "fmax", "fexp",
         "frecip", "fnorm", "stored"] + [f"expert{e}_loaded" for e in range(EXPERTS)]


def sem_number(s):
    return s.num



def _layout(a):
    import numpy as np
    f = {n: np.asarray(v) for n, v in a.items()}

    def rows(m, r=P):
        m = np.asarray(m, np.float32) if m.dtype != np.float32 else m
        out = np.zeros((r, m.shape[1]), np.float32)
        out[:m.shape[0]] = m
        return out

    def pad_in(w):
        out = np.zeros((HEADS, 32, w.shape[1]), np.float32)
        out[:, 0:8] = w.reshape(HEADS, 8, w.shape[1])
        return out.reshape(4, P, w.shape[1]).transpose(1, 0, 2).reshape(P, -1)

    def swap(w):
        return w.reshape(w.shape[0], -1, 2)[:, :, ::-1].reshape(w.shape)

    def fold(w):
        return w.reshape(-1, P, w.shape[1]).transpose(1, 0, 2).reshape(P, -1)

    def cols(v):
        return v.reshape(-1, P).T

    def heads(w):
        return w.transpose(1, 0, 2).reshape(w.shape[1], -1)

    vec = np.zeros((P, NVEC), np.float32)

    def put(name, m):
        at, n = VCOL[name]
        assert m.shape[1] == n
        vec[:m.shape[0], at:at + n] = m
    for name, key in (("x_bq", "bq"), ("x_bk", "bk"), ("x_bcq", "bcq"), ("x_bck", "bck")):
        put(name, cols(f["L0_xattn_" + key]))
    put("x_bp", cols(f["L0_xattn_bp"]))
    put("moe_b1", cols(f["L0_ffn_b1"]))
    for name, key in (("n1_g", "norm1_g"), ("n1_b", "norm1_b"), ("proj_b", "proj_b"), ("n2_g", "norm2_g"),
                      ("n2_b", "norm2_b"), ("fc1_b", "fc1_b"), ("fc2_b", "fc2_b")):
        put(name, cols(f["L1_attn_" + key]))
    for name in ("ln1_g", "ln1_b", "ln2_g", "ln2_b"):
        put(name, cols(f["L1_xattn_" + name]))
    for b in ("a1", "a2"):
        for name in ("lnx_g", "lnx_b", "lny_g", "lny_b", "li1_b", "ln3_g", "ln3_b", "li2_b", "li3_b"):
            v = f[f"L1_xattn_{b}_{name}"]
            put(f"{b}_{name}", cols(v) if v.size >= P else v.reshape(-1, 1))
    put("f_b1", np.concatenate([cols(f[f"L1_ffn_{r}_b1"]) for r in "qkv"], 1))
    vec[:, VCOL["eps"][0]] = EPS

    eye = np.eye(P, dtype=np.float32)
    i = np.arange(P)
    page = np.where(i[None] // 32 <= i[:, None] // 32, 0.0, MASKED).astype(np.float32)
    causal = np.where(i[None] <= i[:, None], 0.0, MASKED).astype(np.float32)
    consts = {"ident": eye, "center": eye - 1.0 / P, "mean": np.full((P, P), 1.0 / P),
              "center64": rows((np.eye(64) - 1.0 / 64).astype(np.float32)),
              "mean64": rows(np.full((64, 64), 1 / 64, np.float32)), "ones": np.ones((P, P)),
              "page": page, "pageT": page.T, "causal": causal, "causalT": causal.T,
              "upper": (i[:, None] > i[None]).astype(np.float32),
              "before": (i[:, None] < i[None]).astype(np.float32),
              "blocks": (i[:, None] // 8 == i[None] // 8).astype(np.float32),
              "headrows": (i[:, None] // 32 == np.arange(4)[None]).astype(np.float32),
              "prio": np.broadcast_to(8.0 - np.arange(8), (P, 8))}
    const = np.concatenate([np.asarray(consts[n], np.float32) for n, _ in CONSTS], 1)

    inv = 1.0 / 10000.0 ** (np.arange(0, 8, 2, dtype=np.float32) / 8)
    ang = np.outer(np.arange(SEQ, dtype=np.float32), inv.astype(np.float32))
    cos, sin = np.zeros((HEADS, 8, SEQ), np.float32), np.zeros((HEADS, 8, SEQ), np.float32)
    for d in range(8):
        cos[:, d] = np.cos(ang[:, d // 2]).astype(np.float32)
        sin[:, d] = (np.sin(ang[:, d // 2]) * (-1.0 if d % 2 == 0 else 1.0)).astype(np.float32)
    cos, sin = cos.reshape(P, SEQ), sin.reshape(P, SEQ)
    l0 = {"wq": f["L0_attn_wq"], "wqs": swap(f["L0_attn_wq"]), "w_down": f["L0_attn_w_down"],
          "wk": f["L0_attn_wk_up"], "wks": swap(f["L0_attn_wk_up"]), "wv": f["L0_attn_wv_up"],
          "wo": pad_in(f["L0_attn_wo"]), "xq": f["L0_xattn_Wq"], "xk": f["L0_xattn_Wk"],
          "xv": f["L0_xattn_Wv"], "cq": f["L0_xattn_Wcq"], "ck": f["L0_xattn_Wck"],
          "cv": f["L0_xattn_Wcv"], "wp": pad_in(f["L0_xattn_Wp"]), "cos": cos,
          "sin": sin, "bv": np.broadcast_to(f["L0_xattn_bv"], (P, P)),
          "bcv": np.broadcast_to(f["L0_xattn_bcv"], (P, P))}
    early = np.concatenate([rows(l0[n]) for n, _ in LAYER0], 1)
    moe = np.concatenate([np.concatenate([f["L0_ffn_W1"][e], fold(f["L0_ffn_W2"][e])], 1)
                          for e in range(EXPERTS)], 1)
    l1 = {"qkv": f["L1_attn_qkv_w"].T, "proj": f["L1_attn_proj_w"].T, "fc1": f["L1_attn_fc1_w"].T,
          "fc2": fold(f["L1_attn_fc2_w"].T)}
    for b in ("a1", "a2"):
        for w in "qkv":
            l1[f"{b}_{w}"] = heads(f[f"L1_xattn_{b}_w{w}"])
        l1[f"{b}_li1"] = fold(f[f"L1_xattn_{b}_li1_w"])
        l1[f"{b}_li2"] = f[f"L1_xattn_{b}_li2_w"]
        l1[f"{b}_li3"] = fold(f[f"L1_xattn_{b}_li3_w"])
    feed = np.concatenate([f[f"L1_ffn_{r}_w1"].transpose(1, 0, 2).reshape(P, -1) for r in "qkv"]
                          + [fold(f[f"L1_ffn_{r}_w2"].reshape(-1, P)) for r in "qkv"], 1)
    l1["nodes"] = np.concatenate([f[f"L1_ffn_{r}_node_w"].T for r in "qkv"], 1)
    l1["node_b"] = np.broadcast_to(np.concatenate([f[f"L1_ffn_{r}_node_b"] for r in "qkv"]), (P, 45))
    late = np.concatenate([rows(l1[n]) for n, _ in LAYER1], 1)

    headsel = np.zeros((P, HEADS, P), np.float32)
    for h in range(HEADS):
        headsel[h, h] = 1.0
    leafsel = np.zeros((48, 24, P), np.float32)
    for r in range(3):
        for leaf in range(LEAVES):
            leafsel[16 * r + leaf, 8 * r + leaf // 2, 64 * (leaf % 2):64 * (leaf % 2) + 64] = OFF
    small = np.zeros((48, 12 * P), np.float32)
    for n, r in enumerate("qkv"):
        small[16 * n:16 * n + 16, n * P:(n + 1) * P] = f[f"L1_ffn_{r}_b2"]
    for e in range(EXPERTS):
        small[e, (3 + e) * P:(4 + e) * P] = 1.0
    small[0:EXPERTS, 11 * P:] = f["L0_ffn_b2"]
    return {"xT": f["x"].reshape(TOKENS, P).T, "ctxT": f["ctx_512"].reshape(TOKENS, CTX).T, "vec": vec,
            "const": const, "early": early, "moe": moe, "feed": feed, "late": late, "wgT": f["L0_ffn_Wg"].T,
            "headsel": headsel.reshape(P, -1), "leafsel": leafsel.reshape(48, -1), "small": small}


def kernel(**inputs):
    import numpy as _np
    import concourse.bacc as _bacc
    from concourse import mybir as _mybir
    from concourse.bass_utils import run_bass_kernel_spmd as _run

    laid = {n: _np.ascontiguousarray(v) for n, v in _layout(inputs).items()}
    known = None
    for _ in range(2):
        nc = _bacc.Bacc("TRN2", target_bir_lowering=False, num_devices=1)
        args = [nc.dram_tensor(f"in_{n}", v.shape, _mybir.dt.from_np(v.dtype), kind="ExternalInput").ap()
                for n, v in laid.items()]
        args.append(nc.dram_tensor("out_0", (P, TOKENS), F32, kind="ExternalOutput").ap())
        known = build(nc, known, args)
    r = _run(nc, [{f"in_{n}": v for n, v in laid.items()}], core_ids=[0])
    return r.results[0]["out_0"].T.reshape(BATCH, SEQ, P)
```

```python
from contextlib import ExitStack

import concourse.bass as bass
from concourse import mybir

F32 = mybir.dt.float32
BF16 = mybir.dt.bfloat16
ACT = mybir.ActivationFunctionType
ALU = mybir.AluOpType
AX = mybir.AxisListType

P = 128
BATCH, SEQ, CTX = 8, 256, 64
TOKENS = BATCH * SEQ
HALF = 512
PASS = 1024
PASSES = TOKENS // PASS
HALVES = PASS // HALF
PB = PASS // SEQ
TILES = PASS // P
HEADS, GROUPS = 16, 4
EXPERTS, HID = 8, 512
CAPACITY = int(round(2 * TOKENS * 1.05 / EXPERTS))
LEAVES, NODES, LEAF = 16, 15, 64
EPS = 1e-5
MASKED = -1e30
OFF = 1e30


class Marks:

    def __init__(self, nc, ctx, known):
        self.nc, self.ctx, self.known = nc, ctx, known
        self.sems, self.count, self.where = {}, {}, "start"
        self.found = {}

    def sem(self, kind):
        if kind not in self.sems:
            self.sems[kind] = self.ctx.enter_context(self.nc.semaphore(kind))
        return self.sems[kind]

    def begin(self, where):
        self.where, self.count = where, {}

    def done(self, kind, *key, n=1):
        self.count[kind] = self.count.get(kind, 0) + n
        name = (self.where, kind) + key
        assert name not in self.found, name
        self.found[name] = self.count[kind]
        return self.sem(kind), n

    def since(self, kind, *key):
        name = (self.where, kind) + key
        if self.known is None:
            return self.sem(kind), 1
        return self.sem(kind), self.known[name]


class Ring:

    def __init__(self, marks, name, banks, shared=False):
        self.marks, self.name, self.banks, self.shared = marks, name, banks, shared
        self.claimed, self.order = {}, []
        self.freed_count = 0

    def begin(self):
        self.claimed, self.freed_count = {}, 0

    def claim(self, *key):
        assert key not in self.claimed, key
        self.claimed[key] = len(self.claimed)
        return self.bank(*key)

    def bank(self, *key):
        n = len(self.banks)
        return self.banks[self.claimed[key] % n]

    def pair(self, key):
        assert self.claimed[key] % 2 == 0
        return self.claimed[key] % len(self.banks)

    def reused(self, *key):
        return self.claimed[key] >= len(self.banks)

    def room(self, *key):
        return self.marks.sem(self.name + "_freed"), self.claimed[key] - len(self.banks) + 1

    def fill(self, *key):
        return self.marks.sem(self.name + "_filled"), 1

    def full(self, *key):
        return self.marks.sem(self.name + "_filled"), self.claimed[key] + 1

    def free(self, *keys):
        for key in keys:
            assert self.shared or self.claimed[key] == self.freed_count, (self.name, key)
            self.freed_count += 1
        return self.marks.sem(self.name + "_freed"), len(keys)

    def freed(self, *key):
        return self.marks.sem(self.name + "_freed"), self.claimed[key] + 1


VECTORS = [
    ("x_bq", 1), ("x_bk", 1), ("x_bcq", 1), ("x_bck", 1), ("x_bp", 1),
    ("moe_b1", 32),
    ("n1_g", 1), ("n1_b", 1), ("proj_b", 1), ("n2_g", 1), ("n2_b", 1), ("fc1_b", 4), ("fc2_b", 1),
    ("ln1_g", 1), ("ln1_b", 1), ("ln2_g", 1), ("ln2_b", 1),
] + [(f"{a}_{v}", n) for a in ("a1", "a2") for v, n in (
    ("lnx_g", 1), ("lnx_b", 1), ("lny_g", 1), ("lny_b", 1), ("li1_b", 1), ("ln3_g", 1), ("ln3_b", 1),
    ("li2_b", 4), ("li3_b", 1))] + [("f_b1", 24), ("eps", 1), ("max_row", 1)]
VCOL, _at = {}, 0
for _name, _n in VECTORS:
    VCOL[_name] = (_at, _n)
    _at += _n
NVEC = _at

CONSTS = [("ident", 128), ("center", 128), ("mean", 128), ("center64", 64), ("mean64", 64), ("ones", 128),
          ("page", 128), ("pageT", 128), ("causal", 128), ("causalT", 128), ("upper", 128),
          ("before", 128), ("blocks", 128), ("prio", 8), ("headrows", 4), ("own8", 128)]
TO_BF16 = ["ident", "page", "pageT", "causal", "causalT", "before", "ones"]
LAYER0 = [("wq", 128), ("wqs", 128), ("w_down", 64), ("wk", 128), ("wks", 128), ("wv", 128), ("wo", 128),
          ("xq", 128), ("xk", 128), ("xv", 128), ("cq", 128), ("ck", 128), ("cv", 128), ("wp", 128),
          ("cos", 256), ("sin", 256), ("bv", 128), ("bcv", 128)]
MOE = [("experts", EXPERTS * 2 * HID)]
FEED = [("f_w1", 3072), ("f_w2", 3072)]
LAYER1 = [("qkv", 384), ("proj", 128), ("fc1", 512), ("fc2", 512)] + [
    (f"{a}_{w}", 512) for a in ("a1", "a2") for w in ("q", "k", "v", "li1", "li2", "li3")] + [
    ("nodes", 45), ("node_b", 45)]


def columns(parts):
    at, out = 0, {}
    for name, n in parts:
        out[name] = (at, n)
        at += n
    return out, at


class Chip:

    def __init__(self, nc, ctx, marks):
        def sb(name, shape, dt=F32):
            return ctx.enter_context(nc.sbuf_tensor(name, shape, dt))
        self.m = marks
        self.vec = sb("vec", [P, NVEC])
        self.ccol, n = columns(CONSTS)
        self.const = sb("const", [P, n])
        self.bcol, n = columns([(x, P) for x in TO_BF16])
        self.bf = sb("bf", [P, n], BF16)
        self.l0col, n0 = columns(LAYER0)
        self.mcol, nm = columns(MOE)
        self.fcol, nf = columns(FEED)
        self.early = sb("early", [P, max(n0, nm)])
        self.l1col, n1 = columns(LAYER1)
        self.late = sb("late", [P, n1])
        self.n0, self.nm, self.n1, self.nf = n0, nm, n1, nf
        self.headsel = sb("headsel", [P, HEADS, P], BF16)
        self.leafsel = sb("leafsel", [48, 24, P], BF16)
        self.small = sb("small", [48, 3 * P + P])
        self.expertsel = sb("expertsel", [P, EXPERTS, P], BF16)
        self.logits = sb("logits", [P, TOKENS // P, EXPERTS])
        self.weight = sb("weight", [P, TOKENS // P, EXPERTS])
        self.weight_now = sb("weight_now", [P, TILES, EXPERTS])
        self.xw = sb("xw", [P, PASS])
        self.ctx = sb("ctx", [CTX, PASS])
        self.xn = sb("xn", [P, PASS])
        self.sq = sb("sq", [P, PASS])
        self.ya = sb("ya", [P, PASS])
        self.yb = sb("yb", [P, PASS])
        self.yc = sb("yc", [P, PASS])
        self.q = sb("q", [P, GROUPS, PASS])
        self.k = sb("k", [P, GROUPS, PASS])
        both = sb("rounded_qk", [P, 2 * GROUPS, PASS], BF16)
        self.qb, self.kb = both[:, 0:GROUPS, :], both[:, GROUPS:, :]
        self.sq_beside = both[:, 0:2, :].rearrange("p g t -> p (g t)").bitcast(F32)
        self.stack = {"k": both, "q": self.k.rearrange("p g t -> p (g t)").bitcast(BF16).rearrange(
            "p (n t) -> p n t", t=PASS)}
        self.sel = self.late[:, 0:6 * 8 * P // 2].bitcast(BF16).rearrange("p (x n m) -> p x n m", x=6, m=P)
        self.part = self.late[:, 3 * PASS:6 * PASS].bitcast(BF16).rearrange("p (x t) -> p x t", t=PASS)
        self.swapped = self.late[:, 6 * PASS:7 * PASS]
        self.v = sb("v", [P, TILES, HEADS, 32])
        self.prob = sb("prob", [P, 4, 2, HALF])
        self.kept = sb("kept", [P, 2, 2, 2, P])
        self.both = self.early[:, 6 * PASS:8 * PASS].rearrange("p (n j t) -> p n j t", n=2, j=4)
        self.maxes = sb("maxes", [P, 2, HEADS, 3])
        self.negmax = sb("negmax", [P, 2, 2, HEADS])
        self.shift = sb("shift", [P, 2, SEQ], BF16)
        self.weighed = sb("weighed", [P, 2, 2 * SEQ])
        self.recip = self.weighed[:, :, SEQ:]
        self.gate = self.q[:, 0:2, :].rearrange("p a t -> p (a t)")[:, 0:12 * P].rearrange(
            "p (a n e) -> p a n e", a=12, e=EXPERTS)
        self.gcol = sb("gcol", [P, 8, 16])
        self.onehot = sb("onehot", [P, 2, 16, EXPERTS], BF16)
        flat = self.prob.rearrange("p a i t -> p (a i t)")
        self.tree = flat[:, 0:2 * TILES * 48].rearrange("p (a t n) -> p a t n", a=2, n=48)
        self.treeb = flat[:, 2 * TILES * 48:3 * TILES * 48].rearrange("p (t n) -> p t n", n=48)
        self.lt = self.ctx[0:48, :]
        self.lm = self.weighed[0:48, 0, :].bitcast(BF16)
        self.share = self.lt[0:3 * EXPERTS, :]
        self.shareb = self.weighed[0:3 * EXPERTS, 1, :].bitcast(BF16)
        self.levels = self.yb[:, 0:TILES * 3 * EXPERTS].rearrange("p (t e) -> p t e", t=TILES)
        self.rounded = self.yc[:, 0:TILES * EXPERTS // 2].bitcast(BF16).rearrange("p (t e) -> p t e", t=TILES)
        self.stat = sb("stat", [P, 2, 8])
        self.ps = ctx.enter_context(nc.psum_tensor("ps", [P, 8, HALF], F32))
        banks = [self.ps[:, i, :] for i in range(8)]
        self.rv = Ring(marks, "rv", banks[0:2])
        self.ro = Ring(marks, "ro", banks[2:4], shared=True)
        self.ra = Ring(marks, "ra", banks[4:8])
        self.bands = None

    def begin(self, where):
        self.m.begin(where)
        for r in (self.rv, self.ro, self.ra):
            r.begin()

    def C(self, name, rows=P):
        a, n = self.ccol[name]
        return self.const[0:rows, a:a + n]

    def B(self, name):
        a, n = self.bcol[name]
        return self.bf[:, a:a + n]

    def W0(self, name, rows=P):
        a, n = self.l0col[name]
        return self.early[0:rows, a:a + n]

    def expert(self, e, which, m):
        at = (2 * e + which) * HID + m * P
        return self.early[:, at:at + P]

    def WF(self, name):
        a, n = self.fcol[name]
        return self.early[:, a:a + n]

    def W1(self, name, rows=P):
        a, n = self.l1col[name]
        return self.late[0:rows, a:a + n]

    def V(self, name, i=0, rows=P):
        a = VCOL[name][0]
        return self.vec[0:rows, a + i:a + i + 1]

    def ra_pair(self, *key):
        at = 4 + self.ra.pair(key)
        return self.ps[:, at:at + 2, :]


def half(s):
    return slice(s * HALF, (s + 1) * HALF)


def tile(t):
    return slice(t * P, (t + 1) * P)


def seq(b):
    return slice(b * SEQ, (b + 1) * SEQ)



def norm_room(K, name):
    return (K.ro, K.sq_beside) if name == "a2y" else (K.rv, K.sq)


def center_pe(K, pe, name, src, ready, rows=P):
    ring, _ = norm_room(K, name)
    for s in range(HALVES):
        bank = ring.claim(name, "c", s)
        for w in ready(s):
            pe.wait_ge(*w)
        if ring.reused(name, "c", s):
            pe.wait_ge(*ring.room(name, "c", s))
        pe.matmul(bank[0:rows, :], K.C("center" if rows == P else "center64", rows), src[0:rows, half(s)],
                  start=True, stop=True).then_inc(*ring.fill(name, "c", s))


def variance_pe(K, pe, name, rows=P):
    _, squares = norm_room(K, name)
    for s in range(HALVES):
        bank = K.ra.claim(name, "v", s)
        pe.wait_ge(*K.m.since("squared", name, s))
        if K.ra.reused(name, "v", s):
            pe.wait_ge(*K.ra.room(name, "v", s))
        pe.matmul(bank[0:rows, :], K.C("mean" if rows == P else "mean64", rows), squares[0:rows, half(s)],
                  start=True, stop=True).then_inc(*K.ra.fill(name, "v", s))


def norm_pe(K, pe, name, src, ready, rows=P):
    center_pe(K, pe, name, src, ready, rows)
    variance_pe(K, pe, name, rows)


def both_tables(act):
    act.preload_act_table_set("natural_log_exp_and_others")


def squares_act(K, act, name, rows=P):
    ring, squares = norm_room(K, name)
    for s in range(HALVES):
        act.wait_ge(*ring.full(name, "c", s))
        act.activation(squares[0:rows, half(s)], ring.bank(name, "c", s)[0:rows, :], ACT.Square).then_inc(
            *K.m.done("squared", name, s))


def rstd_act(K, act, name, rows=P):
    _, rstd = norm_room(K, name)
    for s in range(HALVES):
        act.wait_ge(*K.ra.full(name, "v", s))
        act.activation(rstd[0:rows, half(s)], K.ra.bank(name, "v", s)[0:rows, :], ACT.Ln,
                       bias=K.V("eps", rows=rows)).then_inc(*K.ra.free((name, "v", s)))
        act.wait_ge(*K.ra.freed(name, "v", s))
        act.activation(rstd[0:rows, half(s)], rstd[0:rows, half(s)], ACT.Exp, scale=-0.5).then_inc(
            *K.m.done("rstd", name, s))


def norm_act(K, act, name, rows=P):
    squares_act(K, act, name, rows)
    rstd_act(K, act, name, rows)


def norm_dve(K, dve, name, dst, affine=None, second=None, rows=P):
    ring, rstd = norm_room(K, name)
    for s in range(HALVES):
        dve.wait_ge(*K.m.since("rstd", name, s))
        dve.tensor_tensor(dst[0:rows, half(s)], ring.bank(name, "c", s)[0:rows, :], rstd[0:rows, half(s)],
                          ALU.mult).then_inc(*ring.free((name, "c", s)))
        if second:
            other, g, b = second
            dve.wait_ge(*ring.freed(name, "c", s))
            dve.tensor_scalar(other[0:rows, half(s)], dst[0:rows, half(s)], K.V(g, rows=rows), K.V(b, rows=rows),
                              ALU.mult, ALU.add).then_inc(*K.m.done("affine", name, "second", s))
            dve.wait_ge(*K.m.since("affine", name, "second", s))
        if affine:
            g, b = affine
            dve.wait_ge(*ring.freed(name, "c", s))
            dve.tensor_scalar(dst[0:rows, half(s)], dst[0:rows, half(s)], K.V(g, rows=rows), K.V(b, rows=rows),
                              ALU.mult, ALU.add).then_inc(*K.m.done("affine", name, s))


def normed(K, name):
    return lambda s: [K.rv.freed(name, "c", s)]


def affined(K, name):
    return lambda s: [K.m.since("affine", name, s)]



def project_pe(K, pe, name, weights, src, ready, rows=P, outs=P):
    for g, w in enumerate(weights):
        for s in range(HALVES):
            bank = K.ra.claim(name, g, s)
            if g == 0:
                for x in ready(s):
                    pe.wait_ge(*x)
            if K.ra.reused(name, g, s):
                pe.wait_ge(*K.ra.room(name, g, s))
            pe.matmul(bank[0:outs, :], w, src[0:rows, half(s)], start=True, stop=True).then_inc(
                *K.ra.fill(name, g, s))


def project_act(K, act, name, count, dst, func, bias=None, after=None, outs=P):
    for g in range(count):
        if after:
            for w in after(g):
                act.wait_ge(*w)
        act.wait_ge(*K.ra.full(name, g, 1))
        pair = K.ra_pair(name, g, 0)
        act.activation(dst(g)[0:outs].rearrange("p (s t) -> p s t", s=HALVES), pair[0:outs], func,
                       bias=bias(g) if bias else 0.0).then_inc(*K.ra.free((name, g, 0), (name, g, 1)))


def projected(K, name, g):
    return [K.ra.freed(name, g, 1)]



def project_half_pe(K, pe, name, weights, src, ready, s, groups=range(GROUPS), rows=P):
    for g in groups:
        bank = K.ra.claim(name, g, s)
        for x in ready(s) if g == 0 else []:
            pe.wait_ge(*x)
        if K.ra.reused(name, g, s):
            pe.wait_ge(*K.ra.room(name, g, s))
        pe.matmul(bank, weights[g], src[0:rows, half(s)], start=True, stop=True).then_inc(*K.ra.fill(name, g, s))


def project_half_act(K, act, name, dst, s, groups=range(GROUPS)):
    for g in groups:
        act.wait_ge(*K.ra.full(name, g, s))
        act.activation(dst[:, g, half(s)], K.ra.bank(name, g, s), ACT.Copy).then_inc(*K.ra.free((name, g, s)))


def round_half_dve(K, dve, name, src, dst, s, groups=range(GROUPS)):
    for g in groups:
        dve.wait_ge(*K.ra.freed(name, g, s))
        dve.tensor_copy(dst[:, g, half(s)], src[:, g, half(s)]).then_inc(*K.m.done("rounded", name, g, s))


def round_dve(K, dve, name, src, dst):
    for g in range(GROUPS):
        dve.wait_ge(*K.ra.freed(name, g, 1))
        dve.tensor_copy(dst[:, g, :], src[:, g, :]).then_inc(*K.m.done("rounded", name, g))



def rope_pe(K, pe, name, w, ws, src, ready, rows, halves):
    for s in halves:
        for part, mat in (("plain", w), ("swapped", ws)):
            bank = K.rv.claim(name, s, part)
            if part == "plain":
                for x in ready(s):
                    pe.wait_ge(*x)
            if K.rv.reused(name, s, part):
                pe.wait_ge(*K.rv.room(name, s, part))
            pe.matmul(bank, mat, src[0:rows, half(s)], start=True, stop=True).then_inc(*K.rv.fill(name, s, part))


def rope_dve(K, dve, name, dst, product, halves):
    cos = K.W0("cos").unsqueeze(1).broadcast_to((P, 2, SEQ))
    sin = K.W0("sin").unsqueeze(1).broadcast_to((P, 2, SEQ))
    for s in halves:
        out = dst[:, half(s)].rearrange("p (b t) -> p b t", b=2)
        tmp = product[:, half(s)].rearrange("p (b t) -> p b t", b=2)
        dve.wait_ge(*K.rv.full(name, s, "plain"))
        dve.tensor_tensor(out, K.rv.bank(name, s, "plain").rearrange("p (b t) -> p b t", b=2), cos,
                          ALU.mult).then_inc(*K.rv.free((name, s, "plain")))
        dve.wait_ge(*K.rv.full(name, s, "swapped"))
        dve.tensor_tensor(tmp, K.rv.bank(name, s, "swapped").rearrange("p (b t) -> p b t", b=2), sin,
                          ALU.mult).then_inc(*K.rv.free((name, s, "swapped")))
        dve.wait_ge(*K.rv.freed(name, s, "swapped"))
        dve.tensor_tensor(out, out, tmp, ALU.add).then_inc(*K.m.done("rotated", name, s))



MAX_ROW = 48
LEVELS = {"q": (0, 0, 1, 1, 0, 2), "k": (0, 1, 0, 1, 2, 0)}


def selectors_dve(K, dve):
    dve.wait_ge(*K.m.since("setup", "sel"))
    ident = K.B("ident").rearrange("k (n i d) -> k n i d", i=2, d=8)
    for x, t in enumerate("qk"):
        for c, level in enumerate(LEVELS[t]):
            rows = K.sel[:, 3 * x + level, :, :].rearrange("k n (i m) -> k n i m", i=2)
            dve.tensor_copy(rows[:, :, :, 8 * c:8 * c + 8], ident).then_inc(*K.m.done("setup", "sel", t, c))
    dve.wait_ge(*K.m.since("setup", "sel", "k", 5))


def level(K, t, n):
    return K.part[:, 3 * "qk".index(t) + n, :]


def split_act(K, act, name, ready):
    for s in range(HALVES):
        for t, src in (("q", K.ya), ("k", K.yb)):
            for w in ready(t, s):
                act.wait_ge(*w)
            act.activation(level(K, t, 0)[:, half(s)], src[:, half(s)], ACT.Copy).then_inc(
                *K.m.done("coarse", name, t, 0, s))
        for t, src in (("q", K.ya), ("k", K.yb)):
            act.wait_ge(*K.m.since("fine", name, t, 1, s))
            act.activation(level(K, t, 1)[:, half(s)], src[:, half(s)], ACT.Copy).then_inc(
                *K.m.done("coarse", name, t, 1, s))


def split_dve(K, dve, name, s):
    for n, out in ((0, None), (1, 2)):
        for t, src in (("q", K.ya), ("k", K.yb)):
            dve.wait_ge(*K.m.since("coarse", name, t, n, s))
            to = src if out is None else level(K, t, out)
            dve.tensor_tensor(to[:, half(s)], src[:, half(s)], level(K, t, n)[:, half(s)], ALU.subtract).then_inc(
                *K.m.done("fine", name, t, n + 1, s))


SLOTS = [(t, n) for t in "qk" for n in range(HEADS // 2)]


def stack_pe(K, pe, name, s, slots=SLOTS):
    for t, n in slots:
        bank = K.ra.claim(name, s, t, n)
        if n == 0:
            pe.wait_ge(*K.m.since("coarse", name, t, 1, s))
            pe.wait_ge(*K.m.since("fine", name, t, 2, s))
        if K.ra.reused(name, s, t, n):
            pe.wait_ge(*K.ra.room(name, s, t, n))
        for i in range(3):
            mm = pe.matmul(bank, K.sel[:, 3 * "qk".index(t) + i, n, :], level(K, t, i)[:, half(s)], start=(i == 0),
                           stop=(i == 2))
        mm.then_inc(*K.ra.fill(name, s, t, n))


def stack_act(K, act, name):
    for s in range(HALVES):
        for t, n in SLOTS:
            act.wait_ge(*K.ra.full(name, s, t, n))
            act.activation(K.stack[t][:, n, half(s)], K.ra.bank(name, s, t, n), ACT.Identity,
                           bias=K.V("max_row") if t == "k" else 0.0).then_inc(*K.ra.free((name, s, t, n)))


def stacked(K, name):
    return lambda b, g: [K.ra.freed(name, b // 2, *SLOTS[-1])] if b % 2 == 0 and g == 0 else []


def max_rows_sp(K, sp, name):
    for b in range(PB):
        sp.wait_ge(*K.rv.freed(name, "m", b))
        for i in range(2):
            row = 64 * i + MAX_ROW
            sp.dma_start(K.stack["q"][row:row + 1, :, seq(b)], K.shift[i:HEADS:2, b % 2, :]).then_inc(
                *K.m.done("max_rows", name, b, i, n=16))



def values_pe(K, pe, name, w, src, ready, rows, wide, tiles=range(TILES)):
    if wide:
        for t in tiles:
            bank = K.ra.claim(name, "v", t)
            for x in ready(t // 4):
                pe.wait_ge(*x)
            if K.ra.reused(name, "v", t):
                pe.wait_ge(*K.ra.room(name, "v", t))
            pe.matmul(bank, src[0:rows, tile(t)], w, start=True, stop=True).then_inc(*K.ra.fill(name, "v", t))
        return
    for s in range(HALVES):
        bank = K.rv.claim(name, "v", s)
        for x in ready(s):
            pe.wait_ge(*x)
        if K.rv.reused(name, "v", s):
            pe.wait_ge(*K.rv.room(name, "v", s))
        for i in range(4):
            mm = pe.matmul(bank[:, tile(i)], src[0:rows, tile(4 * s + i)], w, start=True, stop=True)
        mm.then_inc(*K.rv.fill(name, "v", s))


def values_act(K, act, name, tiles=range(0, TILES, 2)):
    for t in tiles:
        act.wait_ge(*K.ra.full(name, "v", t + 1))
        act.activation(K.v[:, t:t + 2, :, :].rearrange("p a h d -> p a (h d)"), K.ra_pair(name, "v", t),
                       ACT.Copy).then_inc(*K.ra.free((name, "v", t), (name, "v", t + 1)))


def values_dve(K, dve, name, bias):
    for s in range(HALVES):
        src = K.rv.bank(name, "v", s).rearrange("p (a j g d) -> p a j g d", a=4, j=4, d=8)
        out = K.v[:, 4 * s:4 * s + 4, :, :].rearrange("p a (j g) m -> p a j g m", j=4)
        dve.wait_ge(*K.rv.full(name, "v", s))
        for g in range(GROUPS):
            dst = out[:, :, :, g, 8 * g:8 * g + 8]
            if bias is None:
                op = dve.tensor_copy(dst, src[:, :, :, g])
            else:
                add = bias.rearrange("p (j g d) -> p j g d", j=4, d=8)[:, :, g]
                op = dve.tensor_tensor(dst, src[:, :, :, g], add.unsqueeze(1).broadcast_to((P, 4, 4, 8)), ALU.add)
            if g < GROUPS - 1:
                op.then_inc(*K.m.done("value", name, s, g))
        op.then_inc(*K.rv.free((name, "v", s)))



def masked(kind):
    return kind in ("page", "causal")


def head(dims, g, j):
    return 4 * g + j if dims == 32 else 4 * j + g


def operands(K, dims, b, g, j):
    h = head(dims, g, j)
    if dims == 8:
        row = 64 * (h % 2)
        return [K.stack[t][row:row + n, h // 2, seq(b)] for n in (MAX_ROW, MAX_ROW + 1) for t in "qk"]
    rows = slice(32 * j, 32 * j + 32)
    return (K.qb[rows, g, seq(b)], K.kb[rows, g, seq(b)], K.bands[:, (GROUPS * b + g) % BANDS, j, :],
            K.k[:, g, seq(b)])


def scores_pe(K, pe, name, b, g, j, dims, kind, ready):
    h = 4 * g + j
    query, key = operands(K, dims, b, g, j)[0:2]
    bank = K.rv.claim(name, "s", b, h)
    if j == 0:
        for w in ready(b, g):
            pe.wait_ge(*w)
    if K.rv.reused(name, "s", b, h):
        pe.wait_ge(*K.rv.room(name, "s", b, h))
    if masked(kind):
        diagonal = bank.rearrange("p (a k) -> p a k", a=4)[:, 0:3:2, :]
        pe.matmul(diagonal, K.B("ident"), K.B(kind).unsqueeze(1).broadcast_to((P, 2, P)), start=True, stop=False,
                  skip_group_check=True)
        pe.matmul(bank[:, 0:P], query[:, 0:P], key[:, 0:P], start=False, stop=False,
                  skip_group_check=True)
        mm = pe.matmul(bank[:, P:3 * P], query[:, P:], key, start=False, stop=True,
                       skip_group_check=True)
    else:
        pe.matmul(bank[:, 0:SEQ], query[:, 0:P], key, start=True, stop=False,
                  skip_group_check=True)
        mm = pe.matmul(bank[:, SEQ:], query[:, P:], key, start=False, stop=True,
                       skip_group_check=True)
    mm.then_inc(*K.rv.fill(name, "s", b, h))


def maxima_dve(K, dve, name, dims, b, g, j, kind):
    h = 4 * g + j
    n, w = (3, P) if masked(kind) else (2, SEQ)
    src = K.rv.bank(name, "s", b, h)[:, 0:n * w].rearrange("p (a k) -> p a k", a=n)
    dve.wait_ge(*K.rv.full(name, "s", b, h))
    dve.tensor_reduce(K.maxes[:, b % 2, head(dims, g, j), 0:n], src, AX.X, ALU.max).then_inc(
        *K.rv.free((name, "s", b, h)))


def shift_dve(K, dve, name, b, kind):
    m, out = K.maxes[:, b % 2], K.negmax[:, b % 2]
    dve.wait_ge(*K.rv.freed(name, "s", b, HEADS - 1))
    if masked(kind):
        dve.tensor_tensor(m[:, :, 1], m[:, :, 1], m[:, :, 2], ALU.max).then_inc(*K.m.done("joined", name, b))
        dve.wait_ge(*K.m.since("joined", name, b))
    dve.tensor_scalar(out, m[:, :, 0:2].rearrange("p h a -> p a h"), -1.0, None, ALU.mult).then_inc(
        *K.m.done("negated", name, b))


def turn_pe(K, pe, name, b):
    bank = K.rv.claim(name, "m", b)
    pe.wait_ge(*K.m.since("negated", name, b))
    if K.rv.reused(name, "m", b):
        pe.wait_ge(*K.rv.room(name, "m", b))
    for a in range(2):
        mm = pe.transpose(bank[0:HEADS, tile(a)], K.negmax[:, b % 2, a, :], K.C("ident"))
    mm.then_inc(*K.rv.fill(name, "m", b))


def turned_dve(K, dve, name, dims, b):
    dve.wait_ge(*K.rv.full(name, "m", b))
    if b >= 2 and dims == 32:
        dve.wait_ge(*K.ra.full(name, "t", b - 2, HEADS - 1))
    elif b >= 2:
        dve.wait_ge(*K.m.since("max_rows", name, b - 2, 1))
    dve.tensor_copy(K.shift[0:HEADS, b % 2, :], K.rv.bank(name, "m", b)[0:HEADS, 0:SEQ]).then_inc(
        *K.rv.free((name, "m", b)))


BANDS = 4


def band_ring(where):
    return where[:, 0:BANDS * 4 * SEQ].rearrange("p (n j t) -> p n j t", n=BANDS, j=4)


def banded(j):
    return "banded_v" if j < 2 else "banded_p"


def bands(K, eng, name, b, g, heads, ready):
    u = GROUPS * b + g
    for w in ready(b, g):
        eng.wait_ge(*w)
    if u >= BANDS:
        ub, ug = divmod(u - BANDS, GROUPS)
        eng.wait_ge(*K.ra.full(name, "t", ub, 4 * ug + 3))
    for j in heads:
        eng.tensor_scalar(K.bands[:, u % BANDS, j, :], K.q[:, g, seq(b)], K.C("headrows")[:, j:j + 1], None,
                           ALU.mult).then_inc(*K.m.done(banded(j), name, b, g, j))


def exact_pe(K, pe, name, b, g, j, dims, kind, ready):
    h = 4 * g + j
    query, key = operands(K, dims, b, g, j)[2:4]
    bank = K.ra.claim(name, "t", b, h)
    if dims == 32:
        pe.wait_ge(*K.m.since(banded(j), name, b, g, j))
        if h == 0:
            pe.wait_ge(*K.rv.freed(name, "m", b))
    elif h == 0:
        pe.wait_ge(*K.m.since("max_rows", name, b, 1))
    if j == 0:
        for w in ready(b, g):
            pe.wait_ge(*w)
    if K.ra.reused(name, "t", b, h):
        pe.wait_ge(*K.ra.room(name, "t", b, h))
    if dims == 32:
        shift = K.shift[:, b % 2, :].unsqueeze(1).broadcast_to((P, 2, SEQ))
        pe.matmul(bank, K.headsel[:, h, :], shift, start=True, stop=False, skip_group_check=True)
    if masked(kind):
        diagonal = bank.rearrange("p (a k) -> p a k", a=4)[:, 0:3:2, :]
        pe.matmul(diagonal, K.B("ident"), K.B(kind + "T").unsqueeze(1).broadcast_to((P, 2, P)), start=True,
                  stop=False, skip_group_check=True)
        pe.matmul(bank[:, 0:SEQ], key[:, 0:P], query, start=False, stop=False, skip_group_check=True)
        mm = pe.matmul(bank[:, SEQ:3 * P], key[:, P:], query[:, P:], start=False, stop=True,
                       skip_group_check=True)
    else:
        pe.matmul(bank[:, 0:SEQ], key[:, 0:P], query, start=(dims == 8), stop=False, skip_group_check=True)
        mm = pe.matmul(bank[:, SEQ:], key[:, P:], query, start=False, stop=True, skip_group_check=True)
    mm.then_inc(*K.ra.fill(name, "t", b, h))


def slot(b, g, i):
    return (2 * (GROUPS * b + g) + i) % 4


def used(K, name, dims, b, g):
    if dims == 32 or g == GROUPS - 1:
        return K.ro.full(name, "o", (b, g) if dims == 32 else b)
    return K.m.since("weighed", name, b, g)


def exps_act(K, act, name, dims, b, g, kind, scale):
    n = 3 * P if masked(kind) else HALF
    for i in range(2):
        h = 4 * g + 2 * i
        u = GROUPS * b + g
        if u >= 2:
            ub, ug = divmod(u - 2, GROUPS)
            act.wait_ge(*used(K, name, dims, ub, ug))
        act.wait_ge(*K.ra.full(name, "t", b, h + 1))
        act.activation(K.prob[:, slot(b, g, i), :, 0:n], K.ra_pair(name, "t", b, h)[:, :, 0:n], ACT.Exp,
                       scale=scale).then_inc(*K.ra.free((name, "t", b, h), (name, "t", b, h + 1)))


def kept_pool(K, pool, name, b, g):
    u = GROUPS * b + g
    for i in range(2):
        for a in range(2):
            src = K.prob[:, slot(b, g, i), a, :].rearrange("p (c q) -> p c q", c=4)[:, 0:4:3, :]
            if i == 0 and a == 0 and u >= 1:
                ub, ug = divmod(u - 1, GROUPS)
                pool.wait_ge(*used(K, name, 32, ub, ug))
            pool.wait_ge(*K.ra.freed(name, "t", b, 4 * g + 2 * i + 1))
            pool.tensor_tensor(K.kept[:, i, a, :, :], src, K.C("upper").unsqueeze(1).broadcast_to((P, 2, P)),
                               ALU.mult).then_inc(*K.m.done("kept", name, b, g, i, a))


def add_tiles_dve(K, dve, name, u):
    b, g = TURNS[u]
    for i in range(2):
        if i == 0 and u >= 2:
            dve.wait_ge(*used(K, name, 32, *TURNS[u - 2]))
        dve.wait_ge(*K.ra.freed(name, "t", b, 4 * g + 2 * i + 1))
        e = K.prob[:, slot(b, g, i), :, :]
        dve.tensor_tensor(K.both[:, u % 2, 2 * i:2 * i + 2, :], e[:, :, 0:SEQ], e[:, :, SEQ:], ALU.add).then_inc(
            *K.m.done("added", name, u, i))


def weigh_pe(K, pe, name, dims, b, g, kind, ready):
    key = (name, "o", (b, g) if dims == 32 else b)
    first, last = dims == 32 or g == 0, dims == 32 or g == GROUPS - 1
    bank = K.ro.claim(*key) if first else K.ro.bank(*key)
    if b == 0 and g == 0:
        for w in ready():
            pe.wait_ge(*w)
    pe.wait_ge(*K.ra.freed(name, "t", b, 4 * g + 3))
    if kind == "upper":
        pe.wait_ge(*K.m.since("kept", name, b, g, 1, 1))
    if dims == 32:
        pe.wait_ge(*K.m.since("added", name, GROUPS * b + g, 1))
    if first and K.ro.reused(*key):
        pe.wait_ge(*K.ro.room(*key))

    def e(j, lo, hi):
        return K.prob[:, slot(b, g, j // 2), j % 2, lo:hi]

    ones = K.C("ones")[:, 0:32] if dims == 32 else K.C("own8")[:, 32 * g:32 * g + 32]
    steps = []
    if masked(kind):
        steps = [("v", 0, 0, SEQ, 0), ("v", 1, P, SEQ, SEQ), ("one", 0, 0, SEQ, 0), ("one", 1, P, SEQ, SEQ)]
    elif kind == "all" and dims == 32:
        steps = [("v", 0, 0, SEQ, 0), ("v", 1, 0, SEQ, SEQ), ("both", 0, 0, SEQ, 0)]
    elif kind == "all":
        steps = [("v", 0, 0, SEQ, 0), ("v", 1, 0, SEQ, SEQ), ("one", 0, 0, SEQ, 0), ("one", 1, 0, SEQ, SEQ)]
    else:
        steps = [("keep", 0, 0, P, 0), ("v", 1, 0, P, SEQ), ("keep", 1, P, SEQ, 0),
                 ("both", 0, 0, SEQ, 0)]
    for n, (what, kc, q0, q1, col) in enumerate(steps):
        for j in range(4):
            value = K.v[:, 2 * b + kc, head(dims, g, j), :]
            if what == "keep":
                moving = K.kept[:, j // 2, j % 2, kc, :]
            elif what == "both":
                moving = K.both[:, (GROUPS * b + g) % 2, j, :]
            else:
                moving = e(j, col, col + q1 - q0)
            at = 0 if what in ("v", "keep") else SEQ
            mm = pe.matmul(bank[32 * j:32 * j + 32, at + q0:at + q1], ones if at else value, moving,
                           start=(first and n == 0), stop=(last and n == len(steps) - 1), skip_group_check=True)
    if last:
        mm.then_inc(*K.ro.fill(*key))
    else:
        mm.then_inc(*K.m.done("weighed", name, b, g))


def results(dims):
    return [((b, g) if dims == 32 else b, u) for u, (b, g) in enumerate(TURNS) if dims == 32 or g == GROUPS - 1]


def result_at(dims, u):
    done = [n for n, (_, at) in enumerate(results(dims)) if at == u]
    return done[0] if done else None


def weighed_act(K, act, name, dims, n):
    key = results(dims)[n][0]
    act.wait_ge(*K.ro.full(name, "o", key))
    if n >= 2:
        act.wait_ge(*K.m.since("divided", name, n - 2))
    act.activation(K.weighed[:, n % 2, :], K.ro.bank(name, "o", key), ACT.Copy).then_inc(
        *K.ro.free((name, "o", key)))


def divide_dve(K, dve, name, dims, n):
    w, key = K.weighed[:, n % 2, :], results(dims)[n][0]
    b, g = key if dims == 32 else (key, 0)
    dve.wait_ge(*K.ro.freed(name, "o", key))
    dve.reciprocal(w[:, SEQ:], w[:, SEQ:]).then_inc(*K.m.done("recip", name, n))
    dve.wait_ge(*K.m.since("recip", name, n))
    dve.tensor_tensor(K.q[:, g, seq(b)], w[:, 0:SEQ], w[:, SEQ:], ALU.mult).then_inc(*K.m.done("divided", name, n))


def divided(K, name, dims, s):
    return [K.m.since("divided", name, (s + 1) * len(results(dims)) // HALVES - 1)]


TURNS = [(b, g) for b in range(PB) for g in range(GROUPS)]
AHEAD = GROUPS + 1


def attention_pe(K, pe, name, dims, kind, rounded, exact, values, stack=None,
                 after=None):
    for u in range(AHEAD):
        for j in range(4):
            if u == GROUPS and j == 1:
                turn_pe(K, pe, name, 0)
            scores_pe(K, pe, name, *TURNS[u], j, dims, kind, rounded)
            if stack and 4 * u + j < len(SLOTS):
                stack_pe(K, pe, stack, 1, [SLOTS[4 * u + j]])
        if after and u < GROUPS:
            after(u)
    for u, (b, g) in enumerate(TURNS):
        for j in range(4):
            if j == 1 and g == GROUPS - 1 and b + 1 < PB:
                turn_pe(K, pe, name, b + 1)
            if u + AHEAD < len(TURNS):
                scores_pe(K, pe, name, *TURNS[u + AHEAD], j, dims, kind, rounded)
            exact_pe(K, pe, name, b, g, j, dims, kind, exact)
        if u:
            weigh_pe(K, pe, name, dims, *TURNS[u - 1], kind, values)
    weigh_pe(K, pe, name, dims, *TURNS[-1], kind, values)


def attention_dve(K, dve, name, dims, kind, ready=None, after=None):
    for u in range(AHEAD):
        if u == GROUPS:
            shift_dve(K, dve, name, 0, kind)
        for j in range(4):
            if u == GROUPS and j == 1:
                turned_dve(K, dve, name, dims, 0)
            maxima_dve(K, dve, name, dims, *TURNS[u], j, kind)
        if u < 2 and dims == 32:
            bands(K, dve, name, *TURNS[u], (0, 1), ready)
        if after and u < GROUPS:
            after(u)
    for u, (b, g) in enumerate(TURNS):
        turn = g == GROUPS - 1 and b + 1 < PB
        if turn:
            shift_dve(K, dve, name, b + 1, kind)
        for j in range(4):
            if turn and j == 1:
                turned_dve(K, dve, name, dims, b + 1)
            if u + AHEAD < len(TURNS):
                maxima_dve(K, dve, name, dims, *TURNS[u + AHEAD], j, kind)
            if j == 0 and u and dims == 32:
                add_tiles_dve(K, dve, name, u - 1)
            if j == 1 and result_at(dims, u - 2) is not None:
                divide_dve(K, dve, name, dims, result_at(dims, u - 2))
            if j == 1 and u + 2 < len(TURNS) and dims == 32:
                bands(K, dve, name, *TURNS[u + 2], (0, 1), ready)
    if dims == 32:
        add_tiles_dve(K, dve, name, len(TURNS) - 1)
    for u in (len(TURNS) - 2, len(TURNS) - 1):
        if result_at(dims, u) is not None:
            divide_dve(K, dve, name, dims, result_at(dims, u))


def attention_act(K, act, name, dims, kind, scale):
    for u, (b, g) in enumerate(TURNS):
        exps_act(K, act, name, dims, b, g, kind, scale)
        if result_at(dims, u - 1) is not None:
            weighed_act(K, act, name, dims, result_at(dims, u - 1))
    weighed_act(K, act, name, dims, result_at(dims, len(TURNS) - 1))


def attention_pool(K, pool, name, kind, ready):
    for b, g in TURNS[:2]:
        bands(K, pool, name, b, g, (2, 3), ready)
    for u, (b, g) in enumerate(TURNS):
        if u + 2 < len(TURNS):
            bands(K, pool, name, *TURNS[u + 2], (2, 3), ready)
        if kind == "upper":
            kept_pool(K, pool, name, b, g)



def gather_pe(K, pe, name, weights, src, ready):
    for s in range(HALVES):
        bank = K.ro.claim(name, s)
        if K.ro.reused(name, s):
            pe.wait_ge(*K.ro.room(name, s))
        for i, w in enumerate(weights):
            for x in ready(i, s):
                pe.wait_ge(*x)
            mm = pe.matmul(bank, w, src(i, s), start=(i == 0), stop=(i == len(weights) - 1))
        mm.then_inc(*K.ro.fill(name, s))


def residual_dve(K, dve, name, dst, base, bias=None, ready=None):
    for s in range(HALVES):
        dve.wait_ge(*K.ro.full(name, s))
        if ready:
            for w in ready(s):
                dve.wait_ge(*w)
        if bias is None:
            op = dve.tensor_tensor(dst[:, half(s)], K.ro.bank(name, s), base[:, half(s)], ALU.add)
        else:
            op = dve.scalar_tensor_tensor(out=dst[:, half(s)], in0=K.ro.bank(name, s), scalar=bias,
                                          in1=base[:, half(s)], op0=ALU.add, op1=ALU.add)
        op.then_inc(*K.ro.free((name, s)))


def added(K, name):
    return lambda s: [K.ro.freed(name, s)]


def add_dve(K, dve, name, dst, a, after):
    for s in range(HALVES):
        for w in after(s):
            dve.wait_ge(*w)
        dve.tensor_tensor(dst[:, half(s)], dst[:, half(s)], a[:, half(s)], ALU.add).then_inc(
            *K.m.done("summed", name, s))


def summed(K, name):
    return lambda s: [K.m.since("summed", name, s)]


def blocks(w, n=4):
    return [w[:, i * P:(i + 1) * P] for i in range(n)]



def ffn_pe(K, pe, name, w1, w2, src, ready):
    project_pe(K, pe, name + "_up", blocks(w1), src, ready)
    gather_pe(K, pe, name + "_down", blocks(w2), lambda i, s: K.k[:, i, half(s)],
              lambda i, s: projected(K, name + "_up", i) if s == 0 else [])


def ffn_act(K, act, name, bias):
    act.preload_act_table_set("gelu_and_others")
    project_act(K, act, name + "_up", 4, lambda g: K.k[:, g, :], ACT.Gelu, bias=lambda g: K.V(bias, g))
    both_tables(act)



def layer0_pe(K, pe):
    norm_pe(K, pe, "l0", K.xw, lambda s: [K.m.since(f"x{s}_loaded")])
    project_pe(K, pe, "lat", [K.W0("w_down")], K.xn, normed(K, "l0"), outs=64)
    for s in range(HALVES):
        rope_pe(K, pe, "rq", K.W0("wq"), K.W0("wqs"), K.xn, normed(K, "l0"), P, [s])
        rope_pe(K, pe, "rk", K.W0("wk", 64), K.W0("wks", 64), K.yc, lambda s: projected(K, "lat", 0), 64, [s])
    values_pe(K, pe, "lv", K.W0("wv", 64), K.yc, lambda s: projected(K, "lat", 0), 64, False)
    stack_pe(K, pe, "sA", 0)
    attention_pe(K, pe, "A", 8, "page", stacked(K, "sA"), lambda b, g: [], lambda: [K.rv.freed("lv", "v", 1)],
                 "sA")
    gather_pe(K, pe, "wo", [K.W0("wo")], lambda i, s: K.q[:, i, half(s)],
              lambda i, s: divided(K, "A", 8, s))

    norm_pe(K, pe, "l1", K.xw, added(K, "wo"))
    project_pe(K, pe, "xq", [K.W0("xq")], K.xn, normed(K, "l1"))
    project_pe(K, pe, "xk", [K.W0("xk")], K.xn, normed(K, "l1"))
    values_pe(K, pe, "xv", K.W0("xv"), K.xn, normed(K, "l1"), P, False)
    stack_pe(K, pe, "sB", 0)
    attention_pe(K, pe, "B", 8, "causal", stacked(K, "sB"), lambda b, g: [], lambda: [K.rv.freed("xv", "v", 1)],
                 "sB")
    gather_pe(K, pe, "wp_self", [K.W0("wp")], lambda i, s: K.q[:, i, half(s)],
              lambda i, s: divided(K, "B", 8, s))

    project_pe(K, pe, "cq", [K.W0("cq")], K.xn, lambda s: [])
    project_pe(K, pe, "ck", [K.W0("ck", 64)], K.ctx, lambda s: [K.m.since("ctx_loaded", 0)], rows=64)
    values_pe(K, pe, "cv", K.W0("cv", 64), K.ctx, lambda s: [], 64, False)
    stack_pe(K, pe, "sC", 0)
    attention_pe(K, pe, "C", 8, "all", stacked(K, "sC"), lambda b, g: [], lambda: [K.rv.freed("cv", "v", 1)],
                 "sC")
    gather_pe(K, pe, "wp_cross", [K.W0("wp")], lambda i, s: K.q[:, i, half(s)],
              lambda i, s: divided(K, "C", 8, s))
    norm_pe(K, pe, "l2", K.xw, added(K, "wp_cross"))
    bank = K.rv.claim("logits")
    pe.wait_ge(*K.rv.freed("l2", "c", 1))
    for t in range(TILES):
        mm = pe.matmul(bank[:, EXPERTS * t:EXPERTS * (t + 1)], K.xn[:, tile(t)], K.wg[:, :], start=True, stop=True)
    mm.then_inc(*K.rv.fill("logits"))


def layer0_act(K, act):
    both_tables(act)
    scale = 1.0 / 8 ** 0.5
    norm_act(K, act, "l0")
    project_act(K, act, "lat", 1, lambda g: K.yc[0:64, :], ACT.Copy, outs=64)
    split_act(K, act, "sA", lambda t, s: [K.m.since("rotated", "r" + t, s)])
    stack_act(K, act, "sA")
    attention_act(K, act, "A", 8, "page", scale)
    norm_act(K, act, "l1")
    project_act(K, act, "xq", 1, lambda g: K.ya, ACT.Identity, bias=lambda g: K.V("x_bq"))
    project_act(K, act, "xk", 1, lambda g: K.yb, ACT.Identity, bias=lambda g: K.V("x_bk"))
    split_act(K, act, "sB", lambda t, s: projected(K, "x" + t, 0))
    stack_act(K, act, "sB")
    attention_act(K, act, "B", 8, "causal", scale)
    project_act(K, act, "cq", 1, lambda g: K.ya, ACT.Identity, bias=lambda g: K.V("x_bcq"))
    project_act(K, act, "ck", 1, lambda g: K.yb, ACT.Identity, bias=lambda g: K.V("x_bck"))
    split_act(K, act, "sC", lambda t, s: projected(K, "c" + t, 0))
    stack_act(K, act, "sC")
    attention_act(K, act, "C", 8, "all", scale)
    norm_act(K, act, "l2")


def layer0_dve(K, dve, i):
    norm_dve(K, dve, "l0", K.xn)
    for s in range(HALVES):
        rope_dve(K, dve, "rq", K.ya, K.swapped, [s])
        rope_dve(K, dve, "rk", K.yb, K.weighed.rearrange("p n t -> p (n t)"), [s])
    for s in range(HALVES):
        split_dve(K, dve, "sA", s)
    values_dve(K, dve, "lv", None)
    attention_dve(K, dve, "A", 8, "page")
    residual_dve(K, dve, "wo", K.xw, K.xw)
    norm_dve(K, dve, "l1", K.xn)
    for s in range(HALVES):
        split_dve(K, dve, "sB", s)
    values_dve(K, dve, "xv", K.W0("bv"))
    attention_dve(K, dve, "B", 8, "causal")
    residual_dve(K, dve, "wp_self", K.xw, K.xw, K.V("x_bp"))
    for s in range(HALVES):
        split_dve(K, dve, "sC", s)
    values_dve(K, dve, "cv", K.W0("bcv"))
    attention_dve(K, dve, "C", 8, "all")
    residual_dve(K, dve, "wp_cross", K.xw, K.xw)
    norm_dve(K, dve, "l2", K.xn)
    dve.wait_ge(*K.rv.full("logits"))
    dve.tensor_copy(K.logits[:, bass.ds(i * TILES, TILES), :], K.rv.bank("logits")[:, 0:EXPERTS * TILES].rearrange(
        "p (t e) -> p t e", e=EXPERTS)).then_inc(*K.rv.free(("logits",)))
    dve.wait_ge(*K.rv.freed("logits"))



def router_pe(K, pe):
    for c in range(2):
        bank = K.ro.claim("place", c)
        pe.wait_ge(*K.m.since("gate", f"choice{c}"))
        flat = K.onehot[:, c].rearrange("p n e -> p (n e)")
        pe.matmul(bank[:, 0:P], K.B("before"), flat, start=True, stop=False, skip_group_check=True)
        for n in range(15):
            pe.matmul(bank[:, 8 * (n + 1):P].rearrange("p (n e) -> p n e", e=EXPERTS), K.B("ones"),
                      K.onehot[:, c, n, :].unsqueeze(1).broadcast_to((P, 15 - n, EXPERTS)), start=False,
                      stop=False, skip_group_check=True)
        if c:
            for n in range(16):
                pe.matmul(bank[:, 0:P].rearrange("p (n e) -> p n e", e=EXPERTS), K.B("ones"),
                          K.onehot[:, 0, n, :].unsqueeze(1).broadcast_to((P, 16, EXPERTS)), start=False,
                          stop=False, skip_group_check=True)
        pe.matmul(bank[:, 0:8], K.B("ones"), K.zeros[:, :], start=False, stop=True,
                  skip_group_check=True).then_inc(*K.ro.fill("place", c))


def router_act(K, act):
    act.wait_ge(*K.m.since("gate", "less"))
    act.activation(K.gate[:, 1], K.gate[:, 0], ACT.Exp).then_inc(*K.m.done("gate_exp", 0))


def router_dve(K, dve):
    g, col = K.gate, K.gcol

    def wide(i):
        return col[:, i, :].unsqueeze(2).broadcast_to((P, 16, EXPERTS))

    prio = K.C("prio").unsqueeze(1).broadcast_to((P, 16, EXPERTS))

    def step(op, key):
        op.then_inc(*K.m.done("gate", key))
        dve.wait_ge(*K.m.since("gate", key))

    logits = K.logits[:, :, :]
    step(dve.tensor_reduce(col[:, 0, :], logits, AX.X, ALU.max), "max")
    dve.tensor_tensor(g[:, 0], logits, wide(0), ALU.subtract).then_inc(*K.m.done("gate", "less"))
    dve.wait_ge(*K.m.since("gate_exp", 0))
    step(dve.tensor_reduce(col[:, 1, :], g[:, 1], AX.X, ALU.add), "sum")
    step(dve.reciprocal(col[:, 2, :], col[:, 1, :]), "recip")
    step(dve.tensor_tensor(g[:, 2], g[:, 1], wide(2), ALU.mult), "gates")
    for c in range(2):
        src, eq, pri, oh = g[:, 2 + 4 * c], g[:, 3 + 4 * c], g[:, 4 + 4 * c], g[:, 5 + 4 * c]
        step(dve.tensor_reduce(col[:, 3 + c, :], src, AX.X, ALU.max), f"top{c}")
        step(dve.tensor_tensor(eq, src, wide(3 + c), ALU.is_equal), f"equal{c}")
        step(dve.tensor_tensor(pri, eq, prio, ALU.mult), f"ranked{c}")
        step(dve.tensor_reduce(col[:, 5 + c, :], pri, AX.X, ALU.max), f"first{c}")
        step(dve.tensor_tensor(oh, pri, wide(5 + c), ALU.is_equal), f"hot{c}")
        step(dve.tensor_copy(K.onehot[:, c], oh), f"choice{c}")
        if c == 0:
            step(dve.scalar_tensor_tensor(out=g[:, 6], in0=oh, scalar=-2.0, in1=src, op0=ALU.mult, op1=ALU.add),
                 "rest")
    for c in range(2):
        oh, a = g[:, 5 + 4 * c], g[:, 3 + 4 * c]
        place = K.ro.bank("place", c)[:, 0:P].rearrange("p (n e) -> p n e", e=EXPERTS)
        dve.wait_ge(*K.ro.full("place", c))
        step(dve.scalar_tensor_tensor(out=a, in0=place, scalar=float(CAPACITY), in1=oh, op0=ALU.is_lt,
                                      op1=ALU.mult), f"within{c}")
        step(dve.tensor_tensor(a, a, wide(3 + c), ALU.mult), f"weight{c}")
    step(dve.tensor_tensor(K.weight[:, :, :], g[:, 3], g[:, 7], ALU.add), "share")



def experts_pe(K, pe):
    def up(e):
        loaded = K.m.since("up0_loaded" if e == 0 else f"expert{e}_loaded", 0)
        project_pe(K, pe, f"up{e}", [K.expert(e, 0, m) for m in range(4)], K.xn,
                   lambda s: [K.m.since(f"xn{s}_loaded"), loaded])

    up(0)
    b2 = K.small[0:3 * EXPERTS, 3 * P:4 * P]
    for s in range(HALVES):
        bank = K.rv.claim("share", s)
        pe.wait_ge(*K.m.since("levelled", 2))
        for i in range(4):
            mm = pe.transpose(bank[0:3 * EXPERTS, tile(i)], K.levels[:, 4 * s + i, :], K.C("ident"))
        mm.then_inc(*K.rv.fill("share", s))
    for s in range(HALVES):
        bank = K.ro.claim("moe", s)
        pe.wait_ge(*K.rv.freed("share", s))
        pe.matmul(bank, b2, K.share[:, half(s)], start=True, stop=False, skip_group_check=True)

    def down(e):
        if e == 0:
            pe.wait_ge(*K.m.since("expert0_loaded", 0))
        for s in range(HALVES):
            pe.wait_ge(*K.rv.freed("moe", e, s))
            for m in range(4):
                mm = pe.matmul(K.ro.bank("moe", s), K.expert(e, 1, m), hidden(K, e)[:, m, half(s)],
                               start=False, stop=(e == EXPERTS - 1 and m == 3), skip_group_check=True)
            if e == EXPERTS - 1:
                mm.then_inc(*K.ro.fill("moe", s))
            else:
                mm.then_inc(*K.m.done("hidden_used", e, s))

    for e in range(EXPERTS):
        if e:
            up(e)
        for s in range(HALVES):
            bank = K.rv.claim("moe", e, s)
            if K.rv.reused("moe", e, s):
                pe.wait_ge(*K.rv.room("moe", e, s))
            pe.matmul(bank, K.expertsel[0:3 * EXPERTS, e, :], K.shareb[:, half(s)], start=True, stop=True).then_inc(
                *K.rv.fill("moe", e, s))
        if e:
            down(e - 1)
    down(EXPERTS - 1)


def hidden(K, e):
    return K.q if e % 2 else K.k


def experts_act(K, act):
    act.preload_act_table_set("gelu_and_others")
    for e in range(EXPERTS):
        project_act(K, act, f"up{e}", 4, lambda g: hidden(K, e)[:, g, :], ACT.Gelu,
                    bias=lambda g: K.V("moe_b1", 4 * e + g),
                    after=lambda g: [K.m.since("hidden_used", e - 2, 1)] if e >= 2 and g == 0 else [])
    both_tables(act)


def experts_dve(K, dve):
    rest = K.weight_now
    dve.wait_ge(*K.m.since("restored", "weight"))
    for n in range(2):
        dve.tensor_copy(K.rounded[:, :, :], rest[:, :, :]).then_inc(*K.m.done("levelling", n, 0))
        dve.wait_ge(*K.m.since("levelling", n, 0))
        dve.tensor_copy(K.levels[:, :, n * EXPERTS:(n + 1) * EXPERTS], K.rounded[:, :, :]).then_inc(
            *K.m.done("levelled", n))
        out = rest if n == 0 else K.levels[:, :, 2 * EXPERTS:]
        dve.tensor_tensor(out[:, :, :], rest[:, :, :], K.rounded[:, :, :], ALU.subtract).then_inc(
            *(K.m.done("levelling", n, 1) if n == 0 else K.m.done("levelled", 2)))
        if n == 0:
            dve.wait_ge(*K.m.since("levelling", 0, 1))
            dve.wait_ge(*K.m.since("levelled", 0))
    for s in range(HALVES):
        bank = K.rv.bank("share", s)[0:3 * EXPERTS, :]
        dve.wait_ge(*K.rv.full("share", s))
        dve.tensor_copy(K.shareb[:, half(s)], bank).then_inc(*K.m.done("share_rounded", s))
        dve.tensor_copy(K.share[:, half(s)], bank).then_inc(*K.rv.free(("share", s)))
    for e in range(EXPERTS):
        for s in range(HALVES):
            h = hidden(K, e)[:, :, half(s)]
            dve.wait_ge(*K.ra.freed(f"up{e}", 3, 1))
            dve.wait_ge(*K.rv.full("moe", e, s))
            dve.tensor_tensor(h, h, K.rv.bank("moe", e, s).unsqueeze(1).broadcast_to((P, 4, HALF)),
                              ALU.mult).then_inc(*K.rv.free(("moe", e, s)))
    residual_dve(K, dve, "moe", K.xw, K.xw, ready=lambda s: [K.m.since("x_loaded", 0)])


def linear_pe(K, pe):
    pe.wait_ge(K.later_loaded, 16)
    """Linear attention: keys and values token-major, their products in one matrix for all heads."""
    kv = K.W1("qkv")[:, P:3 * P]
    for c in range(4):
        bank = K.ra.claim("kv", c)
        for w in affined(K, "n1")(c // 2):
            pe.wait_ge(*w)
        if K.ra.reused("kv", c):
            pe.wait_ge(*K.ra.room("kv", c))
        for i in range(2):
            mm = pe.matmul(bank[:, i * SEQ:(i + 1) * SEQ], K.xn[:, tile(2 * c + i)], kv, start=True, stop=True)
        mm.then_inc(*K.ra.fill("kv", c))
    project_pe(K, pe, "lq", [K.W1("qkv")[:, 0:P]], K.xn, lambda s: [])
    for b in range(PB):
        bank = K.ro.claim("outer", b)
        pe.wait_ge(*K.m.since("elu", "k", b))
        if K.ro.reused("outer", b):
            pe.wait_ge(*K.ro.room("outer", b))
        for i in range(2):
            key = K.q[:, 0, tile(2 * b + i)]
            pe.matmul(bank[:, 0:P], key, K.q[:, 1, tile(2 * b + i)], start=(i == 0), stop=False,
                      skip_group_check=True)
            mm = pe.matmul(bank[:, P:2 * P], key, K.C("ones"), start=False, stop=(i == 1), skip_group_check=True)
        mm.then_inc(*K.ro.fill("outer", b))
    for b in range(PB):
        bank = K.rv.claim("linear", b)
        pe.wait_ge(*K.m.since("elu", "q", b // 2))
        pe.wait_ge(*K.ro.freed("outer", b))
        if K.rv.reused("linear", b):
            pe.wait_ge(*K.rv.room("linear", b))
        for i in range(2):
            mm = pe.matmul(bank[:, i * SEQ:(i + 1) * SEQ], K.q[:, 3, b * SEQ + i * P:b * SEQ + (i + 1) * P],
                           K.yb[:, seq(b)], start=True, stop=True)
        mm.then_inc(*K.rv.fill("linear", b))
    gather_pe(K, pe, "proj", [K.W1("proj")], lambda i, s: K.q[:, 2, half(s)],
              lambda i, s: [K.rv.freed("linear", 2 * s + 1)])


def linear_act(K, act):
    for c in range(4):
        bank = K.ra.bank("kv", c).rearrange("p (i w) -> p i w", i=2)
        at = slice(2 * c * P, 2 * (c + 1) * P)
        act.wait_ge(*K.ra.full("kv", c))
        act.activation(K.q[:, 0, at].rearrange("p (i w) -> p i w", i=2), bank[:, :, 0:P], ACT.Relu).then_inc(
            *K.m.done("elu_part", "relu", c))
        act.activation(K.q[:, 1, at].rearrange("p (i w) -> p i w", i=2), bank[:, :, P:2 * P], ACT.Copy).then_inc(
            *K.m.done("elu_part", "v", c))
        act.activation(K.q[:, 2, at].rearrange("p (i w) -> p i w", i=2), bank[:, :, 0:P], ACT.Exp).then_inc(
            *K.ra.free(("kv", c)))
    act.wait_ge(*K.ra.full("lq", 0, 1))
    pair = K.ra_pair("lq", 0, 0)
    act.activation(K.yb[:, :].rearrange("p (s t) -> p s t", s=2), pair, ACT.Relu).then_inc(
        *K.m.done("elu_part", "relu", "q"))
    act.activation(K.yc[:, :].rearrange("p (s t) -> p s t", s=2), pair, ACT.Exp).then_inc(
        *K.ra.free(("lq", 0, 0), ("lq", 0, 1)))


def linear_dve(K, dve):
    for c in range(4):
        at = slice(2 * c * P, 2 * (c + 1) * P)
        dve.wait_ge(*K.ra.freed("kv", c))
        dve.wait_ge(*K.m.since("elu_part", "v", c))
        dve.scalar_tensor_tensor(out=K.q[:, 0, at], in0=K.q[:, 2, at], scalar=1.0, in1=K.q[:, 0, at], op0=ALU.min,
                                 op1=ALU.add).then_inc(*K.m.done("elu", "k", c))
    for s in range(HALVES):
        dve.wait_ge(*K.ra.freed("lq", 0, 1))
        dve.wait_ge(*K.m.since("elu_part", "relu", "q"))
        dve.scalar_tensor_tensor(out=K.yb[:, half(s)], in0=K.yc[:, half(s)], scalar=1.0, in1=K.yb[:, half(s)],
                                 op0=ALU.min, op1=ALU.add).then_inc(*K.m.done("elu", "q", s))
    for b in range(PB):
        dve.wait_ge(*K.ro.full("outer", b))
        dve.tensor_tensor(K.q[:, 3, seq(b)].rearrange("p (i w) -> p i w", i=2),
                          K.ro.bank("outer", b)[:, 0:SEQ].rearrange("p (i w) -> p i w", i=2),
                          K.C("blocks").unsqueeze(1).broadcast_to((P, 2, P)), ALU.mult).then_inc(
            *K.ro.free(("outer", b)))
    for b in range(PB):
        bank, r = K.rv.bank("linear", b), K.recip[:, b % 2, :]
        dve.wait_ge(*K.rv.full("linear", b))
        dve.tensor_scalar(r, bank[:, SEQ:], 1e-6, None, ALU.add).then_inc(*K.m.done("zsum", b))
        dve.wait_ge(*K.m.since("zsum", b))
        dve.reciprocal(r, r).then_inc(*K.m.done("z", b))
        dve.wait_ge(*K.m.since("z", b))
        dve.tensor_tensor(K.q[:, 2, seq(b)], bank[:, 0:SEQ], r, ALU.mult).then_inc(*K.rv.free(("linear", b)))
    residual_dve(K, dve, "proj", K.ya, K.ya, K.V("proj_b"))


def rounded(K, a, b, g):
    if a == "a2":
        return [K.m.since("rounded", a + x, g, b // 2) for x in "qk"] if b % 2 == 0 else []
    return [K.m.since("rounded", a + x, g) for x in "qk"] if b == 0 else []


def exact(K, a, x, b, g):
    if a == "a2":
        return [K.ra.freed(a + x, g, b // 2)] if b % 2 == 0 else []
    return projected(K, a + x, g) if b == 0 else []


def mixed_pe(K, pe, a, kind, after=None):
    attention_pe(K, pe, a, 32, kind, lambda b, g: rounded(K, a, b, g),
                 lambda b, g: exact(K, a, "k", b, g), lambda: [K.ra.freed(a + "v", "v", TILES - 1)], after=after)
    gather_pe(K, pe, a + "o", blocks(K.W1(a + "_li1")), lambda i, s: K.q[:, i, half(s)],
              lambda i, s: divided(K, a, 32, s) if i == 0 else [])
    center_pe(K, pe, a + "3", K.yc, added(K, a + "o"))


def mixed_ffn_pe(K, pe, a):
    ffn_pe(K, pe, a + "f", K.W1(a + "_li2"), K.W1(a + "_li3"), K.xn, affined(K, a + "3"))


def mixed_ffn_dve(K, dve, a):
    residual_dve(K, dve, a + "f_down", K.yc, K.yc, K.V(a + "_li3_b"))
    add_dve(K, dve, a + "out", K.ya, K.yc, added(K, a + "f_down"))


def mixed_dve(K, dve, a, kind):
    after = None
    if a == "a1":
        round_dve(K, dve, "a1k", K.k, K.kb)
        round_dve(K, dve, "a1q", K.q, K.qb)
    else:
        round_half_dve(K, dve, "a2k", K.k, K.kb, 0)
        round_half_dve(K, dve, "a2q", K.q, K.qb, 0)

        def after(u):
            round_half_dve(K, dve, "a2k", K.k, K.kb, 1, [u])
            round_half_dve(K, dve, "a2q", K.q, K.qb, 1, [u])
    attention_dve(K, dve, a, 32, kind, lambda b, g: exact(K, a, "q", b, g), after)
    residual_dve(K, dve, a + "o", K.yc, K.ya, K.V(a + "_li1_b"))
    norm_dve(K, dve, a + "3", K.xn, affine=(a + "_ln3_g", a + "_ln3_b"))


def half_queries_pe(K, pe, s, groups=range(GROUPS)):
    project_half_pe(K, pe, "a2q", blocks(K.W1("a2_q")), K.xn, affined(K, "a2x"), s, groups)


def a1_and_a2_pe(K, pe):
    project_pe(K, pe, "a1k", blocks(K.W1("a1_k")), K.yb, lambda s: [K.m.since("affine", "a1x", "second", s)])
    project_pe(K, pe, "a1q", blocks(K.W1("a1_q")), K.xn, affined(K, "a1x"))
    mixed_pe(K, pe, "a1", "upper", lambda u: values_pe(K, pe, "a1v", K.W1("a1_v"), K.yb, lambda s: [], P, True,
                                                       (2 * u, 2 * u + 1)))
    center_pe(K, pe, "a2y", K.ctx, lambda s: [K.m.since("ctx_loaded", 0)], rows=CTX)
    variance_pe(K, pe, "a13")
    variance_pe(K, pe, "a2y", rows=CTX)
    mixed_ffn_pe(K, pe, "a1")

    def values(n):
        values_pe(K, pe, "a2v", K.W1("a2_v", CTX), K.yb, affined(K, "a2y"), CTX, True, (2 * n, 2 * n + 1))

    values(0)
    center_pe(K, pe, "ln2", K.ya, summed(K, "a1out"))
    values(1)
    variance_pe(K, pe, "ln2")
    values(2)
    center_pe(K, pe, "a2x", K.ya, affined(K, "ln2"))
    values(3)
    variance_pe(K, pe, "a2x")
    for s in range(HALVES):
        project_half_pe(K, pe, "a2k", blocks(K.W1("a2_k", CTX)), K.yb, affined(K, "a2y"), s, rows=CTX)
    half_queries_pe(K, pe, 0)
    mixed_pe(K, pe, "a2", "all", lambda u: half_queries_pe(K, pe, 1, [u]))
    variance_pe(K, pe, "a23")
    mixed_ffn_pe(K, pe, "a2")


def a1_and_a2_act(K, act):
    project_act(K, act, "a1k", 4, lambda g: K.k[:, g, :], ACT.Copy)
    project_act(K, act, "a1q", 4, lambda g: K.q[:, g, :], ACT.Copy)
    values_act(K, act, "a1v")
    attention_act(K, act, "a1", 32, "upper", 32 ** -0.5)
    squares_act(K, act, "a13")
    squares_act(K, act, "a2y", rows=CTX)
    rstd_act(K, act, "a13")
    rstd_act(K, act, "a2y", rows=CTX)
    ffn_act(K, act, "a1f", "a1_li2_b")
    values_act(K, act, "a2v", [0])
    squares_act(K, act, "ln2")
    values_act(K, act, "a2v", [2])
    rstd_act(K, act, "ln2")
    values_act(K, act, "a2v", [4])
    squares_act(K, act, "a2x")
    values_act(K, act, "a2v", [6])
    rstd_act(K, act, "a2x")
    for s in range(HALVES):
        project_half_act(K, act, "a2k", K.k, s)
    for s in range(HALVES):
        project_half_act(K, act, "a2q", K.q, s)
    attention_act(K, act, "a2", 32, "all", 32 ** -0.5)
    norm_act(K, act, "a23")
    ffn_act(K, act, "a2f", "a2_li2_b")


def a1_and_a2_dve(K, dve):
    mixed_dve(K, dve, "a1", "upper")
    norm_dve(K, dve, "a2y", K.yb, affine=("a2_lny_g", "a2_lny_b"), rows=CTX)
    mixed_ffn_dve(K, dve, "a1")
    norm_dve(K, dve, "ln2", K.ya, affine=("ln2_g", "ln2_b"))
    norm_dve(K, dve, "a2x", K.xn, affine=("a2_lnx_g", "a2_lnx_b"))
    mixed_dve(K, dve, "a2", "all")
    mixed_ffn_dve(K, dve, "a2")


def leaf_rows_pe(K, pe):
    for s in range(HALVES):
        bank = K.rv.claim("leaf", s)
        pe.wait_ge(*K.m.since("tree", "zero", 3))
        if K.rv.reused("leaf", s):
            pe.wait_ge(*K.rv.room("leaf", s))
        for i in range(4):
            mm = pe.transpose(bank[0:48, tile(i)], K.tree[:, 1, 4 * s + i, :], K.C("ident"))
        mm.then_inc(*K.rv.fill("leaf", s))


def leaves_pe(K, pe):
    bank = K.rv.claim("nodes")
    for t in range(TILES):
        for w in normed(K, "l5")(t // 4):
            pe.wait_ge(*w)
        if t == 0 and K.rv.reused("nodes"):
            pe.wait_ge(*K.rv.room("nodes"))
        mm = pe.matmul(bank[:, 45 * t:45 * t + 45], K.xn[:, tile(t)], K.W1("nodes"), start=True, stop=True)
    mm.then_inc(*K.rv.fill("nodes"))
    w1, w2 = K.WF("f_w1"), K.WF("f_w2")
    pe.wait_ge(*K.m.since("feed_loaded", 0))
    for r in range(3):
        outs = [K.ro.claim("leaves", r, s) for s in range(HALVES)]

        def up(m):
            for s in range(HALVES):
                bank = K.ra.claim("hid", r, m, s)
                if K.ra.reused("hid", r, m, s):
                    pe.wait_ge(*K.ra.room("hid", r, m, s))
                pe.matmul(bank, w1[:, r * PASS + m * P:r * PASS + (m + 1) * P], K.xn[:, half(s)], start=True,
                          stop=False, skip_group_check=True)

        def mask(m):
            for s in range(HALVES):
                if r == 0 and m == 0:
                    pe.wait_ge(*K.rv.freed("leaf", s))
                pe.matmul(K.ra.bank("hid", r, m, s), K.leafsel[:, 8 * r + m, :], K.lm[:, half(s)], start=False,
                          stop=True, skip_group_check=True).then_inc(*K.ra.fill("hid", r, m, s))

        def down(m):
            w = w2[:, r * PASS + m * P:r * PASS + (m + 1) * P]
            if m == 0:
                for s in range(HALVES):
                    if K.ro.reused("leaves", r, s):
                        pe.wait_ge(*K.ro.room("leaves", r, s))
            pe.wait_ge(*K.ra.freed("hid", r, m, 1))
            h = (K.q if m < 4 else K.k)[:, m % 4, :]
            b2 = K.small[:, r * P:(r + 1) * P]
            for s in range(HALVES):
                if r < 2:
                    if m == 0:
                        pe.matmul(outs[s], b2, K.lt[:, half(s)], start=True, stop=False, skip_group_check=True)
                    mm = pe.matmul(outs[s], w, h[:, half(s)], start=False, stop=(m == 7), skip_group_check=True)
                else:
                    for i in range(4):
                        t = 4 * s + i
                        if m == 0:
                            pe.matmul(outs[s][:, tile(i)], K.lt[:, tile(t)], b2, start=(i == 0), stop=False,
                                      skip_group_check=True)
                    for i in range(4):
                        t = 4 * s + i
                        mm = pe.matmul(outs[s][:, tile(i)], h[:, tile(t)], w, start=False, stop=(m == 7),
                                       skip_group_check=True)
                if m == 7:
                    mm.then_inc(*K.ro.fill("leaves", r, s))
                elif s == 1:
                    mm.then_inc(*K.m.done("hid_used", r, m))

        up(0)
        up(1)
        if r == 0:
            leaf_rows_pe(K, pe)
        mask(0)
        mask(1)
        for m in range(2, 8):
            up(m)
            mask(m)
            down(m - 2)
        down(6)
        down(7)
    for b in range(PB):
        bank = K.ra.claim("fs", b)
        pe.wait_ge(*K.ro.freed("leaves", 1, 1))
        if K.ra.reused("fs", b):
            pe.wait_ge(*K.ra.room("fs", b))
        for i in range(2):
            mm = pe.matmul(bank[:, i * SEQ:(i + 1) * SEQ], K.ya[:, b * SEQ + i * P:b * SEQ + (i + 1) * P],
                           K.yb[:, seq(b)], start=True, stop=True)
        mm.then_inc(*K.ra.fill("fs", b))
    def turn(b):
        bank = K.ro.claim("ft", b)
        pe.wait_ge(*K.m.since("fnorm", b, 1))
        if K.ro.reused("ft", b):
            pe.wait_ge(*K.ro.room("ft", b))
        for kc in range(2):
            for i in range(2):
                mm = pe.transpose(bank[:, kc * SEQ + i * P:kc * SEQ + (i + 1) * P],
                                  K.prob[:, b, i, kc * P:(kc + 1) * P], K.C("ident"))
        mm.then_inc(*K.ro.fill("ft", b))

    turn(0)
    for b in range(PB):
        if b + 1 < PB:
            turn(b + 1)
        bank = K.rv.claim("fo", b)
        pe.wait_ge(*K.ro.freed("ft", b))
        pe.wait_ge(*K.ro.freed("leaves", 2, 1))
        if K.rv.reused("fo", b):
            pe.wait_ge(*K.rv.room("fo", b))
        for kc in range(2):
            mm = pe.matmul(bank[:, 0:SEQ], K.yc[:, tile(2 * b + kc)], K.q[:, b, kc * SEQ:(kc + 1) * SEQ],
                           start=(kc == 0), stop=(kc == 1))
        mm.then_inc(*K.rv.fill("fo", b))


def leaves_act(K, act):
    for r in range(3):
        for m in range(8):
            if r:
                if m < 7:
                    act.wait_ge(*K.m.since("hid_used", r - 1, m))
                else:
                    act.wait_ge(*K.ro.full("leaves", r - 1, 1))
            act.wait_ge(*K.ra.full("hid", r, m, 1))
            h = (K.q if m < 4 else K.k)[:, m % 4, :]
            act.activation(h.rearrange("p (s t) -> p s t", s=2), K.ra_pair("hid", r, m, 0), ACT.Relu,
                           bias=K.V("f_b1", 8 * r + m)).then_inc(*K.ra.free(("hid", r, m, 0), ("hid", r, m, 1)))
    for b in range(PB):
        for i in range(2):
            act.wait_ge(*K.m.since("fmax", "scaled", b))
            op = act.activation(K.prob[:, b, i, 0:SEQ], K.ra.bank("fs", b)[:, i * SEQ:(i + 1) * SEQ], ACT.Exp,
                                bias=K.stat[:, 0, 2 * b + i:2 * b + i + 1], scale=P ** -0.5,
                                accum_out=K.stat[:, 1, 2 * b + i:2 * b + i + 1])
            if i:
                op.then_inc(*K.ra.free(("fs", b)))
            else:
                op.then_inc(*K.m.done("fexp", b))


def leaves_dve(K, dve):
    d, c = K.tree[:, 0], K.tree[:, 1]

    def step(op, *key):
        op.then_inc(*K.m.done("tree", *key))
        dve.wait_ge(*K.m.since("tree", *key))

    score = K.rv.bank("nodes")[:, 0:45 * TILES].rearrange("p (t n) -> p t n", t=TILES)
    dve.wait_ge(*K.rv.full("nodes"))
    dve.tensor_tensor(d[:, :, 0:45], score, K.W1("node_b").unsqueeze(1).broadcast_to((P, TILES, 45)),
                      ALU.add).then_inc(*K.rv.free(("nodes",)))
    dve.wait_ge(*K.rv.freed("nodes"))
    step(dve.tensor_scalar(d[:, :, 0:45], d[:, :, 0:45], 0.0, None, ALU.is_ge), "right")
    turn = d[:, :, 0:45].rearrange("p t (r n) -> p t r n", r=3)
    a, b = c.rearrange("p t (r n) -> p t r n", r=3), K.treeb[:, :, :].rearrange("p t (r n) -> p t r n", r=3)
    level = [b, a, b, a]
    step(dve.tensor_copy(b[:, :, :, 1], turn[:, :, :, 0]), "one", 0)
    step(dve.tensor_scalar(b[:, :, :, 0], turn[:, :, :, 0], -1.0, 1.0, ALU.mult, ALU.add), "zero", 0)
    for n in (1, 2, 3):
        w = 2 ** n
        old, new = level[n - 1], level[n]
        step(dve.tensor_tensor(new[:, :, :, 1:2 * w:2], old[:, :, :, 0:w], turn[:, :, :, w - 1:2 * w - 1], ALU.mult),
             "one", n)
        step(dve.tensor_tensor(new[:, :, :, 0:2 * w:2], old[:, :, :, 0:w], new[:, :, :, 1:2 * w:2], ALU.subtract),
             "zero", n)
    for s in range(HALVES):
        bank = K.rv.bank("leaf", s)[0:48, :]
        dve.wait_ge(*K.rv.full("leaf", s))
        dve.tensor_scalar(K.lm[:, half(s)], bank, -1.0, None, ALU.add)
        dve.tensor_copy(K.lt[:, half(s)], bank).then_inc(*K.rv.free(("leaf", s)))
    for r, dst in enumerate((K.ya, K.yb, K.yc)):
        for s in range(HALVES):
            dve.wait_ge(*K.ro.full("leaves", r, s))
            dve.tensor_copy(dst[:, half(s)], K.ro.bank("leaves", r, s)).then_inc(*K.ro.free(("leaves", r, s)))
    for b in range(PB):
        at = slice(2 * b, 2 * b + 2)
        dve.wait_ge(*K.ra.full("fs", b))
        dve.tensor_reduce(K.stat[:, 0, at], K.ra.bank("fs", b).rearrange("p (i k) -> p i k", i=2), AX.X,
                          ALU.max).then_inc(*K.m.done("fmax", "raw", b))
        dve.wait_ge(*K.m.since("fmax", "raw", b))
        dve.tensor_scalar(K.stat[:, 0, at], K.stat[:, 0, at], -(P ** -0.5), None, ALU.mult).then_inc(
            *K.m.done("fmax", "scaled", b))

    def normalise(b):
        at = slice(2 * b, 2 * b + 2)
        dve.wait_ge(*K.ra.freed("fs", b))
        dve.wait_ge(*K.m.since("fexp", b))
        dve.reciprocal(K.stat[:, 1, at], K.stat[:, 1, at]).then_inc(*K.m.done("frecip", b))
        dve.wait_ge(*K.m.since("frecip", b))
        for i in range(2):
            e = K.prob[:, b, i, 0:SEQ]
            dve.tensor_scalar(e, e, K.stat[:, 1, 2 * b + i:2 * b + i + 1], None, ALU.mult).then_inc(
                *K.m.done("fnorm", b, i))

    for n in range(PB + 2):
        if n < PB:
            normalise(n)
        if 1 <= n <= PB:
            b = n - 1
            dve.wait_ge(*K.ro.full("ft", b))
            dve.tensor_copy(K.q[:, b, 0:HALF], K.ro.bank("ft", b)).then_inc(*K.ro.free(("ft", b)))
        if n >= 2:
            b = n - 2
            dve.wait_ge(*K.rv.full("fo", b))
            dve.tensor_tensor(K.xw[:, seq(b)], K.rv.bank("fo", b)[:, 0:SEQ], K.xw[:, seq(b)], ALU.add).then_inc(
                *K.rv.free(("fo", b)))


def layer1_pe(K, pe):
    experts_pe(K, pe)
    norm_pe(K, pe, "l3", K.xw, added(K, "moe"))
    norm_pe(K, pe, "n1", K.ya, normed(K, "l3"))
    linear_pe(K, pe)
    norm_pe(K, pe, "n2", K.ya, added(K, "proj"))
    ffn_pe(K, pe, "fc", K.W1("fc1"), K.W1("fc2"), K.xn, affined(K, "n2"))

    norm_pe(K, pe, "l4", K.xw, summed(K, "linear"))
    norm_pe(K, pe, "ln1", K.ya, normed(K, "l4"))
    norm_pe(K, pe, "a1x", K.ya, affined(K, "ln1"))
    a1_and_a2_pe(K, pe)

    norm_pe(K, pe, "l5", K.xw, summed(K, "cross"))
    leaves_pe(K, pe)


def layer1_act(K, act):
    experts_act(K, act)
    norm_act(K, act, "l3")
    norm_act(K, act, "n1")
    linear_act(K, act)
    norm_act(K, act, "n2")
    ffn_act(K, act, "fc", "fc1_b")
    norm_act(K, act, "l4")
    norm_act(K, act, "ln1")
    norm_act(K, act, "a1x")
    a1_and_a2_act(K, act)
    norm_act(K, act, "l5")
    leaves_act(K, act)


def layer1_dve(K, dve):
    experts_dve(K, dve)
    norm_dve(K, dve, "l3", K.ya)
    norm_dve(K, dve, "n1", K.xn, affine=("n1_g", "n1_b"))
    linear_dve(K, dve)
    norm_dve(K, dve, "n2", K.xn, affine=("n2_g", "n2_b"))
    residual_dve(K, dve, "fc_down", K.ya, K.ya, K.V("fc2_b"))
    add_dve(K, dve, "linear", K.xw, K.ya, added(K, "fc_down"))

    norm_dve(K, dve, "l4", K.ya)
    norm_dve(K, dve, "ln1", K.ya, affine=("ln1_g", "ln1_b"))
    norm_dve(K, dve, "a1x", K.xn, affine=("a1_lnx_g", "a1_lnx_b"), second=(K.yb, "a1_lny_g", "a1_lny_b"))
    a1_and_a2_dve(K, dve)
    add_dve(K, dve, "cross", K.xw, K.ya, summed(K, "a2out"))
    norm_dve(K, dve, "l5", K.xn)
    leaves_dve(K, dve)


def layer1_pool(K, pool, i):
    pool.tensor_copy(K.weight_now[:, :, :], K.weight[:, bass.ds(i * TILES, TILES), :]).then_inc(
        *K.m.done("restored", "weight"))
    pool.wait_ge(*K.ro.full("moe", 1))
    for a, kind in (("a1", "upper"), ("a2", "all")):
        attention_pool(K, pool, a, kind, lambda b, g: exact(K, a, "q", b, g))


def build(nc, known, args):
    (xT, ctxT, vec, const, early, moe, feed, late, wgT, leafsel, small, out) = args
    with ExitStack() as ctx:
        marks = Marks(nc, ctx, known)
        for kind in KINDS:
            marks.sem(kind)
        lo = min(sem_number(s) for s in marks.sems.values())
        hi = max(sem_number(s) for s in marks.sems.values())
        assert hi - lo + 1 == len(marks.sems)
        K = Chip(nc, ctx, marks)
        K.later_loaded = ctx.enter_context(nc.semaphore("later_loaded"))
        x_kept = nc.dram_tensor("x_kept", (P, TOKENS), F32, kind="Internal").ap()
        xn_kept = nc.dram_tensor("xn_kept", (P, TOKENS), F32, kind="Internal").ap()
        K.wg = ctx.enter_context(nc.sbuf_tensor("wg", [P, EXPERTS], F32))
        K.zeros = ctx.enter_context(nc.sbuf_tensor("zeros", [P, 8], BF16))

        def clear():
            with nc.Block() as block:
                @block.gpsimd
                def _(pool):
                    pool.sem_clear(range(lo, hi + 1))

        K.begin("setup")
        with nc.Block() as block:
            @block.sync
            def _(sp):
                sp.dma_start(K.const[:, :], const).then_inc(*K.m.done("const_loaded", 0, n=16))
                for n, (dst, src) in enumerate((
                        (K.vec[:, :], vec), (K.early[:, 0:K.n0], early),
                        (K.wg[:, :], wgT))):
                    sp.dma_start(dst, src).then_inc(*K.m.done("weights", n, n=16))
                sp.wait_ge(*K.m.since("weights", 2))

            @block.vector
            def _(dve):
                dve.memset(K.late[:, 0:6 * 8 * P // 2], 0.0).then_inc(*K.m.done("setup", "sel"))
                dve.memset(K.zeros[:, :], 0.0).then_inc(*K.m.done("setup", "zeros"))
                dve.memset(K.shift[:, :, :], 0.0).then_inc(*K.m.done("setup", "shift"))
                dve.wait_ge(*K.m.since("const_loaded", 0))
                for name in TO_BF16:
                    dve.tensor_copy(K.B(name), K.C(name)).then_inc(*K.m.done("setup", name))
                dve.wait_ge(*K.m.since("setup", TO_BF16[-1]))
                dve.tensor_copy(K.headsel[:, :, :], K.B("ident")[:, 0:HEADS].unsqueeze(2).broadcast_to(
                    (P, HEADS, P))).then_inc(*K.m.done("setup", "headsel"))
                selectors_dve(K, dve)
                ident, rows = K.B("ident"), K.expertsel[:, :, 0]
                dve.tensor_tensor(rows, ident[:, 0:8], ident[:, 8:16], ALU.add).then_inc(
                    *K.m.done("setup", "expertsel", 0))
                dve.wait_ge(*K.m.since("setup", "expertsel", 0))
                dve.tensor_tensor(rows, rows, ident[:, 16:24], ALU.add).then_inc(*K.m.done("setup", "expertsel", 1))
                dve.wait_ge(*K.m.since("setup", "expertsel", 1))
                dve.tensor_copy(K.expertsel[:, :, 1:], rows.unsqueeze(2).broadcast_to((P, EXPERTS, P - 1))).then_inc(
                    *K.m.done("setup", "expertsel", 2))
                dve.wait_ge(*K.m.since("setup", "expertsel", 2))

            @block.gpsimd
            def _(pool):
                pool.memset(K.v[:, :, :, :], 0.0).then_inc(*K.m.done("padding", 0))
                pool.wait_ge(*K.m.since("padding", 0))

        with nc.Fori(0, PASSES) as i:
            K.begin("first")
            with nc.Block() as block:
                @block.tensor
                def _(pe):
                    layer0_pe(K, pe)

                @block.sync
                def _(sp):
                    for s in range(HALVES):
                        sp.dma_start(K.xw[:, half(s)], xT[:, bass.ds(i * PASS + s * HALF, HALF)]).then_inc(
                            *K.m.done(f"x{s}_loaded", n=16))
                    sp.dma_start(K.ctx[:, :], ctxT[:, bass.ds(i * PASS, PASS)]).then_inc(
                        *K.m.done("ctx_loaded", 0, n=16))
                    for name in "ABC":
                        max_rows_sp(K, sp, name)
                    sp.wait_ge(*K.ro.freed("wp_cross", 1))
                    sp.dma_start(x_kept[:, bass.ds(i * PASS, PASS)], K.xw[:, :]).then_inc(
                        *K.m.done("x_stored", 0, n=16))
                    for s in range(HALVES):
                        sp.wait_ge(*K.rv.freed("l2", "c", s))
                        sp.dma_start(xn_kept[:, bass.ds(i * PASS + s * HALF, HALF)], K.xn[:, half(s)]).then_inc(
                            *K.m.done("xn_stored", s, n=16))
                    sp.wait_ge(*K.m.since("x_stored", 0))
                    sp.wait_ge(*K.m.since("xn_stored", 1))

                @block.scalar
                def _(act):
                    layer0_act(K, act)

                @block.vector
                def _(dve):
                    layer0_dve(K, dve, i)
            clear()

        K.begin("router")
        with nc.Block() as block:
            @block.tensor
            def _(pe):
                router_pe(K, pe)

            @block.scalar
            def _(act):
                router_act(K, act)
                act.wait_ge(*K.m.since("selectors", 0))
                act.activation(K.leafsel.rearrange("p h m -> p (h m)"),
                               K.k[0:48, 0:3, :].rearrange("p a t -> p (a t)"), ACT.Copy).then_inc(
                    *K.m.done("gate_exp", 1))
                act.wait_ge(*K.m.since("gate_exp", 1))

            @block.vector
            def _(dve):
                router_dve(K, dve)

            @block.sync
            def _(sp):
                sp.dma_start(K.k[0:48, 0:3, :].rearrange("p a t -> p (a t)"), leafsel).then_inc(
                    *K.m.done("selectors", 0, n=16))
                sp.dma_start(K.small[:, :], small).then_inc(*K.m.done("weights", 0, n=16))
                sp.dma_start(K.late[:, :], late).then_inc(K.later_loaded, 16)
                sp.wait_ge(*K.m.since("weights", 0))
        clear()
        K.bands = band_ring(K.early)

        with nc.Fori(0, PASSES) as i:
            K.begin("second")
            with nc.Block() as block:
                @block.tensor
                def _(pe):
                    layer1_pe(K, pe)

                @block.sync
                def _(sp):
                    sp.dma_start(K.xn[:, half(0)], xn_kept[:, bass.ds(i * PASS, HALF)]).then_inc(
                        *K.m.done("xn0_loaded", n=16))
                    sp.dma_start(K.early[:, 0:HID], moe[:, 0:HID]).then_inc(*K.m.done("up0_loaded", 0, n=16))
                    sp.dma_start(K.xn[:, half(1)], xn_kept[:, bass.ds(i * PASS + HALF, HALF)]).then_inc(
                        *K.m.done("xn1_loaded", n=16))
                    sp.dma_start(K.early[:, HID:2 * HID], moe[:, HID:2 * HID]).then_inc(
                        *K.m.done("expert0_loaded", 0, n=16))
                    for e in range(1, EXPERTS):
                        at = slice(2 * HID * e, 2 * HID * (e + 1))
                        sp.dma_start(K.early[:, at], moe[:, at]).then_inc(*K.m.done(f"expert{e}_loaded", 0, n=16))
                    sp.dma_start(K.xw[:, :], x_kept[:, bass.ds(i * PASS, PASS)]).then_inc(
                        *K.m.done("x_loaded", 0, n=16))
                    sp.wait_ge(*K.ro.full("moe", 1))
                    sp.dma_start(K.ctx[:, :], ctxT[:, bass.ds(i * PASS, PASS)]).then_inc(
                        *K.m.done("ctx_loaded", 0, n=16))
                    sp.wait_ge(*K.ra.full("a2", "t", PB - 1, HEADS - 1))
                    sp.dma_start(K.early[:, 0:K.nf], feed).then_inc(*K.m.done("feed_loaded", 0, n=16))
                    for b in range(PB):
                        sp.wait_ge(*K.rv.freed("fo", b))
                        sp.dma_start(out[:, bass.ds(i * PASS + b * SEQ, SEQ)], K.xw[:, seq(b)]).then_inc(
                            *K.m.done("stored", b, n=16))
                    sp.wait_ge(*K.m.since("stored", PB - 1))
                    sp.wait_ge(*K.m.since("ctx_loaded", 0))

                @block.scalar
                def _(act):
                    layer1_act(K, act)

                @block.vector
                def _(dve):
                    layer1_dve(K, dve)

                @block.gpsimd
                def _(pool):
                    layer1_pool(K, pool, i)
            clear()
        return marks.found


KINDS = [
    "rv_filled", "rv_freed", "ro_filled", "ro_freed", "ra_filled", "ra_freed", "squared", "rstd", "affine",
    "rounded", "rotated", "coarse", "fine", "max_rows", "banded_v", "banded_p", "value", "joined", "negated",
    "kept", "added", "recip", "divided", "weighed", "summed", "weights", "const_loaded", "selectors",
    "setup", "padding", "x_loaded", "x0_loaded", "x1_loaded", "xn0_loaded", "xn1_loaded", "up0_loaded",
    "ctx_loaded", "gate", "gate_exp", "x_stored", "xn_stored", "feed_loaded", "restored", "levelling",
    "levelled", "share_rounded", "hidden_used", "elu", "elu_part", "zsum", "z", "tree", "hid_used", "fmax",
    "fexp", "frecip", "fnorm", "stored",
] + [f"expert{e}_loaded" for e in range(EXPERTS)]


def sem_number(s):
    return s.num



def _layout(a):
    import numpy as np
    f = {n: np.asarray(v) for n, v in a.items()}

    def rows(m, r=P):
        m = np.asarray(m, np.float32) if m.dtype != np.float32 else m
        out = np.zeros((r, m.shape[1]), np.float32)
        out[:m.shape[0]] = m
        return out

    def swap(w):
        return w.reshape(w.shape[0], -1, 2)[:, :, ::-1].reshape(w.shape)

    def fold(w):
        return w.reshape(-1, P, w.shape[1]).transpose(1, 0, 2).reshape(P, -1)

    def cols(v):
        return v.reshape(-1, P).T

    def heads(w):
        return w.transpose(1, 0, 2).reshape(w.shape[1], -1)

    vec = np.zeros((P, NVEC), np.float32)

    def put(name, m):
        at, n = VCOL[name]
        assert m.shape[1] == n
        vec[:m.shape[0], at:at + n] = m
    for name, key in (("x_bq", "bq"), ("x_bk", "bk"), ("x_bcq", "bcq"), ("x_bck", "bck")):
        put(name, cols(f["L0_xattn_" + key]))
    put("x_bp", cols(f["L0_xattn_bp"]))
    put("moe_b1", cols(f["L0_ffn_b1"]))
    for name, key in (("n1_g", "norm1_g"), ("n1_b", "norm1_b"), ("proj_b", "proj_b"), ("n2_g", "norm2_g"),
                      ("n2_b", "norm2_b"), ("fc1_b", "fc1_b"), ("fc2_b", "fc2_b")):
        put(name, cols(f["L1_attn_" + key]))
    for name in ("ln1_g", "ln1_b", "ln2_g", "ln2_b"):
        put(name, cols(f["L1_xattn_" + name]))
    for b in ("a1", "a2"):
        for name in ("lnx_g", "lnx_b", "lny_g", "lny_b", "li1_b", "ln3_g", "ln3_b", "li2_b", "li3_b"):
            v = f[f"L1_xattn_{b}_{name}"]
            put(f"{b}_{name}", cols(v) if v.size >= P else v.reshape(-1, 1))
    put("f_b1", np.concatenate([cols(f[f"L1_ffn_{r}_b1"]) for r in "qkv"], 1))
    vec[:, VCOL["eps"][0]] = EPS
    vec[MAX_ROW::64, VCOL["max_row"][0]] = 1.0

    eye = np.eye(P, dtype=np.float32)
    i = np.arange(P)
    page = np.where(i[None] // 32 <= i[:, None] // 32, 0.0, MASKED).astype(np.float32)
    causal = np.where(i[None] <= i[:, None], 0.0, MASKED).astype(np.float32)
    consts = {"ident": eye, "center": eye - 1.0 / P, "mean": np.full((P, P), 1.0 / P),
              "center64": rows((np.eye(64) - 1.0 / 64).astype(np.float32)),
              "mean64": rows(np.full((64, 64), 1 / 64, np.float32)), "ones": np.ones((P, P)),
              "page": page, "pageT": page.T, "causal": causal, "causalT": causal.T,
              "upper": (i[:, None] > i[None]).astype(np.float32),
              "before": (i[:, None] < i[None]).astype(np.float32),
              "blocks": (i[:, None] // 8 == i[None] // 8).astype(np.float32),
              "headrows": (i[:, None] // 32 == np.arange(4)[None]).astype(np.float32),
              "own8": np.broadcast_to((np.arange(32)[None] // 8 == np.arange(4)[:, None]).reshape(1, P), (P, P)),
              "prio": np.broadcast_to(8.0 - np.arange(8), (P, 8))}
    const = np.concatenate([np.asarray(consts[n], np.float32) for n, _ in CONSTS], 1)

    inv = 1.0 / 10000.0 ** (np.arange(0, 8, 2, dtype=np.float32) / 8)
    ang = np.outer(np.arange(SEQ, dtype=np.float32), inv.astype(np.float32))
    cos, sin = np.zeros((HEADS, 8, SEQ), np.float32), np.zeros((HEADS, 8, SEQ), np.float32)
    for d in range(8):
        cos[:, d] = np.cos(ang[:, d // 2]).astype(np.float32)
        sin[:, d] = (np.sin(ang[:, d // 2]) * (-1.0 if d % 2 == 0 else 1.0)).astype(np.float32)
    cos, sin = cos.reshape(P, SEQ), sin.reshape(P, SEQ)
    l0 = {"wq": f["L0_attn_wq"], "wqs": swap(f["L0_attn_wq"]), "w_down": f["L0_attn_w_down"],
          "wk": f["L0_attn_wk_up"], "wks": swap(f["L0_attn_wk_up"]), "wv": f["L0_attn_wv_up"],
          "wo": f["L0_attn_wo"], "xq": f["L0_xattn_Wq"], "xk": f["L0_xattn_Wk"],
          "xv": f["L0_xattn_Wv"], "cq": f["L0_xattn_Wcq"], "ck": f["L0_xattn_Wck"],
          "cv": f["L0_xattn_Wcv"], "wp": f["L0_xattn_Wp"], "cos": cos,
          "sin": sin, "bv": np.broadcast_to(f["L0_xattn_bv"], (P, P)),
          "bcv": np.broadcast_to(f["L0_xattn_bcv"], (P, P))}
    early = np.concatenate([rows(l0[n]) for n, _ in LAYER0], 1)
    moe = np.concatenate([np.concatenate([f["L0_ffn_W1"][e], fold(f["L0_ffn_W2"][e])], 1)
                          for e in range(EXPERTS)], 1)
    l1 = {"qkv": f["L1_attn_qkv_w"].T, "proj": f["L1_attn_proj_w"].T, "fc1": f["L1_attn_fc1_w"].T,
          "fc2": fold(f["L1_attn_fc2_w"].T)}
    for b in ("a1", "a2"):
        for w in "qkv":
            l1[f"{b}_{w}"] = heads(f[f"L1_xattn_{b}_w{w}"])
        l1[f"{b}_li1"] = fold(f[f"L1_xattn_{b}_li1_w"])
        l1[f"{b}_li2"] = f[f"L1_xattn_{b}_li2_w"]
        l1[f"{b}_li3"] = fold(f[f"L1_xattn_{b}_li3_w"])
    feed = np.concatenate([f[f"L1_ffn_{r}_w1"].transpose(1, 0, 2).reshape(P, -1) for r in "qkv"]
                          + [fold(f[f"L1_ffn_{r}_w2"].reshape(-1, P)) for r in "qkv"], 1)
    l1["nodes"] = np.concatenate([f[f"L1_ffn_{r}_node_w"].T for r in "qkv"], 1)
    l1["node_b"] = np.broadcast_to(np.concatenate([f[f"L1_ffn_{r}_node_b"] for r in "qkv"]), (P, 45))
    late = np.concatenate([rows(l1[n]) for n, _ in LAYER1], 1)

    leafsel = np.zeros((48, 24, P), np.float32)
    for r in range(3):
        for leaf in range(LEAVES):
            leafsel[16 * r + leaf, 8 * r + leaf // 2, 64 * (leaf % 2):64 * (leaf % 2) + 64] = OFF
    small = np.zeros((48, 4 * P), np.float32)
    for n, r in enumerate("qkv"):
        small[16 * n:16 * n + 16, n * P:(n + 1) * P] = f[f"L1_ffn_{r}_b2"]
    small[0:3 * EXPERTS, 3 * P:] = np.tile(f["L0_ffn_b2"], (3, 1))
    return {"xT": f["x"].reshape(TOKENS, P).T, "ctxT": f["ctx_512"].reshape(TOKENS, CTX).T, "vec": vec,
            "const": const, "early": early, "moe": moe, "feed": feed, "late": late, "wgT": f["L0_ffn_Wg"].T,
            "leafsel": leafsel.reshape(48, -1), "small": small}


def kernel(**inputs):
    import numpy as _np
    import concourse.bacc as _bacc
    from concourse import mybir as _mybir
    from concourse.bass_utils import run_bass_kernel_spmd as _run

    laid = {n: _np.ascontiguousarray(v) for n, v in _layout(inputs).items()}
    known = None
    for _ in range(2):
        nc = _bacc.Bacc("TRN2", target_bir_lowering=False, num_devices=1)
        args = [nc.dram_tensor(f"in_{n}", v.shape, _mybir.dt.from_np(v.dtype), kind="ExternalInput").ap()
                for n, v in laid.items()]
        args.append(nc.dram_tensor("out_0", (P, TOKENS), F32, kind="ExternalOutput").ap())
        known = build(nc, known, args)
    r = _run(nc, [{f"in_{n}": v for n, v in laid.items()}], core_ids=[0])
    return r.results[0]["out_0"].T.reshape(BATCH, SEQ, P)
```
